# Optimizing a Trainium2 kernel written in Bass

```python
import numpy as np
import jax
import jax.numpy as jnp

def _softmax(x, axis=-1):
    return jax.nn.softmax(x, axis=axis)

def _gelu(x):
    return jax.nn.gelu(x, approximate=True)

def _silu(x):
    return jax.nn.silu(x)

def _sigmoid(x):
    return jax.nn.sigmoid(x)

def _layernorm(x, axis=-1, eps=1e-05):
    m = jnp.mean(x, axis=axis, keepdims=True)
    v = jnp.var(x, axis=axis, keepdims=True)
    return (x - m) / jnp.sqrt(v + eps)

def _scatter_add(tgt, idx, src, axis=0):
    return tgt.at[idx].add(src)

def _segment_sum(src, seg, n):
    return jax.ops.segment_sum(src, seg, n)
kernel_name = 'mk_decoder_preln_d1_seqx_r8_e332f2'

def setup_inputs(seed: int=0):
    np.random.seed(seed)
    _w = jnp.asarray

    def _rec_inputs():
        import jax
        import jax.numpy as jnp
        _rk = jax.random.key(seed)
        x = 7.22e-05 + 1 * jax.random.normal(jax.random.fold_in(_rk, 1), (64, 128, 128), jnp.float32)
        _lenS = 128 - jax.random.randint(jax.random.fold_in(_rk, 7), (64,), 0, max(1, 128 // 4) + 1, jnp.int32)
        _lenS2 = 77 - jax.random.randint(jax.random.fold_in(_rk, 8), (64,), 0, max(1, 77 // 4) + 1, jnp.int32)
        _ctx_768P = jax.random.normal(jax.random.fold_in(_rk, 11), (64, 16, 96), jnp.float32)
        _ctx_768c = jax.random.dirichlet(jax.random.fold_in(_rk, 511), 0.3 * jnp.ones((16,), jnp.float32), (64, 77))
        _ctx_768t = jnp.einsum('bsk,bkd->bsd', _ctx_768c, _ctx_768P)
        _ctx_768t = _ctx_768t * jax.lax.rsqrt(jnp.mean(jnp.square(_ctx_768t)) + 1e-12) * 0.953939
        ctx_768 = -0.000191848 + 0.999787 * (_ctx_768t + 0.3 * jax.random.normal(jax.random.fold_in(_rk, 611), (64, 77, 96), jnp.float32))
        return (x, ctx_768)
    x, ctx_768 = _rec_inputs()

    def _L0_attn_setup():
        import jax, jax.numpy as jnp
        import numpy as np
        B, S, H, NH = (8, 512, 128, 16)
        HD = H // NH
        EPS_ATTN = 1e-06
        EPS_LN = 1e-12
        key = jax.random.key(seed)
        ks = jax.random.split(key, 10)
        s = 1.0 / np.sqrt(H)
        return {'input_tensor': jax.random.normal(ks[0], (B, S, H), dtype=jnp.float32), 'attention_mask': jnp.zeros((B, S), dtype=jnp.int32), 'Wq': jax.random.normal(ks[1], (H, H), dtype=jnp.float32) * s, 'bq': jnp.zeros((H,), dtype=jnp.float32), 'Wk': jax.random.normal(ks[2], (H, H), dtype=jnp.float32) * s, 'bk': jnp.zeros((H,), dtype=jnp.float32), 'Wv': jax.random.normal(ks[3], (H, H), dtype=jnp.float32) * s, 'bv': jnp.zeros((H,), dtype=jnp.float32), 'Wd': jax.random.normal(ks[4], (H, H), dtype=jnp.float32) * s, 'bd': jnp.zeros((H,), dtype=jnp.float32), 'gamma': jnp.ones((H,), dtype=jnp.float32), 'beta': jnp.zeros((H,), dtype=jnp.float32)}
    _L0_attn_all = _L0_attn_setup()
    _L0_attn_in = {k: v for k, v in _L0_attn_all.items() if k in ('attention_mask', 'Wq', 'bq', 'Wk', 'bk', 'Wv', 'bv', 'Wd', 'bd', 'gamma', 'beta')}
    del _L0_attn_all

    def _L0_xattn_setup():
        import jax, jax.numpy as jnp
        import numpy as np
        NUM_HEADS = 16
        CLAMP = 10000.0
        key = jax.random.key(seed)
        ks = jax.random.split(key, 8)
        B, Nq, Nkv, Cq, Ckv = (4, 256, 256, 128, 96)
        s_q = 1.0 / np.sqrt(Cq)
        s_kv = 1.0 / np.sqrt(Ckv)
        return {'query': jax.random.normal(ks[0], (B, Nq, Cq), jnp.float32), 'key_value': jax.random.normal(ks[1], (B, Nkv, Ckv), jnp.float32), 'Wq': jax.random.normal(ks[2], (Cq, Cq), jnp.float32) * s_q, 'bq': jnp.zeros((Cq,), jnp.float32), 'Wk': jax.random.normal(ks[3], (Ckv, Cq), jnp.float32) * s_kv, 'bk': jnp.zeros((Cq,), jnp.float32), 'Wv': jax.random.normal(ks[4], (Ckv, Cq), jnp.float32) * s_kv, 'bv': jnp.zeros((Cq,), jnp.float32), 'Wo': jax.random.normal(ks[5], (Cq, Cq), jnp.float32) * s_q, 'bo': jnp.zeros((Cq,), jnp.float32)}
    _L0_xattn_all = _L0_xattn_setup()
    _L0_xattn_in = {k: v for k, v in _L0_xattn_all.items() if k in ('Wq', 'bq', 'Wk', 'bk', 'Wv', 'bv', 'Wo', 'bo')}
    del _L0_xattn_all

    def _L0_ffn_setup():
        import jax, jax.numpy as jnp
        import numpy as np
        HID, FFN, E, K = (128, 512, 8, 2)
        CAP_FACTOR = 1.25
        key = jax.random.key(seed)
        k1, k2, k3, k4 = jax.random.split(key, 4)
        B, T = (4, 256)
        x = jax.random.normal(k1, (B, T, HID), dtype=jnp.float32)
        router_w = jax.random.normal(k2, (E, HID), dtype=jnp.float32) * 0.02
        w1 = jax.random.normal(k3, (E, HID, FFN), dtype=jnp.float32) * 0.02
        w2 = jax.random.normal(k4, (E, FFN, HID), dtype=jnp.float32) * 0.02
        return {'x': x, 'router_w': router_w, 'w1': w1, 'w2': w2}
    _L0_ffn_all = _L0_ffn_setup()
    _L0_ffn_in = {k: v for k, v in _L0_ffn_all.items() if k in ('router_w', 'w1', 'w2')}
    del _L0_ffn_all
    return {'x': x, 'ctx_768': ctx_768, 'L0_attn_attention_mask': _L0_attn_in['attention_mask'], 'L0_attn_Wq': _L0_attn_in['Wq'], 'L0_attn_bq': _L0_attn_in['bq'], 'L0_attn_Wk': _L0_attn_in['Wk'], 'L0_attn_bk': _L0_attn_in['bk'], 'L0_attn_Wv': _L0_attn_in['Wv'], 'L0_attn_bv': _L0_attn_in['bv'], 'L0_attn_Wd': _L0_attn_in['Wd'], 'L0_attn_bd': _L0_attn_in['bd'], 'L0_attn_gamma': _L0_attn_in['gamma'], 'L0_attn_beta': _L0_attn_in['beta'], 'L0_xattn_Wq': _L0_xattn_in['Wq'], 'L0_xattn_bq': _L0_xattn_in['bq'], 'L0_xattn_Wk': _L0_xattn_in['Wk'], 'L0_xattn_bk': _L0_xattn_in['bk'], 'L0_xattn_Wv': _L0_xattn_in['Wv'], 'L0_xattn_bv': _L0_xattn_in['bv'], 'L0_xattn_Wo': _L0_xattn_in['Wo'], 'L0_xattn_bo': _L0_xattn_in['bo'], 'L0_ffn_router_w': _L0_ffn_in['router_w'], 'L0_ffn_w1': _L0_ffn_in['w1'], 'L0_ffn_w2': _L0_ffn_in['w2']}

def reference(x, ctx_768, L0_attn_attention_mask, L0_attn_Wq, L0_attn_bq, L0_attn_Wk, L0_attn_bk, L0_attn_Wv, L0_attn_bv, L0_attn_Wd, L0_attn_bd, L0_attn_gamma, L0_attn_beta, L0_xattn_Wq, L0_xattn_bq, L0_xattn_Wk, L0_xattn_bk, L0_xattn_Wv, L0_xattn_bv, L0_xattn_Wo, L0_xattn_bo, L0_ffn_router_w, L0_ffn_w1, L0_ffn_w2):
    import jax
    import jax.numpy as jnp

    def _L0_attn_ref(input_tensor, attention_mask, Wq, bq, Wk, bk, Wv, bv, Wd, bd, gamma, beta):
        import jax, jax.numpy as jnp
        import numpy as np
        B, S, H, NH = (8, 512, 128, 16)
        HD = H // NH
        EPS_ATTN = 1e-06
        EPS_LN = 1e-12
        x = input_tensor
        b, s, h = x.shape
        q = (x @ Wq.T + bq).reshape(b, s, NH, HD)
        k = (x @ Wk.T + bk).reshape(b, s, NH, HD)
        v = (x @ Wv.T + bv).reshape(b, s, NH, HD)
        q = jax.nn.elu(q) + 1.0
        k = jax.nn.elu(k) + 1.0
        kv = jnp.einsum('nshd,nshm->nhmd', k, v)
        z = 1.0 / jnp.einsum('nlhd,nhd->nlh', q, k.sum(axis=1) + EPS_ATTN)
        ctx = jnp.einsum('nlhd,nhmd,nlh->nlhm', q, kv, z).reshape(b, s, h)
        hs = ctx @ Wd.T + bd
        hs = hs + x
        mu = hs.mean(axis=-1, keepdims=True)
        var = ((hs - mu) ** 2).mean(axis=-1, keepdims=True)
        out = (hs - mu) / jnp.sqrt(var + EPS_LN) * gamma + beta
        return out

    def _L0_xattn_ref(query, key_value, Wq, bq, Wk, bk, Wv, bv, Wo, bo):
        import jax, jax.numpy as jnp
        import numpy as np
        NUM_HEADS = 16
        CLAMP = 10000.0
        B, Nq, Cq = query.shape
        Nkv = key_value.shape[1]
        H = NUM_HEADS
        D = Cq // H
        scale = D ** (-0.5)
        q = (query @ Wq + bq).reshape(B, Nq, H, D).transpose(0, 2, 1, 3)
        k = (key_value @ Wk + bk).reshape(B, Nkv, H, D).transpose(0, 2, 1, 3)
        v = (key_value @ Wv + bv).reshape(B, Nkv, H, D).transpose(0, 2, 1, 3)
        attn = jnp.einsum('bhqd,bhkd->bhqk', q, k) * scale
        attn = jnp.clip(attn, -CLAMP, CLAMP)
        attn = jax.nn.softmax(attn, axis=-1)
        attn = jnp.where(jnp.any(jnp.isnan(attn)), jnp.asarray(1.0 / Nkv, attn.dtype), attn)
        x = jnp.einsum('bhqk,bhkd->bqhd', attn, v).reshape(B, Nq, Cq)
        return x @ Wo + bo

    def _L0_ffn_ref(x, router_w, w1, w2):
        import jax, jax.numpy as jnp
        import numpy as np
        HID, FFN, E, K = (128, 512, 8, 2)
        CAP_FACTOR = 1.25
        B, T, H = x.shape
        N = B * T
        x_flat = x.reshape(N, H)
        C = max(1, int(CAP_FACTOR * N / E * K))
        logits = x_flat @ router_w.T
        probs = jax.nn.softmax(logits, axis=-1)
        top_v, top_i = jax.lax.top_k(probs, K)
        top_v = top_v / jnp.sum(top_v, axis=-1, keepdims=True)
        out = jnp.zeros_like(x_flat)
        for k in range(K):
            eid = top_i[:, k]
            gate = top_v[:, k]
            onehot = jax.nn.one_hot(eid, E, dtype=jnp.int32)
            pos = jnp.take_along_axis(jnp.cumsum(onehot, axis=0), eid[:, None], axis=1)[:, 0] - 1
            keep = pos < C
            slot = jnp.where(keep, eid * C + pos, E * C)
            buf = jnp.zeros((E * C + 1, H), dtype=x.dtype).at[slot].add(x_flat * keep[:, None].astype(x.dtype))
            expert_in = buf[:E * C].reshape(E, C, H)
            h = jax.nn.gelu(jnp.einsum('ech,ehf->ecf', expert_in, w1), approximate=False)
            y = jnp.einsum('ecf,efh->ech', h, w2)
            tok = y.reshape(E * C, H)[jnp.minimum(slot, E * C - 1)]
            out = out + tok * (gate * keep.astype(x.dtype))[:, None]
        return out.reshape(B, T, H)
    x = x + _L0_attn_ref(_layernorm(x, axis=-1), L0_attn_attention_mask, L0_attn_Wq, L0_attn_bq, L0_attn_Wk, L0_attn_bk, L0_attn_Wv, L0_attn_bv, L0_attn_Wd, L0_attn_bd, L0_attn_gamma, L0_attn_beta)
    x = x + _L0_xattn_ref(_layernorm(x, axis=-1), ctx_768, L0_xattn_Wq, L0_xattn_bq, L0_xattn_Wk, L0_xattn_bk, L0_xattn_Wv, L0_xattn_bv, L0_xattn_Wo, L0_xattn_bo)
    x = x + _L0_ffn_ref(_layernorm(x, axis=-1), L0_ffn_router_w, L0_ffn_w1, L0_ffn_w2)
    return x

_drawn_inputs = setup_inputs


def setup_inputs(seed=0):
    import zlib

    import numpy as np

    out = dict(_drawn_inputs(seed))
    spreads = {'L0_attn_bq': (0.0, 0.8),
     'L0_attn_bk': (0.0, 0.8),
     'L0_attn_bv': (0.0, 0.1),
     'L0_attn_bd': (0.0, 0.1),
     'L0_attn_gamma': (1.0, 0.2),
     'L0_attn_beta': (0.0, 0.1),
     'L0_xattn_bq': (0.0, 0.59),
     'L0_xattn_bk': (0.0, 0.8),
     'L0_xattn_bv': (0.0, 0.1),
     'L0_xattn_bo': (0.0, 0.1)}
    factors = {'L0_attn_Wq': 5.934,
     'L0_attn_Wk': 3.211,
     'L0_ffn_router_w': 3.641,
     'L0_ffn_w1': 3.223,
     'L0_ffn_w2': 3.189}
    for name, (base, spread) in spreads.items():
        noise = np.random.default_rng([zlib.crc32(name.encode()), seed]).standard_normal(out[name].shape)
        drawn = base * np.exp(spread * noise) if base else spread * noise
        out[name] = jnp.asarray(drawn.astype(out[name].dtype))
    for name, factor in factors.items():
        out[name] = (out[name] * factor).astype(out[name].dtype)
    return out
```

```python
from contextlib import ExitStack

import concourse.bass as bass
from concourse import mybir

F32 = mybir.dt.float32
I32 = mybir.dt.int32
U32 = mybir.dt.uint32
ALU = mybir.AluOpType
ACT = mybir.ActivationFunctionType
AX = mybir.AxisListType
ds = bass.ds

P = 128
NB = 64
T = 4
NG = NB // T
NH, HD = 16, 8
HG = 4
NK, CK = 77, 96
E, F = 8, 512
FC = F // P
CAP = max(1, int(1.25 * NB * P / E * 2))
REG = CAP + P
NREG = 2 * E
EMPTY = NREG * REG
NTILE = NB + E
ROW = P + 3
BIG = float(1 << 20)
CLAMP = 10000.0
SCALE = HD ** -0.5
EPS = 1e-5
EPS_ATTN, EPS_ATTN_LN = 1e-6, 1e-12
V_BQ, V_BK, V_BV, V_BD, V_GAMMA, V_BETA, V_BQ2, V_BK2, V_BV2, V_BO2 = range(10)
NV = 10
W_Q, W_K, W_V, W_D, W_Q2, W_O2 = range(6)

USES = [("xnT", "L"), ("aoT", "R"), ("xn2T", "M"), ("q", "L"), ("kp0", "L"), ("kp1", "L"), ("x2", "R"),
        ("pv0", "X"), ("kv0", "L"), ("kv1", "L"), ("pvT0", "X"), ("nd0", "L"), ("nd1", "L"),
        ("cT", "L"), ("pv1", "X"), ("hs", "L"), ("pvT1", "X"), ("xn3T", "R"), ("pv2", "X"),
        ("k2T", "M"), ("pvT2", "X"), ("logits", "R"), ("q2T", "M"), ("pv3", "X"), ("v2", "M"), ("pvT3", "X")]
LAG = {"N": -1, "L": 0, "M": 1, "X": 2, "R": 3}


def runs(stage, i):
    return not isinstance(i, int) or 0 <= i - LAG[stage] < NG


def use_of(name, i):
    at = [n for n, _ in USES].index(name)
    bank = at % 2
    mine = [s for n, s in USES[bank::2]]
    if isinstance(i, int):
        before = sum(min(max(i - LAG[s], 0), NG) for s in mine)
    else:
        before = i * len(mine) - sum(LAG[s] for s in mine)
    return bank, before + sum(1 for n, s in USES[bank:at:2] if runs(s, i))


def decoder_layer(nc, x, ctxT, wA, wC, wr, w1, w2, vrow, vcol, out, expert_rows, y_rows):
    with ExitStack() as ctx:
        def sb(name, shape, dt=F32):
            return ctx.enter_context(nc.sbuf_tensor(name, shape, dt))

        def sem(name):
            return ctx.enter_context(nc.semaphore(name))

        wA_s = sb("wA_s", [P, 6, P])
        wC_s = sb("wC_s", [CK, 2, P])
        wr_s = sb("wr_s", [P, E])
        w1_s = sb("w1_s", [P, E * F])
        w2_s = sb("w2_s", [P, E * FC * P])
        vb = sb("vb", [P, NV, P])
        vc = sb("vc", [P, NV])
        ident = sb("ident", [P, P])
        ones = sb("ones", [P, P])
        before = sb("before", [P, P])
        bmask = sb("bmask", [P, P])
        hmask = sb("hmask", [P, HG])
        hmask16 = sb("hmask16", [P, NH])
        expo = sb("expo", [P, T])
        bq2s = sb("bq2s", [P, 1])
        bv2c = sb("bv2c", [P, P])
        bo_all = sb("bo_all", [P, P])
        tok_i = sb("tok_i", [P, NB], I32)
        e_i = sb("e_i", [P, 3, 2, E], I32)
        e_f = sb("e_f", [P, 3, 2, E])
        j_i = sb("j_i", [P, 1], I32)
        j_f = sb("j_f", [P, 1])
        zeros = sb("zeros", [P, 1024])
        tail = sb("tail", [P, ROW])
        xs = sb("xs", [P, NB, P])
        st = sb("st", [P, T, 6])
        mv = sb("mv", [P, T, 2])
        rs = sb("rs", [P, T])
        xn = sb("xn", [P, T, P])
        xb = sb("xb", [P, T, P])
        xbeta = sb("xbeta", [P, T, P])
        xnT = sb("xnT", [P, T * P])
        eq = sb("eq", [P, T * P])
        rq = sb("rq", [P, T * P])
        qT = sb("qT", [P, T * P])
        kvb = sb("kvb", [P, T, 2 * P + 1])
        ek = sb("ek", [P, T, P])
        rk = sb("rk", [P, T, P])
        kk = sb("kk", [P, T, P])
        kvm = sb("kvm", [P, T, P + NH])
        rdn = sb("rdn", [P, T, NH])
        cx = sb("cx", [P, T, P])
        cT = sb("cT", [P, T * P])
        hs = sb("hs", [P, T, P])
        hst = sb("hst", [P, T, 6])
        hmv = sb("hmv", [P, T, 2])
        hrs = sb("hrs", [P, T])
        hn = sb("hn", [P, T, P])
        hg = sb("hg", [P, T, P])
        x1 = sb("x1", [P, T, P])
        st2 = sb("st2", [P, T, 6])
        mv2 = sb("mv2", [P, T, 2])
        rs2 = sb("rs2", [P, T])
        xn2 = sb("xn2", [P, T, P])
        xn2T = sb("xn2T", [P, T * P])
        cg = sb("cg", [CK, T * NK])
        q2 = sb("q2", [P, T * P])
        k2 = sb("k2", [P, T * NK])
        v2 = sb("v2", [NK, T, NH, 64])
        pvs = sb("pvs", [P, 2, 2 * P])
        kblk = sb("kblk", [P, T, HG, NK])
        mraw = sb("mraw", [P, 2, NH // 2])
        mclip = sb("mclip", [P, 2, NH // 2])
        z = sb("z", [P, 2, NH * NK])
        pT = sb("pT", [NK, 2, NH * P])
        rd = sb("rd", [P, HG, HG])
        ao = sb("ao", [P, T, P])
        aoT = sb("aoT", [P, T * P])
        st3 = sb("st3", [P, T, 6])
        mv3 = sb("mv3", [P, T, 2])
        rs3 = sb("rs3", [P, T])
        row = sb("row", [P, T, ROW])
        xn3T = sb("xn3T", [P, T * P])
        lg = sb("lg", [P, T, E])
        top = sb("top", [P, 2, T])
        hot = sb("hot", [P, T, 2, E])
        tie = sb("tie", [P, T, E])
        tiem = sb("tiem", [P, T])
        low = sb("low", [P, T, E])
        gap = sb("gap", [P, T])
        eg = sb("eg", [P, T])
        eg1 = sb("eg1", [P, T])
        carry = sb("carry", [P, T + 1, 2 * E])
        rank = sb("rank", [P, 2, T, 2 * E])
        pos = sb("pos", [P, T, 2 * E])
        pick = sb("pick", [P, 2, T * 2, E])
        sel = sb("sel", [P, 2, T * 2])
        over = sb("over", [P, T * 2])
        slot_f = sb("slot_f", [P, T * 2])
        slot = sb("slot", [P, T * 2], U32)

        cnt = sb("cnt", [P, 2 * E])
        cnt_i = sb("cnt_i", [P, 2 * E], I32)
        nt = sb("nt", [P, 2 * E])
        tail_f = sb("tail_f", [P, 2 * E])
        tail_i = sb("tail_i", [P, 2 * E], I32)
        ends = sb("ends", [P, 2, E])
        past = sb("past", [P, 2, 2, E])
        psum_ = sb("psum_", [P, 2, 2])
        rowf = sb("rowf", [P, 2])
        none = sb("none", [P, 2])
        tab = sb("tab", [P, 8])
        tab_i = sb("tab_i", [4, P], I32)
        xt = sb("xt", [P, 4, ROW])
        meta = sb("meta", [P, 4, 3])
        xtT = sb("xtT", [P, 2, P])
        hid = sb("hid", [P, 2, F])
        hT = sb("hT", [P, 2, F])
        ys = sb("ys", [P, 4, P])
        yt = sb("yt", [P, 4, 1], U32)
        yb = w1_s[:, 0:4 * T * P].rearrange("p (s k b h) -> p s k b h", s=2, k=2, b=T)
        ob = w1_s[:, 4 * T * P:6 * T * P].rearrange("p (s b h) -> p s b h", s=2, b=T)

        bank = [ctx.enter_context(nc.psum_tensor(f"bank{m}", [P, 512], F32)) for m in range(2)]
        S = ctx.enter_context(nc.psum_tensor("S", [P, HG, 512], F32))
        PT = [ctx.enter_context(nc.psum_tensor(f"PT{m}", [P, 512], F32)) for m in range(2)]

        ranks = S[:, HG - 1, HG * NK:HG * NK + 2 * T * 2 * E]

        weights_in, ffn_in, x_in, ctx_in = sem("weights_in"), sem("ffn_in"), sem("x_in"), sem("ctx_in")
        consts, zeroed, hmask_ready = sem("consts"), sem("zeroed"), sem("hmask_ready")
        vcopied, bo_filled, bo_ready = sem("vcopied"), sem("bo_filled"), sem("bo_ready")
        cleared = sem("cleared")
        filled = [sem(f"filled{m}") for m in range(2)]
        freed = [sem(f"freed{m}") for m in range(2)]
        stats, moments, rs_part, rs_ready = sem("stats"), sem("moments"), sem("rs_part"), sem("rs_ready")
        xn_ready, xb_ready, xbeta_ready = sem("xn_ready"), sem("xb_ready"), sem("xbeta_ready")
        eq_ready, qT_ready = sem("eq_ready"), sem("qT_ready")
        ek_ready, rk_ready, kk_ready = sem("ek_ready"), sem("rk_ready"), sem("kk_ready")
        kvm_ready, rdn_ready = sem("kvm_ready"), sem("rdn_ready")
        hstats, hmoments, hrs_part, hrs_ready = sem("hstats"), sem("hmoments"), sem("hrs_part"), sem("hrs_ready")
        hn_ready, hg_part, hg_ready, x1_ready, x1_kept = (sem("hn_ready"), sem("hg_part"), sem("hg_ready"),
                                                          sem("x1_ready"), sem("x1_kept"))
        stats2, moments2, rs2_part, rs2_ready = sem("stats2"), sem("moments2"), sem("rs2_part"), sem("rs2_ready")
        xn2_ready = sem("xn2_ready")
        kblk_ready, scored = sem("kblk_ready"), sem("scored")
        m_raw, m_clipped, z_ready, z_clipped, p_ready = (sem("m_raw"), sem("m_clipped"), sem("z_ready"),
                                                         sem("z_clipped"), sem("p_ready"))
        pt_filled, pt_freed, rd_ready = sem("pt_filled"), sem("pt_freed"), sem("rd_ready")
        stats3, moments3, rs3_part, rs3_ready = sem("stats3"), sem("moments3"), sem("rs3_part"), sem("rs3_ready")
        xn3_ready, chosen, placed, eg_ready, sent = (sem("xn3_ready"), sem("chosen"), sem("placed"),
                                                     sem("eg_ready"), sem("sent"))

        ranked, ranks_read = sem("ranked"), sem("ranks_read")
        table_steps, tails_known, tails_in = sem("table_steps"), sem("tails_known"), sem("tails_in")
        tab_ready, tabT_filled, tables_ready = sem("tab_ready"), sem("tabT_filled"), sem("tables_ready")
        xt_in, xt_used, meta_ready, xtT_ready, h_filled, hid_ready, hT_filled, hT_ready, y_filled, ys_ready, \
            y_sent = ([sem(f"{name}{m}") for m in range(4)] for name in (
                "xt_in", "xt_used", "meta_ready", "xtT_ready", "h_filled", "hid_ready", "hT_filled", "hT_ready",
                "y_filled", "ys_ready", "y_sent"))
        y_in, y_added, out_ready, out_stored = ([sem(f"{name}{m}") for m in range(2)] for name in (
            "y_in", "y_added", "out_ready", "out_stored"))
        CLEARS = 2 * NB * P // (P * 8) + 1

        block = ctx.enter_context(nc.Block())
        CHOOSE, PLACE = 12, 16

        def bc(ap, axis, n):
            ap = ap.unsqueeze(axis)
            shape = list(ap.shape)
            shape[axis] = n
            return ap.broadcast_to(shape)

        def group(t, g):
            return t[:, ds(g * T, T), :] if not isinstance(g, int) else t[:, g * T:(g + 1) * T, :]

        def wait_apart(eng, sem, count):
            if not isinstance(count, int):
                count = eng.to_reg(count)
            eng.wait_ge(consts, 5)
            eng.wait_ge(sem, count)

        def iterations(eng, body):
            for i in range(LAG["R"] + 1):
                body(i)
            with eng.Fori(LAG["R"] + 1, NG - 1) as i:
                body(i)
            for i in range(NG - 1, NG + LAG["R"]):
                body(i)

        def write_tails(sp):
            sp.wait_ge(tails_known, 1)
            sp.wait_ge(sent, NG * T * 2 * 16)
            for r in range(NREG):
                at = sp.value_load(tail_i[0:1, r:r + 1], min_val=0, max_val=EMPTY - P)
                sp.dma_start(expert_rows[ds(at, P), :], tail[:]).then_inc(tails_in, 16)

        def ffn(eng, body, last):
            for k in range(2):
                for step in range(8):
                    body(k, step // 4, step % 4)
                with eng.Fori(2, NTILE // 4) as r:
                    for u in range(4):
                        body(k, r, u)
                for u in range(last):
                    body(k, NTILE // 4, u)

        def tile_at(k, r, u, lag):
            if isinstance(r, int) and not 0 <= 4 * r + u - lag < NTILE:
                return None
            return (u - lag) % 4, k * (NTILE // 4) + r + (u - lag) // 4, r * 4 + (u - lag)

        def ffn_load(sp):
            sp.wait_ge(tables_ready, 1)
            sp.wait_ge(tails_in, NREG * 16)
            sp.wait_ge(cleared, CLEARS * 16)

            def body(k, r, u):
                t = tile_at(k, r, u, 0)
                if t is None:
                    return
                slot, used, j = t
                if not (isinstance(used, int) and used == 0):
                    sp.wait_ge(xt_used[slot], used)
                    sp.wait_ge(meta_ready[slot], used)
                col = j if isinstance(j, int) else None
                src = tab_i[k:k + 1, j:j + 1] if col is not None else tab_i[k:k + 1, ds(j, 1)]
                at = sp.value_load(src, min_val=0, max_val=EMPTY)
                sp.dma_start(xt[:, slot, :], expert_rows[ds(at, P), :]).then_inc(xt_in[slot], 16)

            ffn(sp, body, 0)

        def ffn_vector(dve):
            def body(k, r, u):
                t = tile_at(k, r, u, 0)
                if t is not None:
                    slot, used, _ = t
                    n2 = slot % 2
                    dve.wait_ge(xt_in[slot], (used + 1) * 16)
                    if not (isinstance(used, int) and used == 0):
                        dve.wait_ge(ys_ready[slot], used)
                    dve.tensor_copy(meta[:, slot, :], xt[:, slot, P:ROW]).then_inc(meta_ready[slot], 1)
                    dve.wait_ge(xt_used[slot], used + 1)
                    dve.tensor_copy(xtT[:, n2, :], bank[n2][:, 0:P]).then_inc(xtT_ready[slot], 1)
                t = tile_at(k, r, u, 1)
                if t is not None:
                    slot, used, _ = t
                    dve.wait_ge(h_filled[slot], used + 1)
                    dve.tensor_copy(hid[:, slot % 2, :], S[:, slot % 2, :]).then_inc(hid_ready[slot], 1)
                t = tile_at(k, r, u, 3)
                if t is not None:
                    slot, used, _ = t
                    if not (isinstance(used, int) and used == 0):
                        dve.wait_ge(y_sent[slot], used * 16)
                    dve.tensor_copy(yt[:, slot, :], meta[:, slot, 0:1].bitcast(I32))
                    dve.wait_ge(y_filled[slot], used + 1)
                    dve.tensor_scalar(ys[:, slot, :], PT[slot % 2][:, 0:P], meta[:, slot, 1 + k:2 + k], None,
                                      ALU.mult).then_inc(ys_ready[slot], 1)

            ffn(dve, body, 3)

        def ffn_scalar(act):
            def body(k, r, u):
                t = tile_at(k, r, u, 2)
                if t is not None:
                    slot, used, _ = t
                    act.wait_ge(hT_filled[slot], used + 1)
                    act.activation(hT[:, slot % 2, :], S[:, 2 + slot % 2, :], ACT.Gelu).then_inc(hT_ready[slot], 1)

            ffn(act, body, 2)

        def ffn_scatter(pool):
            def body(k, r, u):
                t = tile_at(k, r, u, 3)
                if t is not None:
                    slot, used, _ = t
                    wait_apart(pool, ys_ready[slot], used + 1)
                    pool.indirect_dma_start(
                        out=y_rows[k], out_offset=bass.IndirectOffsetOnAxis(ap=yt[:, slot, :], axis=0),
                        in_=ys[:, slot, :], in_offset=None,
                        bounds_check=NB * P - 1, oob_is_err=False).then_inc(y_sent[slot], 16)

            ffn(pool, body, 3)

        def ffn_tensor(pe):
            pe.wait_ge(ffn_in, 32)
            pe.wait_ge(tables_ready, 1)
            pe.wait_ge(z_ready, NB * 4)
            pe.wait_ge(pt_freed, NB * 4)

            def body(k, r, u):
                t = tile_at(k, r, u, 0)
                if t is not None:
                    slot, used, _ = t
                    pe.wait_ge(xt_in[slot], (used + 1) * 16)
                    p = tile_before(slot, used, 2)
                    if p is not None:
                        pe.wait_ge(xtT_ready[p[0]], p[1] + 1)
                    pe.transpose(bank[slot % 2][:, 0:P], xt[:, slot, 0:P], ident[:]).then_inc(xt_used[slot], 1)
                t = tile_at(k, r, u, 1)
                if t is not None:
                    slot, used, j = t
                    src = tab_i[2 + k:3 + k, j:j + 1] if isinstance(j, int) else tab_i[2 + k:3 + k, ds(j, 1)]
                    e = pe.value_load(src, min_val=0, max_val=E - 1)
                    pe.wait_ge(xtT_ready[slot], used + 1)
                    p = tile_before(slot, used, 2)
                    if p is not None:
                        pe.wait_ge(hid_ready[p[0]], p[1] + 1)
                    pe.matmul(S[:, slot % 2, :], xtT[:, slot % 2, :], w1_s[:, ds(e * F, F)],
                              start=True, stop=True).then_inc(h_filled[slot], 1)
                t = tile_at(k, r, u, 2)
                if t is not None:
                    slot, used, _ = t
                    pe.wait_ge(hid_ready[slot], used + 1)
                    p = tile_before(slot, used, 2)
                    if p is not None:
                        pe.wait_ge(hT_ready[p[0]], p[1] + 1)
                    for c in range(FC):
                        ins = pe.transpose(S[:, 2 + slot % 2, c * P:(c + 1) * P],
                                           hid[:, slot % 2, c * P:(c + 1) * P], ident[:])
                    ins.then_inc(hT_filled[slot], 1)
                t = tile_at(k, r, u, 3)
                if t is not None:
                    slot, used, j = t
                    src = tab_i[2 + k:3 + k, j:j + 1] if isinstance(j, int) else tab_i[2 + k:3 + k, ds(j, 1)]
                    e = pe.value_load(src, min_val=0, max_val=E - 1)
                    pe.wait_ge(hT_ready[slot], used + 1)
                    p = tile_before(slot, used, 2)
                    if p is not None:
                        pe.wait_ge(ys_ready[p[0]], p[1] + 1)
                    for c in range(FC):
                        ins = pe.matmul(PT[slot % 2][:, 0:P], hT[:, slot % 2, c * P:(c + 1) * P],
                                        w2_s[:, ds(e * (FC * P) + c * P, P)], start=(c == 0), stop=(c == FC - 1))
                    ins.then_inc(y_filled[slot], 1)

            ffn(pe, body, 3)

        def tile_before(slot, used, back):
            at, n = (slot - back) % 4, used + (slot - back) // 4
            return None if isinstance(n, int) and n < 0 else (at, n)

        def make_tables(dve):
            done = [0]

            def step(ins):
                ins.then_inc(table_steps, 1)
                done[0] += 1
                dve.wait_ge(table_steps, done[0])

            step(dve.tensor_scalar(cnt[:], carry[:, 0, :], float(CAP), None, ALU.min))
            step(dve.tensor_tensor(tail_f[:], cnt[:], e_f[:, 0].rearrange("p k e -> p (k e)"), ALU.add))
            dve.tensor_scalar(tail_i[:], tail_f[:], 1.0, None, ALU.add).then_inc(tails_known, 1)
            step(dve.tensor_scalar(cnt_i[:], cnt[:], float(P - 1), None, ALU.add))
            step(dve.tensor_scalar(cnt_i[:], cnt_i[:], P.bit_length() - 1, None, ALU.arith_shift_right))
            step(dve.tensor_copy(nt[:], cnt_i[:]))
            for k in range(2):
                step(dve.tensor_tensor_scan(ends[:, k, :], ones[:, 0:E], nt[:, k * E:(k + 1) * E], 0.0,
                                            ALU.mult, ALU.add))
            step(dve.tensor_scalar(past[:, 0], ends[:], j_f[:], None, ALU.is_le))
            step(dve.tensor_tensor(past[:, 1], past[:, 0], nt[:].rearrange("p (k e) -> p k e", k=2), ALU.mult))
            step(dve.tensor_reduce(psum_[:], past[:], AX.X, ALU.add))
            step(dve.tensor_scalar(rowf[:], psum_[:, 1], j_f[:], -float(P), ALU.subtract, ALU.mult))
            step(dve.scalar_tensor_tensor(out=rowf[:], in0=psum_[:, 0], scalar=float(REG), in1=rowf[:],
                                          op0=ALU.mult, op1=ALU.add))
            step(dve.tensor_scalar(rowf[:, 1:2], rowf[:, 1:2], float(E * REG), None, ALU.add))
            step(dve.tensor_scalar(none[:], psum_[:, 0], float(E), float(EMPTY), ALU.is_ge, ALU.mult))
            step(dve.tensor_tensor(tab[:, 0:2], rowf[:], none[:], ALU.max))
            step(dve.tensor_scalar(tab[:, 0:2], tab[:, 0:2], float(EMPTY), None, ALU.min))
            step(dve.tensor_scalar(tab[:, 2:4], psum_[:, 0], float(E - 1), None, ALU.min))
            dve.tensor_copy(tab[:, 4:8], tab[:, 0:4]).then_inc(tab_ready, 1)
            dve.wait_ge(tabT_filled, 1)
            dve.tensor_copy(tab_i[:], bank[0][0:4, 0:P]).then_inc(tables_ready, 1)

        def load_y(sp):
            for slot in range(4):
                sp.wait_ge(y_sent[slot], 2 * (NTILE // 4) * 16)

            def body(r, u):
                if not (isinstance(r, int) and r == 0):
                    sp.wait_ge(y_added[u], r)
                g = r * 2 + u
                for k in range(2):
                    src = (y_rows[k][g * T * P:(g + 1) * T * P] if isinstance(g, int)
                           else y_rows[k][ds(g * (T * P), T * P)])
                    sp.dma_start(yb[:, u, k], src.rearrange("(b s) h -> s b h", s=P)).then_inc(y_in[u], 16)

            halves(sp, body)

        def halves(eng, body):
            for u in range(2):
                body(0, u)
            with eng.Fori(1, NG // 2) as r:
                for u in range(2):
                    body(r, u)

        def combine(dve):
            def body(r, u):
                dve.wait_ge(y_in[u], (r + 1) * 32)
                if not (isinstance(r, int) and r == 0):
                    dve.wait_ge(out_stored[u], r * 16)
                dve.tensor_tensor(ob[:, u], yb[:, u, 0], yb[:, u, 1], ALU.add).then_inc(y_added[u], 1)
                dve.wait_ge(y_added[u], r + 1)
                dve.tensor_tensor(ob[:, u], ob[:, u], group(xs, r * 2 + u), ALU.add).then_inc(out_ready[u], 1)

            halves(dve, body)

        def store_out(act):
            def body(r, u):
                g = r * 2 + u
                act.wait_ge(out_ready[u], r + 1)
                dst = out[g * T:(g + 1) * T] if isinstance(g, int) else out[ds(g * T, T)]
                act.dma_start(dst.rearrange("b s h -> s b h"), ob[:, u]).then_inc(out_stored[u], 16)

            halves(act, body)
            for u in range(2):
                act.wait_ge(out_stored[u], NG // 2 * 16)

        @block.tensor
        def _(pe):
            pe.wait_ge(vcopied, 2)
            pe.matmul(PT[0][:, 0:P], bv2c[:], wA_s[:, W_O2], start=True, stop=True).then_inc(bo_filled, 1)
            pe.wait_ge(consts, 5)
            pe.wait_ge(bo_ready, 1)

            def begin(name, i):
                m, u = use_of(name, i)
                if not (isinstance(u, int) and u == 0):
                    pe.wait_ge(freed[m], u)
                return bank[m], filled[m]

            def scores(g, b, ranks_before):
                n = g * T + b
                pe.wait_ge(kblk_ready, n + 1)
                for q in range(HG):
                    if not (isinstance(n, int) and n == 0):
                        pe.wait_ge(z_ready, n * 4 - 3 + q)
                    if q == HG - 1 and b == 0 and not (isinstance(ranks_before, int) and ranks_before < 1):
                        pe.wait_ge(ranks_read, ranks_before)
                    ins = pe.matmul(S[:, q, 0:HG * NK], q2[32 * q:32 * q + 32, b * P:(b + 1) * P],
                                    kblk[32 * q:32 * q + 32, b].rearrange("p h k -> p (h k)"),
                                    start=True, stop=True)
                    if q % 2:
                        ins.then_inc(scored, 1)

            def weights_by_values(g, b, i):
                n = g * T + b
                pe.wait_ge(p_ready, n + 1)

                def transposes(c):
                    if not (isinstance(n, int) and n == 0 and c < 2):
                        pe.wait_ge(pt_freed, n * 4 + c - 1)
                    for h in range(HG):
                        at = (c * HG + h) * NK
                        ins = pe.transpose(PT[c % 2][0:NK, h * P:(h + 1) * P], z[:, b % 2, at:at + NK], ident[:])
                    ins.then_inc(pt_filled, 1)

                transposes(0)
                transposes(1)
                pv, done = begin(f"pv{b}", i)
                for q in range(HG):
                    pe.wait_ge(pt_freed, n * 4 + q + 1)
                    at = slice(64 * (q % 2), 64 * (q % 2) + 64)
                    for j in range(HG):
                        h = q * HG + j
                        ins = pe.matmul(pv[at, (q // 2) * P:(q // 2 + 1) * P], v2[:, b, h, :],
                                        pT[:, b % 2, h * P:(h + 1) * P], start=(j == 0), stop=(j == HG - 1))
                    if q < 2:
                        transposes(q + 2)
                ins.then_inc(done, 1)

            def output_T(g, b, i):
                m, u = use_of(f"pv{b}", i)
                pe.wait_ge(freed[m], u + 1)
                dst, done = begin(f"pvT{b}", i)
                for half in range(2):
                    ins = pe.transpose(dst[:, half * P:(half + 1) * P], pvs[:, b % 2, half * P:(half + 1) * P],
                                       ident[:])
                ins.then_inc(done, 1)

            def each_tile(name, i, lhsT, rhs, width=P, tiles=range(T)):
                dst, done = begin(name, i)
                for n, b in enumerate(tiles):
                    ins = pe.matmul(dst[:, n * width:(n + 1) * width], lhsT(b), rhs(b), start=True, stop=True)
                ins.then_inc(done, 1)

            def transpose_tiles(name, i, src):
                dst, done = begin(name, i)
                for b in range(T):
                    ins = pe.transpose(dst[:, b * P:(b + 1) * P], src(b), ident[:])
                ins.then_inc(done, 1)

            def part(ap):
                return lambda b: ap[:, b * P:(b + 1) * P]

            def body(i):
                L, M, X, R = (runs(stage, i) for stage in "LMXR")
                gm, gx, gr = (i - LAG[stage] for stage in "MXR")
                if L:
                    pe.wait_ge(xn_ready, i * T + T)
                    transpose_tiles("xnT", i, lambda b: xn[:, b, :])
                if X:
                    scores(gx, 0, gr)
                if R:
                    transpose_tiles("aoT", i, lambda b: ao[:, b, :])
                if M:
                    pe.wait_ge(xn2_ready, gm * T + T)
                    transpose_tiles("xn2T", i, lambda b: xn2[:, b, :])
                if L:
                    m, u = use_of("xnT", i)
                    pe.wait_ge(freed[m], u + 1)
                    dst, done = begin("q", i)
                    pe.matmul(dst[:], wA_s[:, W_Q], xnT[:], start=True, stop=True).then_inc(done, 1)
                    for half in range(2):
                        each_tile(f"kp{half}", i, part(xnT),
                                  lambda b: wA_s[:, W_K:W_V + 1].rearrange("p a h -> p (a h)"),
                                  width=2 * P, tiles=range(2 * half, 2 * half + 2))
                if R:
                    m, u = use_of("aoT", i)
                    pe.wait_ge(freed[m], u + 1)
                    each_tile("x2", i, part(aoT), lambda b: wA_s[:, W_O2])
                if X:
                    scores(gx, 1, gr)
                if X:
                    weights_by_values(gx, 0, i)
                if L:
                    m, u = use_of("kp1", i)
                    pe.wait_ge(freed[m], u + 1)
                    pe.wait_ge(kk_ready, i + 1)
                    for half in range(2):
                        each_tile(f"kv{half}", i, lambda b: kk[:, b, :], lambda b: kvb[:, b, P:2 * P + 1],
                                  width=P + 1, tiles=range(2 * half, 2 * half + 2))
                if X:
                    output_T(gx, 0, i)
                if L:
                    pe.wait_ge(qT_ready, i + 1)
                    numerators(i, 0)
                    numerators(i, 1)
                if X:
                    scores(gx, 2, gr)
                if L:
                    m, u = use_of("nd1", i)
                    pe.wait_ge(freed[m], u + 1)
                    transpose_tiles("cT", i, lambda b: cx[:, b, :])
                if X:
                    weights_by_values(gx, 1, i)
                if L:
                    m, u = use_of("cT", i)
                    pe.wait_ge(freed[m], u + 1)
                    each_tile("hs", i, part(cT), lambda b: wA_s[:, W_D])
                if X:
                    output_T(gx, 1, i)
                    scores(gx, 3, gr)
                if R:
                    pe.wait_ge(xn3_ready, gr * T + T)
                    transpose_tiles("xn3T", i, lambda b: row[:, b, 0:P])
                if X:
                    weights_by_values(gx, 2, i)
                if M:
                    pe.wait_ge(ctx_in, gm * 16 + 16)
                    dst, done = begin("k2T", i)
                    pe.matmul(dst[:, 0:T * NK], wC_s[:, 0], cg[:], start=True, stop=True).then_inc(done, 1)
                if X:
                    output_T(gx, 2, i)
                if R:
                    m, u = use_of("xn3T", i)
                    pe.wait_ge(freed[m], u + 1)
                    each_tile("logits", i, part(xn3T), lambda b: wr_s[:], width=E)
                if M:
                    m, u = use_of("xn2T", i)
                    pe.wait_ge(freed[m], u + 1)
                    dst, done = begin("q2T", i)
                    pe.matmul(dst[:], wA_s[:, W_Q2], xn2T[:], start=True, stop=True).then_inc(done, 1)
                if X:
                    weights_by_values(gx, 3, i)
                if M:
                    dst, done = begin("v2", i)
                    for b in range(T):
                        ins = pe.matmul(dst[0:NK, b * P:(b + 1) * P], cg[:, b * NK:(b + 1) * NK], wC_s[:, 1],
                                        start=True, stop=True)
                    ins.then_inc(done, 1)
                if X:
                    output_T(gx, 3, i)
                if R:
                    pe.wait_ge(chosen, (gr + 1) * CHOOSE)
                    pe.wait_ge(z_ready, (gx * T + T) * 4 if X else NB * 4)
                    flat = hot[:].rearrange("p b k e -> p (b k e)")
                    pe.matmul(ranks[:, 0:T * 2 * E], before[:], flat, start=True, stop=True)
                    pe.matmul(ranks[:, T * 2 * E:], ones[:], flat, start=True, stop=True).then_inc(ranked, 1)

            def numerators(i, half):
                m, u = use_of(f"kv{half}", i)
                pe.wait_ge(freed[m], u + 1)
                each_tile(f"nd{half}", i, part(qT), lambda b: kvm[:, b, :], width=P + NH,
                          tiles=range(2 * half, 2 * half + 2))

            iterations(pe, body)
            pe.wait_ge(tab_ready, 1)
            pe.transpose(bank[0][0:4, 0:P], tab[:, 4:8], ident[:]).then_inc(tabT_filled, 1)
            ffn_tensor(pe)

        @block.sync
        def _(sp):
            sp.dma_start(vb[:], vrow.unsqueeze(0).broadcast_to([P, NV, P])).then_inc(weights_in, 16)
            sp.dma_start(vc[:], vcol).then_inc(weights_in, 16)
            sp.dma_start(wA_s[:], wA).then_inc(weights_in, 16)
            sp.dma_start(wC_s[:], wC).then_inc(weights_in, 16)
            sp.dma_start(wr_s[:], wr).then_inc(weights_in, 16)

            def load_x(g):
                if not (isinstance(g, int) and g == 0):
                    sp.wait_ge(x_in, g * 16)
                src = x[ds(g * T, T)] if not isinstance(g, int) else x[g * T:(g + 1) * T]
                sp.dma_start(group(xs, g), src.rearrange("b s h -> s b h")).then_inc(x_in, 16)

            def load_ctx(g):
                c = T * NK
                if not (isinstance(g, int) and g == 0):
                    b, n = use_of("v2", g - 1 + LAG["M"])
                    sp.wait_ge(filled[b], n + 1)
                src = ctxT[:, ds(g * c, c)] if not isinstance(g, int) else ctxT[:, g * c:(g + 1) * c]
                sp.dma_start(cg[:], src).then_inc(ctx_in, 16)

            load_x(0)
            load_ctx(0)
            load_x(1)
            sp.dma_start(w1_s[:], w1).then_inc(ffn_in, 16)
            sp.dma_start(w2_s[:], w2).then_inc(ffn_in, 16)
            load_x(2)
            load_ctx(1)
            load_x(3)
            load_ctx(2)
            with sp.Fori(3, NG - 1) as g:
                load_x(g + 1)
                load_ctx(g)
            load_ctx(NG - 1)
            write_tails(sp)
            ffn_load(sp)
            load_y(sp)

        @block.scalar
        def _(act):
            act.wait_ge(zeroed, 2)
            for rows in y_rows:
                flat = rows.rearrange("(a p r) h -> a p (r h)", p=P, r=8)
                for a in range(flat.shape[0]):
                    act.dma_start(flat[a], zeros[:]).then_inc(cleared, 16)
            act.dma_start(expert_rows[EMPTY:EMPTY + P, :], tail[:]).then_inc(cleared, 16)

            act.wait_ge(weights_in, 80)
            act.mul(bq2s[:], vc[:, V_BQ2:V_BQ2 + 1], SCALE).then_inc(vcopied, 1)
            act.wait_ge(consts, 1)
            act.activation(bv2c[:], ones[:], ACT.Copy, scale=vc[:, V_BV2:V_BV2 + 1]).then_inc(vcopied, 1)
            act.wait_ge(vcopied, 2)

            def empty(dst, name, i, cols=512, rows=P, **kw):
                b, n = use_of(name, i)
                act.wait_ge(filled[b], n + 1)
                if kw:
                    act.activation(dst, bank[b][0:rows, 0:cols], ACT.Identity, **kw).then_inc(freed[b], 1)
                else:
                    act.copy(dst, bank[b][0:rows, 0:cols]).then_inc(freed[b], 1)

            def exponentials(g, b):
                n = g * T + b
                act.wait_ge(z_clipped, n + 1)
                act.activation(z[:, b % 2, :], z[:, b % 2, :], ACT.Exp).then_inc(p_ready, 1)

            def weights_T(g, b, i):
                n = g * T + b
                for c in range(4):
                    act.wait_ge(pt_filled, n * 4 + c + 1)
                    act.copy(pT[:, b % 2, c * 512:(c + 1) * 512], PT[c % 2][0:NK, :]).then_inc(pt_freed, 1)
                empty(pvs[:, b % 2, :], f"pv{b}", i, cols=2 * P)

            def body(i):
                L, M, X, R = (runs(stage, i) for stage in "LMXR")
                gm, gx, gr = (i - LAG[stage] for stage in "MXR")
                if L:
                    empty(xnT[:], "xnT", i)
                if R:
                    empty(aoT[:], "aoT", i)
                if M:
                    empty(xn2T[:], "xn2T", i)
                if L:
                    b, n = use_of("q", i)
                    act.wait_ge(filled[b], n + 1)
                    act.activation(eq[:], bank[b][:], ACT.Exp, bias=vc[:, V_BQ:V_BQ + 1]).then_inc(eq_ready, 1)
                    act.activation(rq[:], bank[b][:], ACT.Relu, bias=vc[:, V_BQ:V_BQ + 1]).then_inc(freed[b], 1)
                if X:
                    exponentials(gx, 0)
                if L:
                    for half in range(2):
                        b, n = use_of(f"kp{half}", i)
                        act.wait_ge(freed[b], n + 1)
                    act.activation(ek[:], kvb[:, :, 0:P], ACT.Exp).then_inc(ek_ready, 1)
                    act.activation(rk[:], kvb[:, :, 0:P], ACT.Relu).then_inc(rk_ready, 1)
                if X:
                    weights_T(gx, 0, i)
                    exponentials(gx, 1)
                if L:
                    empty(cT[:], "cT", i)
                if X:
                    weights_T(gx, 1, i)
                    exponentials(gx, 2)
                if R:
                    empty(xn3T[:], "xn3T", i)
                if X:
                    weights_T(gx, 2, i)
                if M:
                    empty(k2[:], "k2T", i, cols=T * NK, bias=vc[:, V_BK2:V_BK2 + 1])
                if X:
                    exponentials(gx, 3)
                if M:
                    empty(q2[:], "q2T", i, bias=bq2s[:], scale=SCALE)
                if X:
                    weights_T(gx, 3, i)
                if M:
                    m, u = use_of("v2", i)
                    act.wait_ge(filled[m], u + 1)
                    heads = bank[m][0:NK, :].rearrange("k (g j d) -> k g j d", j=HG, d=HD)
                    into = v2[:].rearrange("k b (q j) c -> k (b q) j c", j=HG)
                    for j in range(HG):
                        ins = act.copy(into[:, :, j, j * HD:(j + 1) * HD], heads[:, :, j, :])
                    ins.then_inc(freed[m], 1)
                if R:
                    act.wait_ge(chosen, (gr + 1) * CHOOSE)
                    act.activation(eg[:], gap[:], ACT.Exp).then_inc(eg_ready, 1)

            iterations(act, body)
            ffn_scalar(act)
            store_out(act)

        @block.gpsimd
        def _(pool):
            pool.memset(ones[:], 1.0).then_inc(consts, 1)
            pool.memset(expo[:], -0.5)
            pool.memset(zeros[:], 0.0)
            pool.memset(tail[:], 0.0)
            pool.memset(carry[:], 0.0)
            pool.memset(ident[:], 0.0)
            pool.memset(before[:], 1.0)
            pool.memset(bmask[:], 1.0)
            pool.iota(tok_i[:], pattern=[[P, NB]], base=0, channel_multiplier=1)
            pool.iota(e_i[:, 0], pattern=[[E * REG, 2], [REG, E]], base=-1, channel_multiplier=0)
            pool.iota(e_i[:, 1], pattern=[[0, 2], [-1, E]], base=E, channel_multiplier=0)
            pool.iota(e_i[:, 2], pattern=[[0, 2], [1, E]], base=0, channel_multiplier=0)
            pool.iota(j_i[:], pattern=[[0, 1]], base=0, channel_multiplier=1)
            pool.memset(kvb[:], 1.0)
            pool.memset(v2[:], 0.0).then_inc(zeroed, 1)
            pool.wait_ge(zeroed, 1)
            for j in range(HG):
                pool.memset(v2[:].rearrange("k b (q j) c -> k (b q) j c", j=HG)[:, :, j, 32 + j:33 + j], 1.0)
            pool.iota(tail[:, P:P + 1].bitcast(I32), pattern=[[0, 1]], base=int(BIG), channel_multiplier=0)\
                .then_inc(zeroed, 1)
            pool.affine_select(out=ident[:], in_=ident[:], compare_op=ALU.not_equal, fill=1.0, base=0,
                               pattern=[[-1, P]], channel_multiplier=1)
            pool.affine_select(out=before[:], in_=before[:], compare_op=ALU.is_ge, fill=0.0, base=0,
                               pattern=[[1, P]], channel_multiplier=-1)
            heads = bmask[:].rearrange("p (h d) -> p h d", d=HD)
            pool.affine_select(out=heads, in_=heads, compare_op=ALU.is_ge, fill=0.0, base=0,
                               pattern=[[-HD, NH], [0, HD]], channel_multiplier=1).then_inc(consts, 1)
            pool.wait_ge(consts, 2)
            pool.affine_select(out=heads, in_=heads, compare_op=ALU.is_ge, fill=0.0, base=HD - 1,
                               pattern=[[HD, NH], [0, HD]], channel_multiplier=-1).then_inc(consts, 1)
            pool.tensor_copy(e_f[:], e_i[:]).then_inc(consts, 1)
            pool.tensor_copy(j_f[:], j_i[:]).then_inc(consts, 1)

            def inverse_root(dst, variance, eps, moments, part, ready, g):
                wait_apart(pool, moments, g * T + T)
                pool.tensor_scalar(dst[:], variance, eps, None, ALU.add).then_inc(part, 1)
                pool.wait_ge(part, g + 1)
                pool.tensor_tensor(dst[:], dst[:], expo[:], ALU.pow).then_inc(ready, 1)

            pool.wait_ge(weights_in, 80)
            pool.wait_ge(hmask_ready, 2)
            pool.wait_ge(bo_ready, 1)

            def body(i):
                N, L, M, R = (runs(stage, i) for stage in "NLMR")
                gm, gr = (i - LAG[stage] for stage in "MR")
                if L:
                    pool.wait_ge(xn_ready, i * T + T)
                    pool.tensor_tensor(xb[:], xn[:], bc(vb[:, V_BD], 1, T), ALU.add).then_inc(xb_ready, 1)
                    pool.tensor_tensor(xbeta[:], group(xs, i), bc(vb[:, V_BETA], 1, T), ALU.add)\
                        .then_inc(xbeta_ready, 1)
                if R:
                    inverse_root(rs3, mv3[:, :, 1], EPS, moments3, rs3_part, rs3_ready, gr)
                if L:
                    inverse_root(hrs, hmv[:, :, 1], EPS_ATTN_LN, hmoments, hrs_part, hrs_ready, i)
                    pool.wait_ge(hn_ready, i * T + T)
                    pool.tensor_tensor(hg[:], hn[:], bc(vb[:, V_GAMMA], 1, T), ALU.mult).then_inc(hg_ready, 1)
                    inverse_root(rs2, mv2[:, :, 1], EPS, moments2, rs2_part, rs2_ready, i)
                if N:
                    inverse_root(rs, mv[:, :, 1], EPS, moments, rs_part, rs_ready, i + 1)
                if L:
                    wait_apart(pool, x1_ready, i + 1)
                    pool.tensor_tensor(group(xs, i), x1[:], bc(bo_all[:], 1, T), ALU.add).then_inc(x1_kept, 1)
                if M:
                    m, u = use_of("k2T", i)
                    pool.wait_ge(freed[m], u + 1)
                    for b in range(T):
                        pool.tensor_tensor(kblk[:, b], bc(k2[:, b * NK:(b + 1) * NK], 1, HG),
                                           bc(hmask[:], 2, NK), ALU.mult).then_inc(kblk_ready, 1)
                if R:
                    wait_apart(pool, placed, (gr + 1) * PLACE)
                    for b in range(T):
                        for k in range(2):
                            pool.indirect_dma_start(
                                out=expert_rows, out_offset=bass.IndirectOffsetOnAxis(
                                    ap=slot[:, b * 2 + k:b * 2 + k + 1], axis=0),
                                in_=row[:, b, :], in_offset=None,
                                bounds_check=EMPTY - 1, oob_is_err=False).then_inc(sent, 16)

            inverse_root(rs, mv[:, :, 1], EPS, moments, rs_part, rs_ready, 0)
            iterations(pool, body)
            ffn_scatter(pool)

        @block.vector
        def _(dve):
            dve.wait_ge(consts, 5)
            dve.tensor_reduce(hmask[:], bmask[:].rearrange("p (q j d) -> p j q d", q=HG, d=HD)[:, :, :, 0],
                              AX.X, ALU.add).then_inc(hmask_ready, 1)
            dve.tensor_copy(hmask16[:], bmask[:].rearrange("p (h d) -> p h d", d=HD)[:, :, 0]).then_inc(hmask_ready, 1)
            dve.wait_ge(hmask_ready, 2)
            dve.wait_ge(bo_filled, 1)
            dve.tensor_tensor(bo_all[:], PT[0][:, 0:P], vb[:, V_BO2], ALU.add).then_inc(bo_ready, 1)

            def moments_of(src, st, mv, sem_stats, sem_moments, g):
                for b in range(T):
                    dve.bn_stats(st[:, b, :], src(b)).then_inc(sem_stats, 1)
                for b in range(T):
                    wait_apart(dve, sem_stats, g * T + b + 1)
                    dve.bn_aggr(mv[:, b, :], st[:, b, :]).then_inc(sem_moments, 1)

            def normal(dst, src, mv, rs, rs_ready, ready, g):
                dve.wait_ge(rs_ready, g + 1)
                for b in range(T):
                    dve.tensor_scalar(dst(b), src(b), mv[:, b, 0:1], rs[:, b:b + 1], ALU.subtract, ALU.mult)\
                       .then_inc(ready, 1)

            def tile_of(g):
                return lambda b: (xs[:, g * T + b, :] if isinstance(g, int)
                                  else xs[:, ds(g * T + b, 1), :].rearrange("p a h -> p (a h)"))

            def softmax_shift(g, b):
                n = g * T + b
                for half in range(2):
                    qs = slice(2 * half, 2 * half + 2)
                    dve.wait_ge(scored, n * 2 + half + 1)
                    dve.tensor_reduce(mraw[:, half, :].rearrange("p (q h) -> p q h", q=2),
                                      S[:, qs, 0:HG * NK].rearrange("p q (h k) -> p q h k", k=NK),
                                      AX.X, ALU.max).then_inc(m_raw, 1)
                    dve.wait_ge(m_raw, n * 2 + half + 1)
                    dve.tensor_scalar(mclip[:, half, :], mraw[:, half, :], CLAMP, -CLAMP, ALU.min, ALU.max)\
                       .then_inc(m_clipped, 1)
                    dve.wait_ge(m_clipped, n * 2 + half + 1)
                    if not (isinstance(n, int) and n < 2):
                        dve.wait_ge(pt_filled, n * 4 - 4)
                    for q in range(2):
                        c = (2 * half + q) * HG * NK
                        dve.scalar_tensor_tensor(
                            out=z[:, b % 2, c:c + HG * NK].rearrange("p (h k) -> p h k", k=NK),
                            in0=S[:, 2 * half + q, 0:HG * NK].rearrange("p (h k) -> p h k", k=NK),
                            scalar=-CLAMP, in1=bc(mclip[:, half, q * HG:(q + 1) * HG], 2, NK),
                            op0=ALU.max, op1=ALU.subtract).then_inc(z_ready, 1)

                dve.wait_ge(z_ready, n * 4 + 4)
                dve.tensor_scalar(z[:, b % 2, :], z[:, b % 2, :], 0.0, None, ALU.min).then_inc(z_clipped, 1)

            def softmax_divide(g, b, i):
                n = g * T + b
                m, u = use_of(f"pvT{b}", i)
                pv = bank[m][:, 0:2 * P].rearrange("p (q c) -> p q c", c=64)
                dve.wait_ge(filled[m], u + 1)
                dve.reciprocal(rd[:], pv[:, :, 32:32 + HG]).then_inc(rd_ready, 1)
                dve.wait_ge(rd_ready, n + 1)
                dve.tensor_tensor(ao[:, b, :].rearrange("p (q j d) -> p q j d", j=HG, d=HD),
                                  pv[:, :, 0:32].rearrange("p q (j d) -> p q j d", d=HD),
                                  bc(rd[:], 3, HD), ALU.mult).then_inc(freed[m], 1)

            def choose(g, i):
                done = [0]

                def step(ins):
                    ins.then_inc(chosen, 1)
                    done[0] += 1

                def settle():
                    dve.wait_ge(chosen, g * CHOOSE + done[0])

                m, u = use_of("logits", i)
                dve.wait_ge(filled[m], u + 1)
                dve.tensor_copy(lg[:], bank[m][:, 0:T * E].rearrange("p (b e) -> p b e", e=E)).then_inc(freed[m], 1)
                dve.wait_ge(freed[m], u + 1)
                src = lg
                for k in range(2):
                    step(dve.tensor_reduce(top[:, k, :], src[:], AX.X, ALU.max))
                    settle()
                    step(dve.tensor_tensor(tie[:], src[:], bc(top[:, k, :], 2, E), ALU.is_equal))
                    settle()
                    step(dve.tensor_tensor(tie[:], tie[:], bc(e_f[:, 1, 0, :], 1, T), ALU.mult))
                    settle()
                    step(dve.tensor_reduce(tiem[:], tie[:], AX.X, ALU.max))
                    settle()
                    step(dve.tensor_tensor(hot[:, :, k, :], bc(e_f[:, 1, 0, :], 1, T), bc(tiem[:], 2, E),
                                           ALU.is_equal))
                    if k == 0:
                        settle()
                        step(dve.scalar_tensor_tensor(out=low[:], in0=hot[:, :, 0, :], scalar=-3e38,
                                                      in1=lg[:], op0=ALU.mult, op1=ALU.add))
                        settle()
                        src = low
                step(dve.tensor_tensor(gap[:], top[:, 1, :], top[:, 0, :], ALU.subtract))
                assert done[0] == CHOOSE

            def place(g):
                done = [0]

                def step(ins):
                    ins.then_inc(placed, 1)
                    done[0] += 1

                def settle():
                    dve.wait_ge(placed, g * PLACE + done[0])

                dve.wait_ge(ranked, g + 1)
                dve.tensor_copy(rank[:].rearrange("p a b e -> p (a b e)"), ranks).then_inc(ranks_read, 1)
                dve.wait_ge(eg_ready, g + 1)
                step(dve.tensor_scalar(eg1[:], eg[:], 1.0, None, ALU.add))
                settle()
                step(dve.reciprocal(row[:, :, P + 1], eg1[:]))
                settle()
                step(dve.tensor_tensor(row[:, :, P + 2], eg[:], row[:, :, P + 1], ALU.mult))
                toks = tok_i[:, g * T:(g + 1) * T] if isinstance(g, int) else tok_i[:, ds(g * T, T)]
                step(dve.tensor_copy(row[:, :, P].bitcast(I32), toks))
                wait_apart(dve, ranks_read, g + 1)
                for b in range(T):
                    if b:
                        settle()
                    step(dve.tensor_tensor(carry[:, b + 1, :], carry[:, b, :], rank[:, 1, b, :], ALU.add))
                settle()
                step(dve.tensor_tensor(pos[:], rank[:, 0], carry[:, 0:T, :], ALU.add))
                settle()
                step(dve.tensor_copy(carry[:, 0, :], carry[:, T, :]))
                hot8 = hot[:].rearrange("p b k e -> p (b k) e")
                step(dve.tensor_tensor(pick[:, 0], hot8, pos[:].rearrange("p b (k e) -> p (b k) e", k=2), ALU.mult))
                step(dve.tensor_tensor(pick[:, 1].rearrange("p (b k) e -> p b (k e)", k=2),
                                       hot[:].rearrange("p b k e -> p b (k e)"),
                                       bc(e_f[:, 0].rearrange("p k e -> p (k e)"), 1, T), ALU.mult))
                settle()
                step(dve.tensor_reduce(sel[:], pick[:], AX.X, ALU.add))
                settle()
                step(dve.tensor_scalar(over[:], sel[:, 0], float(CAP), BIG, ALU.is_gt, ALU.mult))
                step(dve.tensor_tensor(slot_f[:], sel[:, 0], sel[:, 1], ALU.add))
                settle()
                step(dve.tensor_tensor(slot[:], slot_f[:], over[:], ALU.add))
                assert done[0] == PLACE

            def body(i):
                N, L, X, R = (runs(stage, i) for stage in "NLXR")
                gx, gr = (i - LAG[stage] for stage in "XR")
                if X:
                    softmax_shift(gx, 0)
                if L:
                    dve.wait_ge(eq_ready, i + 1)
                    m, u = use_of("q", i)
                    dve.wait_ge(freed[m], u + 1)
                    dve.scalar_tensor_tensor(out=qT[:], in0=eq[:], scalar=1.0, in1=rq[:], op0=ALU.min, op1=ALU.add)\
                       .then_inc(qT_ready, 1)
                    for half in range(2):
                        m, u = use_of(f"kp{half}", i)
                        dve.wait_ge(filled[m], u + 1)
                        dve.tensor_tensor(kvb[:, 2 * half:2 * half + 2, 0:2 * P],
                                          bank[m][:].rearrange("p (b h) -> p b h", b=2),
                                          bc(vb[:, V_BK:V_BV + 1].rearrange("p a h -> p (a h)"), 1, 2),
                                          ALU.add).then_inc(freed[m], 1)
                if R:
                    m, u = use_of("x2", i)
                    dve.wait_ge(filled[m], u + 1)
                    dve.wait_ge(x1_kept, gr + 1)
                    dve.tensor_tensor(group(xs, gr), bank[m][:].rearrange("p (b h) -> p b h", b=T),
                                      group(xs, gr), ALU.add).then_inc(freed[m], 1)
                if L:
                    dve.wait_ge(ek_ready, i + 1)
                    dve.wait_ge(rk_ready, i + 1)
                    dve.scalar_tensor_tensor(out=kk[:], in0=ek[:], scalar=1.0, in1=rk[:], op0=ALU.min, op1=ALU.add)\
                       .then_inc(kk_ready, 1)
                if X:
                    softmax_shift(gx, 1)
                if R:
                    m, u = use_of("x2", i)
                    wait_apart(dve, freed[m], u + 1)
                    moments_of(tile_of(gr), st3, mv3, stats3, moments3, gr)
                if L:
                    for half in range(2):
                        m, u = use_of(f"kv{half}", i)
                        pair = slice(2 * half, 2 * half + 2)
                        got = bank[m][:, 0:2 * (P + 1)].rearrange("p (b h) -> p b h", b=2)
                        dve.wait_ge(filled[m], u + 1)
                        dve.tensor_tensor(kvm[:, pair, 0:P], got[:, :, 0:P], bc(bmask[:], 1, 2), ALU.mult)\
                           .then_inc(kvm_ready, 1)
                        dve.scalar_tensor_tensor(out=kvm[:, pair, P:P + NH],
                                                 in0=got[:, :, P:P + 1].broadcast_to([P, 2, NH]), scalar=EPS_ATTN,
                                                 in1=bc(hmask16[:], 1, 2), op0=ALU.add, op1=ALU.mult)\
                           .then_inc(freed[m], 1)
                if X:
                    softmax_divide(gx, 0, i)
                if L:
                    attention_divide(i, 0)
                    attention_divide(i, 1)
                if R:
                    if not (isinstance(gr, int) and gr == 0):
                        dve.wait_ge(sent, gr * (T * 2 * 16))
                    normal(lambda b: row[:, b, 0:P], tile_of(gr), mv3, rs3, rs3_ready, xn3_ready, gr)
                if X:
                    softmax_shift(gx, 2)
                if L:
                    m, u = use_of("hs", i)
                    dve.wait_ge(filled[m], u + 1)
                    dve.wait_ge(xb_ready, i + 1)
                    dve.tensor_tensor(hs[:], bank[m][:].rearrange("p (b h) -> p b h", b=T), xb[:], ALU.add)\
                       .then_inc(freed[m], 1)
                    wait_apart(dve, freed[m], u + 1)
                    moments_of(lambda b: hs[:, b, :], hst, hmv, hstats, hmoments, i)
                if X:
                    softmax_divide(gx, 1, i)
                if L:
                    normal(lambda b: hn[:, b, :], lambda b: hs[:, b, :], hmv, hrs, hrs_ready, hn_ready, i)
                if X:
                    softmax_shift(gx, 3)
                if L:
                    dve.wait_ge(hg_ready, i + 1)
                    dve.wait_ge(xbeta_ready, i + 1)
                    dve.tensor_tensor(x1[:], hg[:], xbeta[:], ALU.add).then_inc(x1_ready, 1)
                    wait_apart(dve, x1_ready, i + 1)
                    moments_of(lambda b: x1[:, b, :], st2, mv2, stats2, moments2, i)
                if N:
                    wait_apart(dve, x_in, (i + 1) * 16 + 16)
                    moments_of(tile_of(i + 1), st, mv, stats, moments, i + 1)
                if X:
                    softmax_divide(gx, 2, i)
                if R:
                    choose(gr, i)
                if L:
                    normal(lambda b: xn2[:, b, :], lambda b: x1[:, b, :], mv2, rs2, rs2_ready, xn2_ready, i)
                if N:
                    normal(lambda b: xn[:, b, :], tile_of(i + 1), mv, rs, rs_ready, xn_ready, i + 1)
                if X:
                    softmax_divide(gx, 3, i)
                if R:
                    place(gr)

            def attention_divide(i, half):
                m, u = use_of(f"nd{half}", i)
                pair = slice(2 * half, 2 * half + 2)
                got = bank[m][:, 0:2 * (P + NH)].rearrange("p (b h) -> p b h", b=2)
                dve.wait_ge(filled[m], u + 1)
                dve.reciprocal(rdn[:, pair, :], got[:, :, P:P + NH]).then_inc(rdn_ready, 1)
                dve.wait_ge(rdn_ready, i * 2 + half + 1)
                dve.tensor_tensor(cx[:, pair, :].rearrange("p b (h d) -> p b h d", d=HD),
                                  got[:, :, 0:P].rearrange("p b (h d) -> p b h d", d=HD),
                                  bc(rdn[:, pair, :], 3, HD), ALU.mult).then_inc(freed[m], 1)

            dve.wait_ge(x_in, 16)
            moments_of(tile_of(0), st, mv, stats, moments, 0)
            normal(lambda b: xn[:, b, :], tile_of(0), mv, rs, rs_ready, xn_ready, 0)
            iterations(dve, body)
            make_tables(dve)
            ffn_vector(dve)
            combine(dve)


def kernel(**inputs):
    import numpy as np
    import concourse.bacc as bacc
    from concourse.bass_utils import run_bass_kernel_spmd

    a = {k: np.asarray(v) for k, v in inputs.items()}
    A, C, M = "L0_attn_", "L0_xattn_", "L0_ffn_"
    vectors = [a[A + n] for n in ("bq", "bk", "bv", "bd", "gamma", "beta")] + \
              [a[C + n] for n in ("bq", "bk", "bv", "bo")]
    arrays = {
        "x": a["x"],
        "ctxT": a["ctx_768"].reshape(NB * NK, CK).T,
        "wA": np.stack([a[A + "Wq"].T, a[A + "Wk"].T, a[A + "Wv"].T, a[A + "Wd"].T, a[C + "Wq"], a[C + "Wo"]], axis=1),
        "wC": np.stack([a[C + "Wk"], a[C + "Wv"]], axis=1),
        "wr": a[M + "router_w"].T,
        "w1": a[M + "w1"].transpose(1, 0, 2).reshape(P, E * F),
        "w2": a[M + "w2"].reshape(E, FC, P, P).transpose(2, 0, 1, 3).reshape(P, E * FC * P),
        "vrow": np.stack(vectors),
        "vcol": np.stack(vectors, axis=1),
    }
    arrays = {k: np.ascontiguousarray(v) for k, v in arrays.items()}
    nc = bacc.Bacc("TRN2", target_bir_lowering=False, num_devices=1)
    args = [nc.dram_tensor(k, v.shape, F32, kind="ExternalInput").ap() for k, v in arrays.items()]
    out = nc.dram_tensor("out", [NB, P, P], F32, kind="ExternalOutput").ap()
    expert_rows = nc.dram_tensor("expert_rows", [EMPTY + P, ROW], F32, kind="Internal").ap()
    y_rows = [nc.dram_tensor(f"y_rows{k}", [NB * P, P], F32, kind="Internal").ap() for k in range(2)]
    decoder_layer(nc, *args, out, expert_rows, y_rows)
    r = run_bass_kernel_spmd(nc, [arrays], core_ids=[0])
    return r.results[0]["out"]
```

```python
from contextlib import ExitStack

import concourse.bass as bass
from concourse import mybir

F32 = mybir.dt.float32
I32 = mybir.dt.int32
U32 = mybir.dt.uint32
ALU = mybir.AluOpType
ACT = mybir.ActivationFunctionType
AX = mybir.AxisListType
ds = bass.ds

P = 128
NB = 64
T = 4
NG = NB // T
NH, HD = 16, 8
HG = 4
NK, CK = 77, 96
E, F = 8, 512
FC = F // P
CAP = max(1, int(1.25 * NB * P / E * 2))
B = 2
BLK = B * P
REG = CAP + BLK
NREG = 2 * E
EMPTY = NREG * REG
NBLK = NB // B + E
ROW = P + 3
BIG = float(1 << 20)
CLAMP = 10000.0
SCALE = HD ** -0.5
EPS = 1e-5
EPS_ATTN, EPS_ATTN_LN = 1e-6, 1e-12
V_BQ, V_BK, V_BV, V_BD, V_GAMMA, V_BETA, V_BQ2, V_BK2, V_BV2, V_BO2 = range(10)
NV = 10
W_Q, W_K, W_V, W_D, W_Q2, W_O2 = range(6)

USES = [("xnT", "L"), ("aoT", "R"), ("xn2T", "M"), ("q", "L"), ("x2", "R"), ("kp0", "L"), ("kp1", "L"),
        ("pv0", "X"), ("kv0", "L"), ("kv1", "L"), ("pvT0", "X"), ("nd0", "L"), ("nd1", "L"),
        ("cT", "L"), ("pv1", "X"), ("hs", "L"), ("pvT1", "X"), ("xn3T", "R"), ("pv2", "X"),
        ("k2T", "M"), ("pvT2", "X"), ("logits", "R"), ("q2T", "M"), ("pv3", "X"), ("v2", "M"), ("pvT3", "X")]
LAG = {"N": -1, "L": 0, "M": 1, "X": 2, "R": 3, "W": 4, "V": 5}


def runs(stage, i):
    return not isinstance(i, int) or 0 <= i - LAG[stage] < NG


def use_of(name, i):
    at = [n for n, _ in USES].index(name)
    bank = at % 2
    mine = [s for n, s in USES[bank::2]]
    if isinstance(i, int):
        before = sum(min(max(i - LAG[s], 0), NG) for s in mine)
    else:
        before = i * len(mine) - sum(LAG[s] for s in mine)
    return bank, before + sum(1 for n, s in USES[bank:at:2] if runs(s, i))


def decoder_layer(nc, x, ctxT, wA, wC, wr, w1, w2, vrow, vcol, out, expert_rows, y_rows):
    with ExitStack() as ctx:
        def sb(name, shape, dt=F32):
            return ctx.enter_context(nc.sbuf_tensor(name, shape, dt))

        def sem(name):
            return ctx.enter_context(nc.semaphore(name))

        wA_s = sb("wA_s", [P, 6, P])
        wC_s = sb("wC_s", [CK, 2, P])
        wr_s = sb("wr_s", [P, E])
        w1_s = sb("w1_s", [P, E * F])
        w2_s = sb("w2_s", [P, E * FC * P])
        vb = sb("vb", [P, NV, P])
        vc = sb("vc", [P, NV])
        ident = sb("ident", [P, P])
        ones = sb("ones", [P, P])
        before = sb("before", [P, P])
        bmask = sb("bmask", [P, P])
        hmask = sb("hmask", [P, HG])
        hmask16 = sb("hmask16", [P, NH])
        expo = sb("expo", [P, T])
        bq2s = sb("bq2s", [P, 1])
        bv2c = sb("bv2c", [P, P])
        bo_all = sb("bo_all", [P, P])
        tok_i = sb("tok_i", [P, NB], I32)
        e_i = sb("e_i", [P, 3, 2, E], I32)
        e_f = sb("e_f", [P, 3, 2, E])
        j_i = sb("j_i", [P, 1], I32)
        j_f = sb("j_f", [P, 1])
        zeros = sb("zeros", [P, 1024])
        tail = sb("tail", [P, B, ROW])
        xs = sb("xs", [P, NB, P])
        st = sb("st", [P, T, 6])
        mv = sb("mv", [P, T, 2])
        rs = sb("rs", [P, T])
        xn = sb("xn", [P, T, P])
        xb_xbeta = sb("xb_xbeta", [P, 2 * T, P])
        xb, xbeta = xb_xbeta[:, 0:T], xb_xbeta[:, T:2 * T]
        xnT = sb("xnT", [P, T * P])
        eq = sb("eq", [P, T * P])
        rq = sb("rq", [P, T * P])
        qT = sb("qT", [P, T * P])
        kvb = sb("kvb", [P, T, 2 * P + 1])
        ek = sb("ek", [P, T, P])
        rk = sb("rk", [P, T, P])
        kk = sb("kk", [P, T, P])
        kvm = sb("kvm", [P, T, P + NH])
        rdn = sb("rdn", [P, T, NH])
        cx = sb("cx", [P, T, P])
        cT = sb("cT", [P, T * P])
        hs_hn = sb("hs_hn", [P, 2 * T, P])
        hs, hn = hs_hn[:, 0:T], hs_hn[:, T:2 * T]
        hst = sb("hst", [P, T, 6])
        hmv = sb("hmv", [P, T, 2])
        hrs = sb("hrs", [P, T])
        x1_hg = sb("x1_hg", [P, 2 * T, P])
        x1, hg = x1_hg[:, 0:T], x1_hg[:, T:2 * T]
        st2 = sb("st2", [P, T, 6])
        mv2 = sb("mv2", [P, T, 2])
        rs2 = sb("rs2", [P, T])
        xn2 = sb("xn2", [P, T, P])
        xn2T = sb("xn2T", [P, T * P])
        cg = sb("cg", [CK, T * NK])
        q2 = sb("q2", [P, T * P])
        k2 = sb("k2", [P, T * NK])
        v2 = sb("v2", [NK, T, NH, 64])
        pvs = sb("pvs", [P, 2, 2 * P])
        kblk = sb("kblk", [P, T, HG, NK])
        mraw = sb("mraw", [P, 2, NH // 2])
        mclip = sb("mclip", [P, 2, NH // 2])
        z = sb("z", [P, 2, NH * NK])
        pT = sb("pT", [NK, 2, NH * P])
        rd = sb("rd", [P, HG, HG])
        ao = sb("ao", [P, T, P])
        aoT = sb("aoT", [P, T * P])
        st3 = sb("st3", [P, T, 6])
        mv3 = sb("mv3", [P, T, 2])
        rs3 = sb("rs3", [P, T])
        xn3 = sb("xn3", [P, T, P])
        row = sb("row", [P, T, ROW])
        xn3T = sb("xn3T", [P, T * P])
        lg = sb("lg", [P, T, E])
        top = sb("top", [P, 2, T])
        hot = sb("hot", [P, T, 2, E])
        tie = sb("tie", [P, T, E])
        tiem = sb("tiem", [P, T])
        low = sb("low", [P, T, E])
        gap = sb("gap", [P, T])
        eg = sb("eg", [P, T])
        eg1 = sb("eg1", [P, T])
        carry = sb("carry", [P, T + 1, 2 * E])
        rank = sb("rank", [P, 2, T, 2 * E])
        pos = sb("pos", [P, T, 2 * E])
        pick = sb("pick", [P, 2, T * 2, E])
        sel = sb("sel", [P, 2, T * 2])
        over = sb("over", [P, T * 2])
        slot_f = sb("slot_f", [P, T * 2])
        slot = sb("slot", [P, T * 2], U32)

        cnt = sb("cnt", [P, 2 * E])
        cnt_i = sb("cnt_i", [P, 2 * E], I32)
        nt = sb("nt", [P, 2 * E])
        tail_f = sb("tail_f", [P, 2 * E])
        tail_i = sb("tail_i", [P, 2 * E], I32)
        ends = sb("ends", [P, 2, E])
        past = sb("past", [P, 2, 2, E])
        psum_ = sb("psum_", [P, 2, 2])
        rowf = sb("rowf", [P, 2])
        none = sb("none", [P, 2])
        tab = sb("tab", [P, 8])
        tab_i = sb("tab_i", [4, P], I32)
        xt = sb("xt", [P, 4, B, ROW])
        meta = sb("meta", [P, 4, B, 3])
        xtT = sb("xtT", [P, 2, BLK])
        hT = z[:, :, 0:FC * BLK]
        w1_e = hs_hn[:].rearrange("p (s a) h -> p s (a h)", s=2)
        w2_e = xb_xbeta[:].rearrange("p (s a) h -> p s (a h)", s=2)
        ys = x1_hg[:].rearrange("p (s a) h -> p s a h", a=B)
        yT = eq[:].rearrange("p (s c) -> p s c", s=2)
        yt = sb("yt", [P, 4, B], U32)
        yb = w1_s[:, 0:4 * T * P].rearrange("p (s k b h) -> p s k b h", s=2, k=2, b=T)
        ob = w1_s[:, 4 * T * P:6 * T * P].rearrange("p (s b h) -> p s b h", s=2, b=T)

        bank = [ctx.enter_context(nc.psum_tensor(f"bank{m}", [P, 512], F32)) for m in range(2)]
        S = ctx.enter_context(nc.psum_tensor("S", [P, HG, 512], F32))
        PT = [ctx.enter_context(nc.psum_tensor(f"PT{m}", [P, 512], F32)) for m in range(2)]

        ranks = S[:, HG - 1, HG * NK:HG * NK + 2 * T * 2 * E]

        weights_in, ffn_in, x_in, ctx_in = sem("weights_in"), sem("ffn_in"), sem("x_in"), sem("ctx_in")
        consts, zeroed, hmask_ready = sem("consts"), sem("zeroed"), sem("hmask_ready")
        vcopied, bo_filled, bo_ready = sem("vcopied"), sem("bo_filled"), sem("bo_ready")
        cleared = sem("cleared")
        filled = [sem(f"filled{m}") for m in range(2)]
        freed = [sem(f"freed{m}") for m in range(2)]
        stats, moments, rs_part, rs_ready = sem("stats"), sem("moments"), sem("rs_part"), sem("rs_ready")
        xn_ready, xb_ready, xbeta_ready = sem("xn_ready"), sem("xb_ready"), sem("xbeta_ready")
        eq_ready, qT_ready = sem("eq_ready"), sem("qT_ready")
        ek_ready, rk_ready, kk_ready = sem("ek_ready"), sem("rk_ready"), sem("kk_ready")
        kvm_ready, rdn_ready = sem("kvm_ready"), sem("rdn_ready")
        hstats, hmoments, hrs_part, hrs_ready = sem("hstats"), sem("hmoments"), sem("hrs_part"), sem("hrs_ready")
        hn_ready, hg_part, hg_ready, x1_ready, x1_kept = (sem("hn_ready"), sem("hg_part"), sem("hg_ready"),
                                                          sem("x1_ready"), sem("x1_kept"))
        stats2, moments2, rs2_part, rs2_ready = sem("stats2"), sem("moments2"), sem("rs2_part"), sem("rs2_ready")
        xn2_ready = sem("xn2_ready")
        kblk_ready, scored = sem("kblk_ready"), sem("scored")
        m_raw, m_clipped, z_ready, z_clipped, p_ready = (sem("m_raw"), sem("m_clipped"), sem("z_ready"),
                                                         sem("z_clipped"), sem("p_ready"))
        pt_filled, pt_freed, rd_ready = sem("pt_filled"), sem("pt_freed"), sem("rd_ready")
        stats3, moments3, rs3_part, rs3_ready = sem("stats3"), sem("moments3"), sem("rs3_part"), sem("rs3_ready")
        xn3_ready, chosen, placed, eg_ready, sent = (sem("xn3_ready"), sem("chosen"), sem("placed"),
                                                     sem("eg_ready"), sem("sent"))

        ranked, ranks_read, row_filled = sem("ranked"), sem("ranks_read"), sem("row_filled")
        table_steps, tails_known, tails_in = sem("table_steps"), sem("tails_known"), sem("tails_in")
        tab_ready, tabT_filled, tables_ready = sem("tab_ready"), sem("tabT_filled"), sem("tables_ready")
        w1_ready, w2_ready = ([sem(f"{name}{m}") for m in range(4)] for name in ("w1_ready", "w2_ready"))
        xt_in, xt_used, meta_ready, xtT_ready, h_filled, hT_ready, yT_filled, yT_ready, y_filled, ys_ready, \
            y_sent = ([sem(f"{name}{m}") for m in range(4)] for name in (
                "xt_in", "xt_used", "meta_ready", "xtT_ready", "h_filled", "hT_ready", "yT_filled", "yT_ready",
                "y_filled", "ys_ready", "y_sent"))
        y_in, y_added, out_ready, out_stored = ([sem(f"{name}{m}") for m in range(2)] for name in (
            "y_in", "y_added", "out_ready", "out_stored"))
        CLEARS = 2 * NB * P // (P * 8) + 1

        block = ctx.enter_context(nc.Block())
        CHOOSE, PLACE = 12, 16

        def bc(ap, axis, n):
            ap = ap.unsqueeze(axis)
            shape = list(ap.shape)
            shape[axis] = n
            return ap.broadcast_to(shape)

        def group(t, g):
            return t[:, ds(g * T, T), :] if not isinstance(g, int) else t[:, g * T:(g + 1) * T, :]

        def wait_apart(eng, sem, count):
            if not isinstance(count, int):
                count = eng.to_reg(count)
            eng.wait_ge(consts, 5)
            eng.wait_ge(sem, count)

        def iterations(eng, body):
            for i in range(LAG["V"] + 1):
                body(i)
            with eng.Fori(LAG["V"] + 1, NG - 1) as i:
                body(i)
            for i in range(NG - 1, NG + LAG["V"]):
                body(i)

        def write_tails(sp):
            sp.wait_ge(tails_known, 1)
            sp.wait_ge(sent, NG * T * 2 * 16)
            for r in range(NREG):
                at = sp.value_load(tail_i[0:1, r:r + 1], min_val=0, max_val=EMPTY - BLK)
                sp.dma_start(expert_rows[ds(at, BLK), :].rearrange("(p a) r -> p a r", a=B), tail[:]).then_inc(tails_in, 16)

        def ffn(eng, body, last):
            for k in range(2):
                for step in range(8):
                    body(k, step // 4, step % 4)
                with eng.Fori(2, NBLK // 4) as r:
                    for u in range(4):
                        body(k, r, u)
                for u in range(last):
                    body(k, NBLK // 4, u)

        def block_at(k, r, u, lag):
            if isinstance(r, int) and not 0 <= 4 * r + u - lag < NBLK:
                return None
            return (u - lag) % 4, k * (NBLK // 4) + r + (u - lag) // 4, r * 4 + (u - lag)

        def block_before(slot, used, back):
            at, n = (slot - back) % 4, used + (slot - back) // 4
            return None if isinstance(n, int) and n < 0 else (at, n)

        def entry(row, j):
            return tab_i[row:row + 1, j:j + 1] if isinstance(j, int) else tab_i[row:row + 1, ds(j, 1)]

        def ffn_load(sp):
            sp.wait_ge(tables_ready, 1)
            sp.wait_ge(tails_in, NREG * 16)
            sp.wait_ge(cleared, CLEARS * 16)

            def body(k, r, u):
                t = block_at(k, r, u, 0)
                if t is None:
                    return
                slot, used, j = t
                if not (isinstance(used, int) and used == 0):
                    sp.wait_ge(xt_used[slot], used)
                    sp.wait_ge(meta_ready[slot], used)
                at = sp.value_load(entry(k, j), min_val=0, max_val=EMPTY)
                sp.dma_start(xt[:, slot], expert_rows[ds(at, BLK), :].rearrange("(p a) r -> p a r", a=B))\
                  .then_inc(xt_in[slot], 16)

            ffn(sp, body, 0)

        def ffn_tensor(pe):
            pe.wait_ge(ffn_in, 32)
            pe.wait_ge(tables_ready, 1)
            pe.wait_ge(z_ready, NB * 4)
            pe.wait_ge(pt_freed, NB * 4)

            def body(k, r, u):
                t = block_at(k, r, u, 0)
                if t is not None:
                    slot, used, _ = t
                    pe.wait_ge(xt_in[slot], (used + 1) * 16)
                    p = block_before(slot, used, 2)
                    if p is not None:
                        pe.wait_ge(xtT_ready[p[0]], p[1] + 1)
                    for a in range(B):
                        ins = pe.transpose(bank[slot % 2][:, a * P:(a + 1) * P], xt[:, slot, a, 0:P], ident[:])
                    ins.then_inc(xt_used[slot], 1)
                t = block_at(k, r, u, 1)
                if t is not None:
                    slot, used, _ = t
                    pe.wait_ge(w1_ready[slot], used + 1)
                    pe.wait_ge(xtT_ready[slot], used + 1)
                    p = block_before(slot, used, 2)
                    if p is not None:
                        pe.wait_ge(hT_ready[p[0]], p[1] + 1)
                    for c in range(FC):
                        ins = pe.matmul(S[:, 2 * (slot % 2) + c // 2, (c % 2) * BLK:(c % 2 + 1) * BLK],
                                        w1_e[:, slot % 2, c * P:(c + 1) * P], xtT[:, slot % 2, :], start=True, stop=True)
                    ins.then_inc(h_filled[slot], 1)
                t = block_at(k, r, u, 2)
                if t is not None:
                    slot, used, _ = t
                    pe.wait_ge(w2_ready[slot], used + 1)
                    pe.wait_ge(hT_ready[slot], used + 1)
                    p = block_before(slot, used, 2)
                    if p is not None:
                        pe.wait_ge(ys_ready[p[0]], p[1] + 1)
                    for c in range(FC):
                        ins = pe.matmul(PT[slot % 2][:, 0:BLK], w2_e[:, slot % 2, c * P:(c + 1) * P],
                                        hT[:, slot % 2, c * BLK:(c + 1) * BLK], start=(c == 0), stop=(c == FC - 1))
                    ins.then_inc(yT_filled[slot], 1)
                t = block_at(k, r, u, 3)
                if t is not None:
                    slot, used, _ = t
                    pe.wait_ge(yT_ready[slot], used + 1)
                    for a in range(B):
                        ins = pe.transpose(PT[slot % 2][:, BLK + a * P:BLK + (a + 1) * P],
                                           yT[:, slot % 2, a * P:(a + 1) * P], ident[:])
                    ins.then_inc(y_filled[slot], 1)

            ffn(pe, body, 3)

        def ffn_vector(dve):
            def body(k, r, u):
                t = block_at(k, r, u, 0)
                if t is not None:
                    slot, used, j = t
                    e = dve.value_load(entry(2 + k, j), min_val=0, max_val=E - 1)
                    p = block_before(slot, used, 2)
                    if p is not None:
                        wait_apart(dve, h_filled[p[0]], p[1] + 1)
                    dve.tensor_copy(w1_e[:, slot % 2, :], w1_s[:, ds(e * F, F)]).then_inc(w1_ready[slot], 1)
                    dve.wait_ge(xt_in[slot], (used + 1) * 16)
                    if not (isinstance(used, int) and used == 0):
                        dve.wait_ge(ys_ready[slot], used)
                    dve.tensor_copy(meta[:, slot], xt[:, slot, :, P:ROW]).then_inc(meta_ready[slot], 1)
                    dve.wait_ge(xt_used[slot], used + 1)
                    dve.tensor_copy(xtT[:, slot % 2, :], bank[slot % 2][:, 0:BLK]).then_inc(xtT_ready[slot], 1)
                t = block_at(k, r, u, 2)
                if t is not None:
                    slot, used, _ = t
                    dve.wait_ge(yT_filled[slot], used + 1)
                    dve.tensor_copy(yT[:, slot % 2, :], PT[slot % 2][:, 0:BLK]).then_inc(yT_ready[slot], 1)
                t = block_at(k, r, u, 3)
                if t is not None:
                    slot, used, _ = t
                    if not (isinstance(used, int) and used == 0):
                        dve.wait_ge(y_sent[slot], used * B * 16)
                    dve.tensor_copy(yt[:, slot, :], meta[:, slot, :, 0].bitcast(I32))
                    dve.wait_ge(y_filled[slot], used + 1)
                    for a in range(B):
                        ins = dve.tensor_scalar(ys[:, slot, a, :], PT[slot % 2][:, BLK + a * P:BLK + (a + 1) * P],
                                                meta[:, slot, a, 1 + k:2 + k], None, ALU.mult)
                    ins.then_inc(ys_ready[slot], 1)

            dve.wait_ge(ffn_in, 32)
            dve.wait_ge(tables_ready, 1)
            ffn(dve, body, 3)

        def ffn_scalar(act):
            def body(k, r, u):
                t = block_at(k, r, u, 1)
                if t is not None:
                    slot, used, j = t
                    e = act.value_load(entry(2 + k, j), min_val=0, max_val=E - 1)
                    p = block_before(slot, used, 2)
                    if p is not None:
                        wait_apart(act, yT_filled[p[0]], p[1] + 1)
                    act.copy(w2_e[:, slot % 2, :], w2_s[:, ds(e * (FC * P), FC * P)]).then_inc(w2_ready[slot], 1)
                    act.wait_ge(h_filled[slot], used + 1)
                    q = 2 * (slot % 2)
                    act.activation(hT[:, slot % 2, :], S[:, q:q + 2, :].rearrange("p q c -> p (q c)"), ACT.Gelu)\
                       .then_inc(hT_ready[slot], 1)

            act.wait_ge(ffn_in, 32)
            act.wait_ge(tables_ready, 1)
            ffn(act, body, 1)

        def ffn_scatter(pool):
            def body(k, r, u):
                t = block_at(k, r, u, 3)
                if t is not None:
                    slot, used, _ = t
                    wait_apart(pool, ys_ready[slot], used + 1)
                    for a in range(B):
                        pool.indirect_dma_start(
                            out=y_rows[k], out_offset=bass.IndirectOffsetOnAxis(ap=yt[:, slot, a:a + 1], axis=0),
                            in_=ys[:, slot, a, :], in_offset=None,
                            bounds_check=NB * P - 1, oob_is_err=False).then_inc(y_sent[slot], 16)

            ffn(pool, body, 3)

        def make_tables(dve):
            done = [0]

            def step(ins):
                ins.then_inc(table_steps, 1)
                done[0] += 1
                dve.wait_ge(table_steps, done[0])

            step(dve.tensor_scalar(cnt[:], carry[:, 0, :], float(CAP), None, ALU.min))
            step(dve.tensor_tensor(tail_f[:], cnt[:], e_f[:, 0].rearrange("p k e -> p (k e)"), ALU.add))
            dve.tensor_scalar(tail_i[:], tail_f[:], 1.0, None, ALU.add).then_inc(tails_known, 1)
            step(dve.tensor_scalar(cnt_i[:], cnt[:], float(BLK - 1), None, ALU.add))
            step(dve.tensor_scalar(cnt_i[:], cnt_i[:], BLK.bit_length() - 1, None, ALU.arith_shift_right))
            step(dve.tensor_copy(nt[:], cnt_i[:]))
            for k in range(2):
                step(dve.tensor_tensor_scan(ends[:, k, :], ones[:, 0:E], nt[:, k * E:(k + 1) * E], 0.0,
                                            ALU.mult, ALU.add))
            step(dve.tensor_scalar(past[:, 0], ends[:], j_f[:], None, ALU.is_le))
            step(dve.tensor_tensor(past[:, 1], past[:, 0], nt[:].rearrange("p (k e) -> p k e", k=2), ALU.mult))
            step(dve.tensor_reduce(psum_[:], past[:], AX.X, ALU.add))
            step(dve.tensor_scalar(rowf[:], psum_[:, 1], j_f[:], -float(BLK), ALU.subtract, ALU.mult))
            step(dve.scalar_tensor_tensor(out=rowf[:], in0=psum_[:, 0], scalar=float(REG), in1=rowf[:],
                                          op0=ALU.mult, op1=ALU.add))
            step(dve.tensor_scalar(rowf[:, 1:2], rowf[:, 1:2], float(E * REG), None, ALU.add))
            step(dve.tensor_scalar(none[:], psum_[:, 0], float(E), float(EMPTY), ALU.is_ge, ALU.mult))
            step(dve.tensor_tensor(tab[:, 0:2], rowf[:], none[:], ALU.max))
            step(dve.tensor_scalar(tab[:, 0:2], tab[:, 0:2], float(EMPTY), None, ALU.min))
            step(dve.tensor_scalar(tab[:, 2:4], psum_[:, 0], float(E - 1), None, ALU.min))
            dve.tensor_copy(tab[:, 4:8], tab[:, 0:4]).then_inc(tab_ready, 1)
            dve.wait_ge(tabT_filled, 1)
            dve.tensor_copy(tab_i[:], bank[0][0:4, 0:P]).then_inc(tables_ready, 1)

        def load_y(sp):
            for slot in range(4):
                sp.wait_ge(y_sent[slot], 2 * (NBLK // 4) * B * 16)

            def body(r, u):
                if not (isinstance(r, int) and r == 0):
                    sp.wait_ge(y_added[u], r)
                g = r * 2 + u
                for k in range(2):
                    src = (y_rows[k][g * T * P:(g + 1) * T * P] if isinstance(g, int)
                           else y_rows[k][ds(g * (T * P), T * P)])
                    sp.dma_start(yb[:, u, k], src.rearrange("(b s) h -> s b h", s=P)).then_inc(y_in[u], 16)

            halves(sp, body)

        def halves(eng, body):
            for u in range(2):
                body(0, u)
            with eng.Fori(1, NG // 2) as r:
                for u in range(2):
                    body(r, u)

        def combine(dve):
            def body(r, u):
                dve.wait_ge(y_in[u], (r + 1) * 32)
                if not (isinstance(r, int) and r == 0):
                    dve.wait_ge(out_stored[u], r * 16)
                dve.tensor_tensor(ob[:, u], yb[:, u, 0], yb[:, u, 1], ALU.add).then_inc(y_added[u], 1)
                dve.wait_ge(y_added[u], r + 1)
                dve.tensor_tensor(ob[:, u], ob[:, u], group(xs, r * 2 + u), ALU.add).then_inc(out_ready[u], 1)

            halves(dve, body)

        def store_out(act):
            def body(r, u):
                g = r * 2 + u
                act.wait_ge(out_ready[u], r + 1)
                dst = out[g * T:(g + 1) * T] if isinstance(g, int) else out[ds(g * T, T)]
                act.dma_start(dst.rearrange("b s h -> s b h"), ob[:, u]).then_inc(out_stored[u], 16)

            halves(act, body)
            for u in range(2):
                act.wait_ge(out_stored[u], NG // 2 * 16)

        @block.tensor
        def _(pe):
            pe.wait_ge(vcopied, 2)
            pe.matmul(PT[0][:, 0:P], bv2c[:], wA_s[:, W_O2], start=True, stop=True).then_inc(bo_filled, 1)
            pe.wait_ge(consts, 5)
            pe.wait_ge(bo_ready, 1)

            def begin(name, i):
                m, u = use_of(name, i)
                if not (isinstance(u, int) and u == 0):
                    pe.wait_ge(freed[m], u)
                return bank[m], filled[m]

            def scores(g, b, quadrants=range(HG)):
                n = g * T + b
                pe.wait_ge(kblk_ready, n + 1)
                for q in quadrants:
                    if not (isinstance(n, int) and n == 0):
                        pe.wait_ge(z_ready, n * 4 - 3 + q)
                    ins = pe.matmul(S[:, q, 0:HG * NK], q2[32 * q:32 * q + 32, b * P:(b + 1) * P],
                                    kblk[32 * q:32 * q + 32, b].rearrange("p h k -> p (h k)"),
                                    start=True, stop=True)
                    if q % 2:
                        ins.then_inc(scored, 1)

            def transposes(g, b, c):
                n = g * T + b
                if not (isinstance(n, int) and n == 0 and c < 2):
                    pe.wait_ge(pt_freed, n * 4 + c - 1)
                for h in range(HG):
                    at = (c * HG + h) * NK
                    ins = pe.transpose(PT[c % 2][0:NK, h * P:(h + 1) * P], z[:, b % 2, at:at + NK], ident[:])
                ins.then_inc(pt_filled, 1)

            def weights_T(g, b):
                pe.wait_ge(p_ready, g * T + b + 1)
                transposes(g, b, 0)
                transposes(g, b, 1)

            def by_values(g, b, i):
                n = g * T + b
                pv, done = begin(f"pv{b}", i)
                for q in range(HG):
                    pe.wait_ge(pt_freed, n * 4 + q + 1)
                    at = slice(64 * (q % 2), 64 * (q % 2) + 64)
                    for j in range(HG):
                        h = q * HG + j
                        ins = pe.matmul(pv[at, (q // 2) * P:(q // 2 + 1) * P], v2[:, b, h, :],
                                        pT[:, b % 2, h * P:(h + 1) * P], start=(j == 0), stop=(j == HG - 1))
                    if q < 2:
                        transposes(g, b, q + 2)
                ins.then_inc(done, 1)

            def output_T(g, b, i):
                m, u = use_of(f"pv{b}", i)
                pe.wait_ge(freed[m], u + 1)
                dst, done = begin(f"pvT{b}", i)
                for half in range(2):
                    ins = pe.transpose(dst[:, half * P:(half + 1) * P], pvs[:, b % 2, half * P:(half + 1) * P],
                                       ident[:])
                ins.then_inc(done, 1)

            def each_tile(name, i, lhsT, rhs, width=P, tiles=range(T)):
                dst, done = begin(name, i)
                for n, b in enumerate(tiles):
                    ins = pe.matmul(dst[:, n * width:(n + 1) * width], lhsT(b), rhs(b), start=True, stop=True)
                ins.then_inc(done, 1)

            def transpose_tiles(name, i, src):
                dst, done = begin(name, i)
                for b in range(T):
                    ins = pe.transpose(dst[:, b * P:(b + 1) * P], src(b), ident[:])
                ins.then_inc(done, 1)

            def part(ap):
                return lambda b: ap[:, b * P:(b + 1) * P]

            def body(i):
                L, M, X, R = (runs(stage, i) for stage in "LMXR")
                gm, gx, gr = (i - LAG[stage] for stage in "MXR")
                if X:
                    scores(gx, 0, range(2))
                if L:
                    pe.wait_ge(xn_ready, i * T + T)
                    transpose_tiles("xnT", i, lambda b: xn[:, b, :])
                if R:
                    transpose_tiles("aoT", i, lambda b: ao[:, b, :])
                if X:
                    if not (isinstance(gr, int) and gr < 1):
                        pe.wait_ge(ranks_read, gr)
                    scores(gx, 0, range(2, 4))
                if M:
                    pe.wait_ge(xn2_ready, gm * T + T)
                    transpose_tiles("xn2T", i, lambda b: xn2[:, b, :])
                if L:
                    m, u = use_of("xnT", i)
                    pe.wait_ge(freed[m], u + 1)
                    dst, done = begin("q", i)
                    pe.matmul(dst[:], wA_s[:, W_Q], xnT[:], start=True, stop=True).then_inc(done, 1)
                if R:
                    m, u = use_of("aoT", i)
                    pe.wait_ge(freed[m], u + 1)
                    each_tile("x2", i, part(aoT), lambda b: wA_s[:, W_O2])
                if L:
                    keys_and_values(i, 0)
                    keys_and_values(i, 1)
                if X:
                    weights_T(gx, 0)
                    scores(gx, 1)
                    by_values(gx, 0, i)
                if L:
                    m, u = use_of("kp1", i)
                    pe.wait_ge(freed[m], u + 1)
                    pe.wait_ge(kk_ready, i + 1)
                    for half in range(2):
                        each_tile(f"kv{half}", i, lambda b: kk[:, b, :], lambda b: kvb[:, b, P:2 * P + 1],
                                  width=P + 1, tiles=range(2 * half, 2 * half + 2))
                if X:
                    output_T(gx, 0, i)
                if L:
                    pe.wait_ge(qT_ready, i + 1)
                    numerators(i, 0)
                    numerators(i, 1)
                if X:
                    scores(gx, 2)
                    weights_T(gx, 1)
                if L:
                    m, u = use_of("nd1", i)
                    pe.wait_ge(freed[m], u + 1)
                    transpose_tiles("cT", i, lambda b: cx[:, b, :])
                if X:
                    by_values(gx, 1, i)
                if L:
                    m, u = use_of("cT", i)
                    pe.wait_ge(freed[m], u + 1)
                    each_tile("hs", i, part(cT), lambda b: wA_s[:, W_D])
                if X:
                    output_T(gx, 1, i)
                    scores(gx, 3)
                    weights_T(gx, 2)
                if R:
                    pe.wait_ge(xn3_ready, gr * T + T)
                    transpose_tiles("xn3T", i, lambda b: xn3[:, b, :])
                if X:
                    by_values(gx, 2, i)
                if M:
                    pe.wait_ge(ctx_in, gm * 16 + 16)
                    dst, done = begin("k2T", i)
                    pe.matmul(dst[:, 0:T * NK], wC_s[:, 0], cg[:], start=True, stop=True).then_inc(done, 1)
                if X:
                    output_T(gx, 2, i)
                if R:
                    m, u = use_of("xn3T", i)
                    pe.wait_ge(freed[m], u + 1)
                    each_tile("logits", i, part(xn3T), lambda b: wr_s[:], width=E)
                if X:
                    weights_T(gx, 3)
                if M:
                    m, u = use_of("xn2T", i)
                    pe.wait_ge(freed[m], u + 1)
                    dst, done = begin("q2T", i)
                    pe.matmul(dst[:], wA_s[:, W_Q2], xn2T[:], start=True, stop=True).then_inc(done, 1)
                if X:
                    by_values(gx, 3, i)
                if M:
                    dst, done = begin("v2", i)
                    for b in range(T):
                        ins = pe.matmul(dst[0:NK, b * P:(b + 1) * P], cg[:, b * NK:(b + 1) * NK], wC_s[:, 1],
                                        start=True, stop=True)
                    ins.then_inc(done, 1)
                if R:
                    pe.wait_ge(chosen, (gr + 1) * CHOOSE)
                    pe.wait_ge(z_ready, (gx * T + T) * 4 if X else NB * 4)
                    if not (isinstance(gr, int) and gr == 0):
                        pe.wait_ge(ranks_read, gr)
                    flat = hot[:].rearrange("p b k e -> p (b k e)")
                    pe.matmul(ranks[:, 0:T * 2 * E], before[:], flat, start=True, stop=True)
                    pe.matmul(ranks[:, T * 2 * E:], ones[:], flat, start=True, stop=True).then_inc(ranked, 1)
                if X:
                    output_T(gx, 3, i)

            def keys_and_values(i, half):
                each_tile(f"kp{half}", i, part(xnT), lambda b: wA_s[:, W_K:W_V + 1].rearrange("p a h -> p (a h)"),
                          width=2 * P, tiles=range(2 * half, 2 * half + 2))

            def numerators(i, half):
                m, u = use_of(f"kv{half}", i)
                pe.wait_ge(freed[m], u + 1)
                each_tile(f"nd{half}", i, part(qT), lambda b: kvm[:, b, :], width=P + NH,
                          tiles=range(2 * half, 2 * half + 2))

            iterations(pe, body)
            pe.wait_ge(tab_ready, 1)
            pe.transpose(bank[0][0:4, 0:P], tab[:, 4:8], ident[:]).then_inc(tabT_filled, 1)
            ffn_tensor(pe)

        @block.sync
        def _(sp):
            sp.dma_start(vb[:], vrow.unsqueeze(0).broadcast_to([P, NV, P])).then_inc(weights_in, 16)
            sp.dma_start(vc[:], vcol).then_inc(weights_in, 16)
            sp.dma_start(wA_s[:], wA).then_inc(weights_in, 16)
            sp.dma_start(wC_s[:], wC).then_inc(weights_in, 16)
            sp.dma_start(wr_s[:], wr).then_inc(weights_in, 16)

            def load_x(g):
                if not (isinstance(g, int) and g == 0):
                    sp.wait_ge(x_in, g * 16)
                src = x[ds(g * T, T)] if not isinstance(g, int) else x[g * T:(g + 1) * T]
                sp.dma_start(group(xs, g), src.rearrange("b s h -> s b h")).then_inc(x_in, 16)

            def load_ctx(g):
                c = T * NK
                if not (isinstance(g, int) and g == 0):
                    b, n = use_of("v2", g - 1 + LAG["M"])
                    sp.wait_ge(filled[b], n + 1)
                src = ctxT[:, ds(g * c, c)] if not isinstance(g, int) else ctxT[:, g * c:(g + 1) * c]
                sp.dma_start(cg[:], src).then_inc(ctx_in, 16)

            load_x(0)
            load_ctx(0)
            load_x(1)
            sp.dma_start(w1_s[:], w1).then_inc(ffn_in, 16)
            sp.dma_start(w2_s[:], w2).then_inc(ffn_in, 16)
            load_x(2)
            load_ctx(1)
            load_x(3)
            load_ctx(2)
            with sp.Fori(3, NG - 1) as g:
                load_x(g + 1)
                load_ctx(g)
            load_ctx(NG - 1)
            write_tails(sp)
            ffn_load(sp)
            load_y(sp)

        @block.scalar
        def _(act):
            act.wait_ge(zeroed, 2)
            for rows in y_rows:
                flat = rows.rearrange("(a p r) h -> a p (r h)", p=P, r=8)
                for a in range(flat.shape[0]):
                    act.dma_start(flat[a], zeros[:]).then_inc(cleared, 16)
            act.dma_start(expert_rows[EMPTY:EMPTY + BLK, :].rearrange("(p a) r -> p a r", a=B), tail[:]).then_inc(cleared, 16)

            act.wait_ge(weights_in, 80)
            act.mul(bq2s[:], vc[:, V_BQ2:V_BQ2 + 1], SCALE).then_inc(vcopied, 1)
            act.wait_ge(consts, 1)
            act.activation(bv2c[:], ones[:], ACT.Copy, scale=vc[:, V_BV2:V_BV2 + 1]).then_inc(vcopied, 1)
            act.wait_ge(vcopied, 2)

            def empty(dst, name, i, cols=512, rows=P, **kw):
                b, n = use_of(name, i)
                act.wait_ge(filled[b], n + 1)
                if kw:
                    act.activation(dst, bank[b][0:rows, 0:cols], ACT.Identity, **kw).then_inc(freed[b], 1)
                else:
                    act.copy(dst, bank[b][0:rows, 0:cols]).then_inc(freed[b], 1)

            def exponentials(g, b):
                n = g * T + b
                act.wait_ge(z_clipped, n + 1)
                act.activation(z[:, b % 2, :], z[:, b % 2, :], ACT.Exp).then_inc(p_ready, 1)

            def weights_T(g, b, quadrants):
                n = g * T + b
                for c in quadrants:
                    act.wait_ge(pt_filled, n * 4 + c + 1)
                    act.copy(pT[:, b % 2, c * 512:(c + 1) * 512], PT[c % 2][0:NK, :]).then_inc(pt_freed, 1)

            def products(b, i):
                empty(pvs[:, b % 2, :], f"pv{b}", i, cols=2 * P)

            def body(i):
                L, M, X, R, W = (runs(stage, i) for stage in "LMXRW")
                gm, gx, gr, gw = (i - LAG[stage] for stage in "MXRW")
                if L:
                    empty(xnT[:], "xnT", i)
                if R:
                    empty(aoT[:], "aoT", i)
                if M:
                    empty(xn2T[:], "xn2T", i)
                if L:
                    b, n = use_of("q", i)
                    act.wait_ge(filled[b], n + 1)
                    act.activation(eq[:], bank[b][:], ACT.Exp, bias=vc[:, V_BQ:V_BQ + 1]).then_inc(eq_ready, 1)
                    act.activation(rq[:], bank[b][:], ACT.Relu, bias=vc[:, V_BQ:V_BQ + 1]).then_inc(freed[b], 1)
                if X:
                    exponentials(gx, 0)
                if X:
                    weights_T(gx, 0, range(2))
                if L:
                    for half in range(2):
                        b, n = use_of(f"kp{half}", i)
                        act.wait_ge(freed[b], n + 1)
                    act.activation(ek[:], kvb[:, :, 0:P], ACT.Exp).then_inc(ek_ready, 1)
                    act.activation(rk[:], kvb[:, :, 0:P], ACT.Relu).then_inc(rk_ready, 1)
                if X:
                    weights_T(gx, 0, range(2, 4))
                    products(0, i)
                if W:
                    if not (isinstance(gw, int) and gw == 0):
                        act.wait_ge(sent, gw * (T * 2 * 16))
                    act.copy(row[:, :, 0:P], xn3[:]).then_inc(row_filled, 1)
                if X:
                    exponentials(gx, 1)
                    weights_T(gx, 1, range(2))
                if L:
                    empty(cT[:], "cT", i)
                if X:
                    weights_T(gx, 1, range(2, 4))
                    products(1, i)
                    exponentials(gx, 2)
                    weights_T(gx, 2, range(2))
                if R:
                    empty(xn3T[:], "xn3T", i)
                if X:
                    weights_T(gx, 2, range(2, 4))
                    products(2, i)
                if M:
                    empty(k2[:], "k2T", i, cols=T * NK, bias=vc[:, V_BK2:V_BK2 + 1])
                if X:
                    exponentials(gx, 3)
                    weights_T(gx, 3, range(2))
                if M:
                    empty(q2[:], "q2T", i, bias=bq2s[:], scale=SCALE)
                if X:
                    weights_T(gx, 3, range(2, 4))
                    products(3, i)
                if M:
                    m, u = use_of("v2", i)
                    act.wait_ge(filled[m], u + 1)
                    heads = bank[m][0:NK, :].rearrange("k (g j d) -> k g j d", j=HG, d=HD)
                    into = v2[:].rearrange("k b (q j) c -> k (b q) j c", j=HG)
                    for j in range(HG):
                        ins = act.copy(into[:, :, j, j * HD:(j + 1) * HD], heads[:, :, j, :])
                    ins.then_inc(freed[m], 1)
                if R:
                    act.wait_ge(chosen, (gr + 1) * CHOOSE)
                    act.activation(eg[:], gap[:], ACT.Exp).then_inc(eg_ready, 1)

            iterations(act, body)
            ffn_scalar(act)
            store_out(act)

        @block.gpsimd
        def _(pool):
            pool.memset(ones[:], 1.0).then_inc(consts, 1)
            pool.memset(expo[:], -0.5)
            pool.memset(zeros[:], 0.0)
            pool.memset(tail[:], 0.0)
            pool.memset(carry[:], 0.0)
            pool.memset(ident[:], 0.0)
            pool.memset(before[:], 1.0)
            pool.memset(bmask[:], 1.0)
            pool.iota(tok_i[:], pattern=[[P, NB]], base=0, channel_multiplier=1)
            pool.iota(e_i[:, 0], pattern=[[E * REG, 2], [REG, E]], base=-1, channel_multiplier=0)
            pool.iota(e_i[:, 1], pattern=[[0, 2], [-1, E]], base=E, channel_multiplier=0)
            pool.iota(e_i[:, 2], pattern=[[0, 2], [1, E]], base=0, channel_multiplier=0)
            pool.iota(j_i[:], pattern=[[0, 1]], base=0, channel_multiplier=1)
            pool.memset(kvb[:], 1.0)
            pool.memset(v2[:], 0.0).then_inc(zeroed, 1)
            pool.wait_ge(zeroed, 1)
            for j in range(HG):
                pool.memset(v2[:].rearrange("k b (q j) c -> k (b q) j c", j=HG)[:, :, j, 32 + j:33 + j], 1.0)
            pool.iota(tail[:, :, P].bitcast(I32), pattern=[[0, B]], base=int(BIG), channel_multiplier=0)\
                .then_inc(zeroed, 1)
            pool.affine_select(out=ident[:], in_=ident[:], compare_op=ALU.not_equal, fill=1.0, base=0,
                               pattern=[[-1, P]], channel_multiplier=1)
            pool.affine_select(out=before[:], in_=before[:], compare_op=ALU.is_ge, fill=0.0, base=0,
                               pattern=[[1, P]], channel_multiplier=-1)
            heads = bmask[:].rearrange("p (h d) -> p h d", d=HD)
            pool.affine_select(out=heads, in_=heads, compare_op=ALU.is_ge, fill=0.0, base=0,
                               pattern=[[-HD, NH], [0, HD]], channel_multiplier=1).then_inc(consts, 1)
            pool.wait_ge(consts, 2)
            pool.affine_select(out=heads, in_=heads, compare_op=ALU.is_ge, fill=0.0, base=HD - 1,
                               pattern=[[HD, NH], [0, HD]], channel_multiplier=-1).then_inc(consts, 1)
            pool.tensor_copy(e_f[:], e_i[:]).then_inc(consts, 1)
            pool.tensor_copy(j_f[:], j_i[:]).then_inc(consts, 1)

            def inverse_root(dst, variance, eps, moments, part, ready, g):
                wait_apart(pool, moments, g * T + T)
                pool.tensor_scalar(dst[:], variance, eps, None, ALU.add).then_inc(part, 1)
                pool.wait_ge(part, g + 1)
                pool.tensor_tensor(dst[:], dst[:], expo[:], ALU.pow).then_inc(ready, 1)

            pool.wait_ge(weights_in, 80)
            pool.wait_ge(hmask_ready, 2)
            pool.wait_ge(bo_ready, 1)

            def body(i):
                N, L, M, R, V = (runs(stage, i) for stage in "NLMRV")
                gm, gr, gv = (i - LAG[stage] for stage in "MRV")
                if V:
                    pool.wait_ge(row_filled, gv + 1)
                    wait_apart(pool, placed, (gv + 1) * PLACE)
                    for b in range(T):
                        for k in range(2):
                            pool.indirect_dma_start(
                                out=expert_rows, out_offset=bass.IndirectOffsetOnAxis(
                                    ap=slot[:, b * 2 + k:b * 2 + k + 1], axis=0),
                                in_=row[:, b, :], in_offset=None,
                                bounds_check=EMPTY - 1, oob_is_err=False).then_inc(sent, 16)
                if L:
                    pool.wait_ge(xn_ready, i * T + T)
                    pool.tensor_tensor(xb[:], xn[:], bc(vb[:, V_BD], 1, T), ALU.add).then_inc(xb_ready, 1)
                    pool.tensor_tensor(xbeta[:], group(xs, i), bc(vb[:, V_BETA], 1, T), ALU.add)\
                        .then_inc(xbeta_ready, 1)
                if R:
                    inverse_root(rs3, mv3[:, :, 1], EPS, moments3, rs3_part, rs3_ready, gr)
                if L:
                    inverse_root(hrs, hmv[:, :, 1], EPS_ATTN_LN, hmoments, hrs_part, hrs_ready, i)
                    pool.wait_ge(hn_ready, i * T + T)
                    pool.tensor_tensor(hg[:], hn[:], bc(vb[:, V_GAMMA], 1, T), ALU.mult).then_inc(hg_ready, 1)
                if M:
                    m, u = use_of("k2T", i)
                    pool.wait_ge(freed[m], u + 1)
                    for b in range(T):
                        pool.tensor_tensor(kblk[:, b], bc(k2[:, b * NK:(b + 1) * NK], 1, HG),
                                           bc(hmask[:], 2, NK), ALU.mult).then_inc(kblk_ready, 1)
                if L:
                    inverse_root(rs2, mv2[:, :, 1], EPS, moments2, rs2_part, rs2_ready, i)
                if N:
                    inverse_root(rs, mv[:, :, 1], EPS, moments, rs_part, rs_ready, i + 1)
                if L:
                    wait_apart(pool, x1_ready, i + 1)
                    pool.tensor_tensor(group(xs, i), x1[:], bc(bo_all[:], 1, T), ALU.add).then_inc(x1_kept, 1)


            inverse_root(rs, mv[:, :, 1], EPS, moments, rs_part, rs_ready, 0)
            iterations(pool, body)
            ffn_scatter(pool)

        @block.vector
        def _(dve):
            dve.wait_ge(consts, 5)
            dve.tensor_reduce(hmask[:], bmask[:].rearrange("p (q j d) -> p j q d", q=HG, d=HD)[:, :, :, 0],
                              AX.X, ALU.add).then_inc(hmask_ready, 1)
            dve.tensor_copy(hmask16[:], bmask[:].rearrange("p (h d) -> p h d", d=HD)[:, :, 0]).then_inc(hmask_ready, 1)
            dve.wait_ge(hmask_ready, 2)
            dve.wait_ge(bo_filled, 1)
            dve.tensor_tensor(bo_all[:], PT[0][:, 0:P], vb[:, V_BO2], ALU.add).then_inc(bo_ready, 1)

            def moments_of(src, st, mv, sem_stats, sem_moments, g):
                for b in range(T):
                    dve.bn_stats(st[:, b, :], src(b)).then_inc(sem_stats, 1)
                for b in range(T):
                    wait_apart(dve, sem_stats, g * T + b + 1)
                    dve.bn_aggr(mv[:, b, :], st[:, b, :]).then_inc(sem_moments, 1)

            def normal(dst, src, mv, rs, rs_ready, ready, g):
                dve.wait_ge(rs_ready, g + 1)
                for b in range(T):
                    dve.tensor_scalar(dst(b), src(b), mv[:, b, 0:1], rs[:, b:b + 1], ALU.subtract, ALU.mult)\
                       .then_inc(ready, 1)

            def tile_of(g):
                return lambda b: (xs[:, g * T + b, :] if isinstance(g, int)
                                  else xs[:, ds(g * T + b, 1), :].rearrange("p a h -> p (a h)"))

            def softmax_shift(g, b):
                n = g * T + b
                for half in range(2):
                    qs = slice(2 * half, 2 * half + 2)
                    dve.wait_ge(scored, n * 2 + half + 1)
                    dve.tensor_reduce(mraw[:, half, :].rearrange("p (q h) -> p q h", q=2),
                                      S[:, qs, 0:HG * NK].rearrange("p q (h k) -> p q h k", k=NK),
                                      AX.X, ALU.max).then_inc(m_raw, 1)
                dve.wait_ge(m_raw, n * 2 + 2)
                dve.tensor_scalar(mclip[:], mraw[:], CLAMP, -CLAMP, ALU.min, ALU.max).then_inc(m_clipped, 1)
                dve.wait_ge(m_clipped, n + 1)
                if not (isinstance(n, int) and n < 2):
                    dve.wait_ge(pt_filled, n * 4 - 4)
                for q in range(HG):
                    c = q * HG * NK
                    dve.scalar_tensor_tensor(
                        out=z[:, b % 2, c:c + HG * NK].rearrange("p (h k) -> p h k", k=NK),
                        in0=S[:, q, 0:HG * NK].rearrange("p (h k) -> p h k", k=NK),
                        scalar=-CLAMP, in1=bc(mclip[:, q // 2, (q % 2) * HG:(q % 2 + 1) * HG], 2, NK),
                        op0=ALU.max, op1=ALU.subtract).then_inc(z_ready, 1)

                dve.wait_ge(z_ready, n * 4 + 4)
                dve.tensor_scalar(z[:, b % 2, :], z[:, b % 2, :], 0.0, None, ALU.min).then_inc(z_clipped, 1)

            def softmax_divide(g, b, i):
                n = g * T + b
                m, u = use_of(f"pvT{b}", i)
                pv = bank[m][:, 0:2 * P].rearrange("p (q c) -> p q c", c=64)
                dve.wait_ge(filled[m], u + 1)
                dve.reciprocal(rd[:], pv[:, :, 32:32 + HG]).then_inc(rd_ready, 1)
                dve.wait_ge(rd_ready, n + 1)
                dve.tensor_tensor(ao[:, b, :].rearrange("p (q j d) -> p q j d", j=HG, d=HD),
                                  pv[:, :, 0:32].rearrange("p q (j d) -> p q j d", d=HD),
                                  bc(rd[:], 3, HD), ALU.mult).then_inc(freed[m], 1)

            def choose(g, i):
                done = [0]

                def step(ins):
                    ins.then_inc(chosen, 1)
                    done[0] += 1

                def settle():
                    dve.wait_ge(chosen, g * CHOOSE + done[0])

                m, u = use_of("logits", i)
                dve.wait_ge(filled[m], u + 1)
                dve.tensor_copy(lg[:], bank[m][:, 0:T * E].rearrange("p (b e) -> p b e", e=E)).then_inc(freed[m], 1)
                dve.wait_ge(freed[m], u + 1)
                src = lg
                for k in range(2):
                    step(dve.tensor_reduce(top[:, k, :], src[:], AX.X, ALU.max))
                    settle()
                    step(dve.tensor_tensor(tie[:], src[:], bc(top[:, k, :], 2, E), ALU.is_equal))
                    settle()
                    step(dve.tensor_tensor(tie[:], tie[:], bc(e_f[:, 1, 0, :], 1, T), ALU.mult))
                    settle()
                    step(dve.tensor_reduce(tiem[:], tie[:], AX.X, ALU.max))
                    settle()
                    step(dve.tensor_tensor(hot[:, :, k, :], bc(e_f[:, 1, 0, :], 1, T), bc(tiem[:], 2, E),
                                           ALU.is_equal))
                    if k == 0:
                        settle()
                        step(dve.scalar_tensor_tensor(out=low[:], in0=hot[:, :, 0, :], scalar=-3e38,
                                                      in1=lg[:], op0=ALU.mult, op1=ALU.add))
                        settle()
                        src = low
                step(dve.tensor_tensor(gap[:], top[:, 1, :], top[:, 0, :], ALU.subtract))
                assert done[0] == CHOOSE

            def place(g):
                done = [0]

                def step(ins):
                    ins.then_inc(placed, 1)
                    done[0] += 1

                def settle():
                    dve.wait_ge(placed, g * PLACE + done[0])

                if not (isinstance(g, int) and g == 0):
                    dve.wait_ge(sent, g * (T * 2 * 16))
                dve.wait_ge(eg_ready, g + 1)
                step(dve.tensor_scalar(eg1[:], eg[:], 1.0, None, ALU.add))
                settle()
                step(dve.reciprocal(row[:, :, P + 1], eg1[:]))
                settle()
                step(dve.tensor_tensor(row[:, :, P + 2], eg[:], row[:, :, P + 1], ALU.mult))
                toks = tok_i[:, g * T:(g + 1) * T] if isinstance(g, int) else tok_i[:, ds(g * T, T)]
                step(dve.tensor_copy(row[:, :, P].bitcast(I32), toks))
                wait_apart(dve, ranks_read, g + 1)
                for b in range(T):
                    if b:
                        settle()
                    step(dve.tensor_tensor(carry[:, b + 1, :], carry[:, b, :], rank[:, 1, b, :], ALU.add))
                settle()
                step(dve.tensor_tensor(pos[:], rank[:, 0], carry[:, 0:T, :], ALU.add))
                settle()
                step(dve.tensor_copy(carry[:, 0, :], carry[:, T, :]))
                hot8 = hot[:].rearrange("p b k e -> p (b k) e")
                step(dve.tensor_tensor(pick[:, 0], hot8, pos[:].rearrange("p b (k e) -> p (b k) e", k=2), ALU.mult))
                step(dve.tensor_tensor(pick[:, 1].rearrange("p (b k) e -> p b (k e)", k=2),
                                       hot[:].rearrange("p b k e -> p b (k e)"),
                                       bc(e_f[:, 0].rearrange("p k e -> p (k e)"), 1, T), ALU.mult))
                settle()
                step(dve.tensor_reduce(sel[:], pick[:], AX.X, ALU.add))
                settle()
                step(dve.tensor_scalar(over[:], sel[:, 0], float(CAP), BIG, ALU.is_gt, ALU.mult))
                step(dve.tensor_tensor(slot_f[:], sel[:, 0], sel[:, 1], ALU.add))
                settle()
                step(dve.tensor_tensor(slot[:], slot_f[:], over[:], ALU.add))
                assert done[0] == PLACE

            def body(i):
                N, L, X, R, W = (runs(stage, i) for stage in "NLXRW")
                gx, gr, gw = (i - LAG[stage] for stage in "XRW")
                if X:
                    softmax_shift(gx, 0)
                if R:
                    m, u = use_of("x2", i)
                    dve.wait_ge(filled[m], u + 1)
                    dve.wait_ge(x1_kept, gr + 1)
                    dve.tensor_tensor(group(xs, gr), bank[m][:].rearrange("p (b h) -> p b h", b=T),
                                      group(xs, gr), ALU.add).then_inc(freed[m], 1)
                if L:
                    for half in range(2):
                        m, u = use_of(f"kp{half}", i)
                        dve.wait_ge(filled[m], u + 1)
                        dve.tensor_tensor(kvb[:, 2 * half:2 * half + 2, 0:2 * P],
                                          bank[m][:].rearrange("p (b h) -> p b h", b=2),
                                          bc(vb[:, V_BK:V_BV + 1].rearrange("p a h -> p (a h)"), 1, 2),
                                          ALU.add).then_inc(freed[m], 1)
                    dve.wait_ge(eq_ready, i + 1)
                    m, u = use_of("q", i)
                    dve.wait_ge(freed[m], u + 1)
                    dve.scalar_tensor_tensor(out=qT[:], in0=eq[:], scalar=1.0, in1=rq[:], op0=ALU.min, op1=ALU.add)\
                       .then_inc(qT_ready, 1)
                    dve.wait_ge(ek_ready, i + 1)
                    dve.wait_ge(rk_ready, i + 1)
                    dve.scalar_tensor_tensor(out=kk[:], in0=ek[:], scalar=1.0, in1=rk[:], op0=ALU.min, op1=ALU.add)\
                       .then_inc(kk_ready, 1)
                if X:
                    softmax_shift(gx, 1)
                if L:
                    for half in range(2):
                        m, u = use_of(f"kv{half}", i)
                        pair = slice(2 * half, 2 * half + 2)
                        got = bank[m][:, 0:2 * (P + 1)].rearrange("p (b h) -> p b h", b=2)
                        dve.wait_ge(filled[m], u + 1)
                        dve.tensor_tensor(kvm[:, pair, 0:P], got[:, :, 0:P], bc(bmask[:], 1, 2), ALU.mult)\
                           .then_inc(kvm_ready, 1)
                        dve.scalar_tensor_tensor(out=kvm[:, pair, P:P + NH],
                                                 in0=got[:, :, P:P + 1].broadcast_to([P, 2, NH]), scalar=EPS_ATTN,
                                                 in1=bc(hmask16[:], 1, 2), op0=ALU.add, op1=ALU.mult)\
                           .then_inc(freed[m], 1)
                if X:
                    softmax_divide(gx, 0, i)
                if R:
                    m, u = use_of("x2", i)
                    wait_apart(dve, freed[m], u + 1)
                    moments_of(tile_of(gr), st3, mv3, stats3, moments3, gr)
                if L:
                    attention_divide(i, 0)
                    attention_divide(i, 1)
                if R:
                    if not (isinstance(gr, int) and gr == 0):
                        dve.wait_ge(row_filled, gr)
                    normal(lambda b: xn3[:, b, :], tile_of(gr), mv3, rs3, rs3_ready, xn3_ready, gr)
                if X:
                    softmax_shift(gx, 2)
                if W:
                    place(gw)
                if L:
                    m, u = use_of("hs", i)
                    dve.wait_ge(filled[m], u + 1)
                    dve.wait_ge(xb_ready, i + 1)
                    dve.tensor_tensor(hs[:], bank[m][:].rearrange("p (b h) -> p b h", b=T), xb[:], ALU.add)\
                       .then_inc(freed[m], 1)
                    wait_apart(dve, freed[m], u + 1)
                    moments_of(lambda b: hs[:, b, :], hst, hmv, hstats, hmoments, i)
                if X:
                    softmax_divide(gx, 1, i)
                if X:
                    softmax_shift(gx, 3)
                if L:
                    normal(lambda b: hn[:, b, :], lambda b: hs[:, b, :], hmv, hrs, hrs_ready, hn_ready, i)
                if X:
                    softmax_divide(gx, 2, i)
                if R:
                    choose(gr, i)
                if L:
                    dve.wait_ge(hg_ready, i + 1)
                    dve.wait_ge(xbeta_ready, i + 1)
                    dve.tensor_tensor(x1[:], hg[:], xbeta[:], ALU.add).then_inc(x1_ready, 1)
                    wait_apart(dve, x1_ready, i + 1)
                    moments_of(lambda b: x1[:, b, :], st2, mv2, stats2, moments2, i)
                if N:
                    wait_apart(dve, x_in, (i + 1) * 16 + 16)
                    moments_of(tile_of(i + 1), st, mv, stats, moments, i + 1)
                if L:
                    normal(lambda b: xn2[:, b, :], lambda b: x1[:, b, :], mv2, rs2, rs2_ready, xn2_ready, i)
                if R:
                    dve.wait_ge(ranked, gr + 1)
                    dve.tensor_copy(rank[:].rearrange("p a b e -> p (a b e)"), ranks).then_inc(ranks_read, 1)
                if N:
                    normal(lambda b: xn[:, b, :], tile_of(i + 1), mv, rs, rs_ready, xn_ready, i + 1)
                if X:
                    softmax_divide(gx, 3, i)

            def attention_divide(i, half):
                m, u = use_of(f"nd{half}", i)
                pair = slice(2 * half, 2 * half + 2)
                got = bank[m][:, 0:2 * (P + NH)].rearrange("p (b h) -> p b h", b=2)
                dve.wait_ge(filled[m], u + 1)
                dve.reciprocal(rdn[:, pair, :], got[:, :, P:P + NH]).then_inc(rdn_ready, 1)
                dve.wait_ge(rdn_ready, i * 2 + half + 1)
                dve.tensor_tensor(cx[:, pair, :].rearrange("p b (h d) -> p b h d", d=HD),
                                  got[:, :, 0:P].rearrange("p b (h d) -> p b h d", d=HD),
                                  bc(rdn[:, pair, :], 3, HD), ALU.mult).then_inc(freed[m], 1)

            dve.wait_ge(x_in, 16)
            moments_of(tile_of(0), st, mv, stats, moments, 0)
            normal(lambda b: xn[:, b, :], tile_of(0), mv, rs, rs_ready, xn_ready, 0)
            iterations(dve, body)
            make_tables(dve)
            ffn_vector(dve)
            combine(dve)


def kernel(**inputs):
    import numpy as np
    import concourse.bacc as bacc
    from concourse.bass_utils import run_bass_kernel_spmd

    a = {k: np.asarray(v) for k, v in inputs.items()}
    A, C, M = "L0_attn_", "L0_xattn_", "L0_ffn_"
    vectors = [a[A + n] for n in ("bq", "bk", "bv", "bd", "gamma", "beta")] + \
              [a[C + n] for n in ("bq", "bk", "bv", "bo")]
    arrays = {
        "x": a["x"],
        "ctxT": a["ctx_768"].reshape(NB * NK, CK).T,
        "wA": np.stack([a[A + "Wq"].T, a[A + "Wk"].T, a[A + "Wv"].T, a[A + "Wd"].T, a[C + "Wq"], a[C + "Wo"]], axis=1),
        "wC": np.stack([a[C + "Wk"], a[C + "Wv"]], axis=1),
        "wr": a[M + "router_w"].T,
        "w1": a[M + "w1"].transpose(1, 0, 2).reshape(P, E * F),
        "w2": a[M + "w2"].reshape(E, FC, P, P).transpose(2, 0, 1, 3).reshape(P, E * FC * P),
        "vrow": np.stack(vectors),
        "vcol": np.stack(vectors, axis=1),
    }
    arrays = {k: np.ascontiguousarray(v) for k, v in arrays.items()}
    nc = bacc.Bacc("TRN2", target_bir_lowering=False, num_devices=1)
    args = [nc.dram_tensor(k, v.shape, F32, kind="ExternalInput").ap() for k, v in arrays.items()]
    out = nc.dram_tensor("out", [NB, P, P], F32, kind="ExternalOutput").ap()
    expert_rows = nc.dram_tensor("expert_rows", [EMPTY + BLK, ROW], F32, kind="Internal").ap()
    y_rows = [nc.dram_tensor(f"y_rows{k}", [NB * P, P], F32, kind="Internal").ap() for k in range(2)]
    decoder_layer(nc, *args, out, expert_rows, y_rows)
    r = run_bass_kernel_spmd(nc, [arrays], core_ids=[0])
    return r.results[0]["out"]
```

```python
from contextlib import ExitStack

import concourse.bass as bass
from concourse import mybir

F32 = mybir.dt.float32
I32 = mybir.dt.int32
U32 = mybir.dt.uint32
ALU = mybir.AluOpType
ACT = mybir.ActivationFunctionType
AX = mybir.AxisListType
ds = bass.ds

P = 128
NB = 64
T = 4
NG = NB // T
NH, HD = 16, 8
HG = 4
NK, CK = 77, 96
E, F = 8, 512
FC = F // P
CAP = max(1, int(1.25 * NB * P / E * 2))
B = 2
BLK = B * P
REG = CAP + BLK
NREG = 2 * E
EMPTY = NREG * REG
NBLK = NB // B + E
FIRST = (2, NBLK // 4 - NG // 2 + 1)
ROW = P + 3
BIG = float(1 << 20)
CLAMP = 10000.0
SCALE = HD ** -0.5
EPS = 1e-5
EPS_ATTN, EPS_ATTN_LN = 1e-6, 1e-12
V_BQ, V_BK, V_BV, V_BD, V_GAMMA, V_BETA, V_BQ2, V_BK2, V_BV2, V_BO2 = range(10)
NV = 10
W_Q, W_K, W_V, W_D, W_Q2, W_O2 = range(6)

USES = [("xnT", "L"), ("aoT", "R"), ("xn2T", "M"), ("q", "L"), ("x2", "R"), ("kp0", "L"), ("kp1", "L"),
        ("pv0", "X"), ("kv0", "L"), ("kv1", "L"), ("pvT0", "X"), ("nd0", "L"), ("nd1", "L"),
        ("cT", "L"), ("pv1", "X"), ("hs", "L"), ("pvT1", "X"), ("xn3T", "R"), ("pv2", "X"),
        ("k2T", "M"), ("pvT2", "X"), ("lgT", "R"), ("q2T", "M"), ("pv3", "X"), ("v2", "M"), ("pvT3", "X")]
LAG = {"N": -1, "L": 0, "M": 1, "X": 2, "R": 3, "W": 4, "V": 5}


def runs(stage, i):
    return not isinstance(i, int) or 0 <= i - LAG[stage] < NG


def use_of(name, i):
    at = [n for n, _ in USES].index(name)
    bank = at % 2
    mine = [s for n, s in USES[bank::2]]
    if isinstance(i, int):
        before = sum(min(max(i - LAG[s], 0), NG) for s in mine)
    else:
        before = i * len(mine) - sum(LAG[s] for s in mine)
    return bank, before + sum(1 for n, s in USES[bank:at:2] if runs(s, i))


def decoder_layer(nc, x, ctxT, wA, wC, wr, w1, w2, vrow, vcol, out, expert_rows, y_rows):
    with ExitStack() as ctx:
        def sb(name, shape, dt=F32):
            return ctx.enter_context(nc.sbuf_tensor(name, shape, dt))

        def sem(name):
            return ctx.enter_context(nc.semaphore(name))

        wA_s = sb("wA_s", [P, 6, P])
        wC_s = sb("wC_s", [CK, 2, P])
        wr_s = sb("wr_s", [P, E])
        w1_s = sb("w1_s", [P, E * F])
        w2_s = sb("w2_s", [P, E * FC * P])
        vb = sb("vb", [P, NV, P])
        vc = sb("vc", [P, NV])
        ident = sb("ident", [P, P])
        ones = sb("ones", [P, P])
        before = sb("before", [P, P])
        bmask = sb("bmask", [P, P])
        hmask = sb("hmask", [P, HG])
        hmask16 = sb("hmask16", [P, NH])
        expo = sb("expo", [P, T])
        minus = sb("minus", [P, T])
        bq2s = sb("bq2s", [P, 1])
        bv2c = sb("bv2c", [P, P])
        bo_all = sb("bo_all", [P, P])
        tok_i = sb("tok_i", [P, NB], I32)
        e_i = sb("e_i", [P, 3, 2, E], I32)
        e_f = sb("e_f", [P, 3, 2, E])
        j_i = sb("j_i", [P, 1], I32)
        j_f = sb("j_f", [P, 1])
        zeros = sb("zeros", [P, 1024])
        tail = sb("tail", [P, B, ROW])
        xs = sb("xs", [P, NB, P])
        st = sb("st", [P, T, 6])
        mv = sb("mv", [P, T, 2])
        rs = sb("rs", [P, T])
        shift = sb("shift", [P, T])
        shift3 = sb("shift3", [P, T])
        xn = sb("xn", [P, T, P])
        xb_xbeta = sb("xb_xbeta", [P, 2 * T, P])
        xb, xbeta = xb_xbeta[:, 0:T], xb_xbeta[:, T:2 * T]
        xnT = sb("xnT", [P, T * P])
        eq = sb("eq", [P, T * P])
        rq = sb("rq", [P, T * P])
        qT_cT = sb("qT_cT", [P, 2, T * P])
        qT, cT = qT_cT[:, 0], qT_cT[:, 1]
        kvb = sb("kvb", [P, T, 2 * P + 1])
        ek = sb("ek", [P, T, P])
        rk = sb("rk", [P, T, P])
        kk = sb("kk", [P, T, P])
        kvm = sb("kvm", [P, T, P + NH])
        rdn = sb("rdn", [P, T, NH])
        cx = sb("cx", [P, T, P])
        hs_hn = sb("hs_hn", [P, 2 * T, P])
        hs, hn = hs_hn[:, 0:T], hs_hn[:, T:2 * T]
        hst = sb("hst", [P, T, 6])
        hmv = sb("hmv", [P, T, 2])
        hrs = sb("hrs", [P, T])
        x1_hg = sb("x1_hg", [P, 2 * T, P])
        x1, hg = x1_hg[:, 0:T], x1_hg[:, T:2 * T]
        st2 = sb("st2", [P, T, 6])
        mv2 = sb("mv2", [P, T, 2])
        rs2 = sb("rs2", [P, T])
        xn2 = sb("xn2", [P, T, P])
        xn2T = sb("xn2T", [P, T * P])
        cg = sb("cg", [CK, T * NK])
        q2 = sb("q2", [P, T * P])
        k2 = sb("k2", [P, T * NK])
        v2 = sb("v2", [NK, T, NH, 64])
        pvs = sb("pvs", [P, 2, 2 * P])
        kblk = sb("kblk", [P, T, HG, NK])
        mraw = sb("mraw", [P, 2, NH // 2])
        mclip = sb("mclip", [P, 2, NH // 2])
        z = sb("z", [P, 2, NH * NK])
        pT = sb("pT", [NK, 2, NH * P])
        rd = sb("rd", [P, HG, HG])
        ao = sb("ao", [P, T, P])
        aoT = sb("aoT", [P, T * P])
        st3 = sb("st3", [P, T, 6])
        mv3 = sb("mv3", [P, T, 2])
        rs3 = sb("rs3", [P, T])
        xn3 = sb("xn3", [P, T, P])
        row = sb("row", [P, T, ROW])
        xn3T = sb("xn3T", [P, T * P])
        lgT = sb("lgT", [E, T * P])
        lg = sb("lg", [P, T, E])
        top = sb("top", [P, 2, T])
        hot = sb("hot", [P, T, 2, E])
        hot_kept = sb("hot_kept", [P, T, 2, E])
        tie = sb("tie", [P, T, E])
        tiem = sb("tiem", [P, T])
        low = sb("low", [P, T, E])
        gap = sb("gap", [P, T])
        eg = sb("eg", [P, T])
        eg1 = sb("eg1", [P, T])
        carry = sb("carry", [P, T + 1, 2 * E])
        rank = sb("rank", [P, 2, T, 2 * E])
        pos = sb("pos", [P, T, 2 * E])
        pick = sb("pick", [P, 2, T * 2, E])
        sel = sb("sel", [P, 2, T * 2])
        over = sb("over", [P, T * 2])
        slot_f = sb("slot_f", [P, T * 2])
        slot = sb("slot", [P, T * 2], U32)

        cnt = sb("cnt", [P, 2 * E])
        cnt_i = sb("cnt_i", [P, 2 * E], I32)
        nt = sb("nt", [P, 2 * E])
        tail_f = sb("tail_f", [P, 2 * E])
        tail_i = sb("tail_i", [P, 2 * E], I32)
        ends = sb("ends", [P, 2, E])
        past = sb("past", [P, 2, 2, E])
        sums = sb("sums", [P, 2, 2])
        rowf = sb("rowf", [P, 2])
        none = sb("none", [P, 2])
        tab = sb("tab", [P, 8])
        tab_i = sb("tab_i", [4, P], I32)
        xt = sb("xt", [P, 4, B, ROW])
        meta = sb("meta", [P, 4, B, 3])
        xtT = sb("xtT", [P, 2, BLK])
        hT = z[:, :, 0:FC * BLK]
        w1_e = hs_hn[:].rearrange("p (s a) h -> p s (a h)", s=2)
        w2_e = xb_xbeta[:].rearrange("p (s a) h -> p s (a h)", s=2)
        ys = x1_hg[:].rearrange("p (s a) h -> p s a h", a=B)
        yT = eq[:].rearrange("p (s c) -> p s c", s=2)
        yt = sb("yt", [P, 4, B], U32)
        y0b = qT_cT[:].rearrange("p v (b h) -> p v b h", b=T)
        yb = w1_s[:, 0:4 * T * P].rearrange("p (s b h) -> p s b h", s=4, b=T)
        ob = w1_s[:, 4 * T * P:8 * T * P].rearrange("p (s b h) -> p s b h", s=4, b=T)

        bank = [ctx.enter_context(nc.psum_tensor(f"bank{m}", [P, 512], F32)) for m in range(2)]
        S = ctx.enter_context(nc.psum_tensor("S", [P, HG, 512], F32))
        PT = [ctx.enter_context(nc.psum_tensor(f"PT{m}", [P, 512], F32)) for m in range(2)]

        ranks = S[:, HG - 1, HG * NK:HG * NK + 2 * T * 2 * E]
        logits = S[:, HG - 1, HG * NK + 2 * T * 2 * E:HG * NK + 2 * T * 2 * E + T * E]

        weights_in, ffn_in, x_in, ctx_in = sem("weights_in"), sem("ffn_in"), sem("x_in"), sem("ctx_in")
        consts, zeroed, hmask_ready = sem("consts"), sem("zeroed"), sem("hmask_ready")
        vectors_ready, bo_filled, bo_ready = sem("vectors_ready"), sem("bo_filled"), sem("bo_ready")
        cleared = sem("cleared")
        filled = [sem(f"filled{m}") for m in range(2)]
        freed = [sem(f"freed{m}") for m in range(2)]
        stats, moments, rs_part, rs_ready = sem("stats"), sem("moments"), sem("rs_part"), sem("rs_ready")
        xn_ready, xb_ready, xbeta_ready = sem("xn_ready"), sem("xb_ready"), sem("xbeta_ready")
        eq_clipped = sem("eq_clipped")
        eq_ready, qT_ready = sem("eq_ready"), sem("qT_ready")
        ek_ready, rk_ready, kk_ready = sem("ek_ready"), sem("rk_ready"), sem("kk_ready")
        kvm_ready, rdn_ready = sem("kvm_ready"), sem("rdn_ready")
        hstats, hmoments, hrs_part, hrs_ready = sem("hstats"), sem("hmoments"), sem("hrs_part"), sem("hrs_ready")
        hn_ready, hg_ready, x1_ready, x1_kept = sem("hn_ready"), sem("hg_ready"), sem("x1_ready"), sem("x1_kept")
        stats2, moments2, rs2_part, rs2_ready = sem("stats2"), sem("moments2"), sem("rs2_part"), sem("rs2_ready")
        xn2_ready = sem("xn2_ready")
        kblk_ready, scored = sem("kblk_ready"), sem("scored")
        m_raw, m_clipped, z_ready, z_clipped, p_ready = (sem("m_raw"), sem("m_clipped"), sem("z_ready"),
                                                         sem("z_clipped"), sem("p_ready"))
        pt_filled, pt_freed, rd_ready = sem("pt_filled"), sem("pt_freed"), sem("rd_ready")
        stats3, moments3, rs3_part, rs3_ready = sem("stats3"), sem("moments3"), sem("rs3_part"), sem("rs3_ready")
        xn3_ready, chosen, placed, eg_ready, sent = (sem("xn3_ready"), sem("chosen"), sem("placed"),
                                                     sem("eg_ready"), sem("sent"))

        gate_steps = sem("gate_steps")
        counted = sem("counted")
        kept, routed = sem("kept"), sem("routed")
        ranked, ranks_read, row_filled = sem("ranked"), sem("ranks_read"), sem("row_filled")
        table_steps, tails_known, tails_in = sem("table_steps"), sem("tails_known"), sem("tails_in")
        tab_ready, tabT_filled, tables_ready = sem("tab_ready"), sem("tabT_filled"), sem("tables_ready")
        w1_ready, w2_ready = ([sem(f"{name}{m}") for m in range(4)] for name in ("w1_ready", "w2_ready"))
        xt_in, xt_used, meta_ready, xtT_ready, h_filled, hT_ready, yT_filled, yT_ready, y_filled, ys_ready, \
            y_sent = ([sem(f"{name}{m}") for m in range(4)] for name in (
                "xt_in", "xt_used", "meta_ready", "xtT_ready", "h_filled", "hT_ready", "yT_filled", "yT_ready",
                "y_filled", "ys_ready", "y_sent"))
        y0_in, y0_added = ([sem(f"{name}{m}") for m in range(2)] for name in ("y0_in", "y0_added"))
        y_in, out_ready, out_stored = ([sem(f"{name}{m}") for m in range(4)] for name in (
            "y_in", "out_ready", "out_stored"))
        CLEARS = 2 * NB * P // (P * 8) + 1

        block = ctx.enter_context(nc.Block())
        CHOOSE, COUNT, PLACE = 13, 6, 6

        def bc(ap, axis, n):
            ap = ap.unsqueeze(axis)
            shape = list(ap.shape)
            shape[axis] = n
            return ap.broadcast_to(shape)

        def group(t, g):
            return t[:, ds(g * T, T), :] if not isinstance(g, int) else t[:, g * T:(g + 1) * T, :]

        def tile_of(g):
            return lambda b: (xs[:, g * T + b, :] if isinstance(g, int)
                              else xs[:, ds(g * T + b, 1), :].rearrange("p a h -> p (a h)"))

        def wait_apart(eng, sem, count):
            if not isinstance(count, int):
                count = eng.to_reg(count)
            eng.wait_ge(consts, 5)
            eng.wait_ge(sem, count)

        def iterations(eng, body):
            for i in range(LAG["V"] + 1):
                body(i)
            with eng.Fori(LAG["V"] + 1, NG - 1) as i:
                body(i)
            for i in range(NG - 1, NG + LAG["V"]):
                body(i)

        def write_tails(eng, regions):
            eng.wait_ge(tails_known, 1)
            for r in regions:
                at = eng.value_load(tail_i[0:1, r:r + 1], min_val=0, max_val=EMPTY - BLK)
                eng.dma_start(expert_rows[ds(at, BLK), :].rearrange("(p a) r -> p a r", a=B), tail[:])\
                   .then_inc(tails_in, 16)

        def ffn(eng, body, last):
            for k in range(2):
                first = FIRST[k]
                for step in range(4 * first):
                    body(k, step // 4, step % 4)
                with eng.Fori(first, NBLK // 4) as r:
                    for u in range(4):
                        body(k, r, u)
                for u in range(last):
                    body(k, NBLK // 4, u)

        def group_at(k, r, u):
            if k == 0 or u % 2 == 0 or isinstance(r, int) and not FIRST[1] - 1 <= r < NBLK // 4:
                return None
            return u // 2, (r - (FIRST[1] - 1)) * 2 + u // 2

        def block_at(k, r, u, lag):
            if isinstance(r, int) and not 0 <= 4 * r + u - lag < NBLK:
                return None
            return (u - lag) % 4, k * (NBLK // 4) + r + (u - lag) // 4, r * 4 + (u - lag)

        def block_before(slot, used, back):
            at, n = (slot - back) % 4, used + (slot - back) // 4
            return None if isinstance(n, int) and n < 0 else (at, n)

        def entry(row, j):
            return tab_i[row:row + 1, j:j + 1] if isinstance(j, int) else tab_i[row:row + 1, ds(j, 1)]

        def ffn_load(sp):
            sp.wait_ge(tables_ready, 1)
            sp.wait_ge(tails_in, NREG * 16)
            sp.wait_ge(sent, NG * T * 2 * 16)
            sp.wait_ge(cleared, CLEARS * 16)

            def body(k, r, u):
                t = block_at(k, r, u, 0)
                if t is None:
                    return
                slot, used, j = t
                if not (isinstance(used, int) and used == 0):
                    sp.wait_ge(xt_used[slot], used)
                    sp.wait_ge(meta_ready[slot], used)
                at = sp.value_load(entry(k, j), min_val=0, max_val=EMPTY)
                sp.dma_start(xt[:, slot], expert_rows[ds(at, BLK), :].rearrange("(p a) r -> p a r", a=B))\
                  .then_inc(xt_in[slot], 16)
                t = group_at(k, r, u)
                if t is not None:
                    v, g = t
                    if isinstance(g, int) and g == 0:
                        for slot in range(4):
                            sp.wait_ge(y_sent[slot], NBLK // 4 * B * 16)
                    if not isinstance(r, int):
                        sp.wait_ge(y0_added[v], r - (FIRST[1] - 1))
                    load_y(sp, 0, g, y0b[:, v], y0_in[v])

            ffn(sp, body, 0)

        def ffn_tensor(pe):
            pe.wait_ge(ffn_in, 32)
            pe.wait_ge(tables_ready, 1)
            pe.wait_ge(z_ready, NB * 4)
            pe.wait_ge(pt_freed, NB * 4)

            def body(k, r, u):
                t = block_at(k, r, u, 0)
                if t is not None:
                    slot, used, _ = t
                    pe.wait_ge(xt_in[slot], (used + 1) * 16)
                    p = block_before(slot, used, 2)
                    if p is not None:
                        pe.wait_ge(xtT_ready[p[0]], p[1] + 1)
                    for a in range(B):
                        ins = pe.transpose(bank[slot % 2][:, a * P:(a + 1) * P], xt[:, slot, a, 0:P], ident[:])
                    ins.then_inc(xt_used[slot], 1)
                t = block_at(k, r, u, 1)
                if t is not None:
                    slot, used, _ = t
                    pe.wait_ge(w1_ready[slot], used + 1)
                    pe.wait_ge(xtT_ready[slot], used + 1)
                    p = block_before(slot, used, 2)
                    if p is not None:
                        pe.wait_ge(hT_ready[p[0]], p[1] + 1)
                    for c in range(FC):
                        ins = pe.matmul(S[:, 2 * (slot % 2) + c // 2, (c % 2) * BLK:(c % 2 + 1) * BLK],
                                        w1_e[:, slot % 2, c * P:(c + 1) * P], xtT[:, slot % 2, :],
                                        start=True, stop=True)
                    ins.then_inc(h_filled[slot], 1)
                t = block_at(k, r, u, 2)
                if t is not None:
                    slot, used, _ = t
                    pe.wait_ge(w2_ready[slot], used + 1)
                    pe.wait_ge(hT_ready[slot], used + 1)
                    p = block_before(slot, used, 2)
                    if p is not None:
                        pe.wait_ge(ys_ready[p[0]], p[1] + 1)
                    for c in range(FC):
                        ins = pe.matmul(PT[slot % 2][:, 0:BLK], w2_e[:, slot % 2, c * P:(c + 1) * P],
                                        hT[:, slot % 2, c * BLK:(c + 1) * BLK], start=(c == 0), stop=(c == FC - 1))
                    ins.then_inc(yT_filled[slot], 1)
                t = block_at(k, r, u, 3)
                if t is not None:
                    slot, used, _ = t
                    pe.wait_ge(yT_ready[slot], used + 1)
                    for a in range(B):
                        ins = pe.transpose(PT[slot % 2][:, BLK + a * P:BLK + (a + 1) * P],
                                           yT[:, slot % 2, a * P:(a + 1) * P], ident[:])
                    ins.then_inc(y_filled[slot], 1)

            ffn(pe, body, 3)

        def ffn_vector(dve):
            def body(k, r, u):
                t = block_at(k, r, u, 0)
                if t is not None:
                    slot, used, j = t
                    e = dve.value_load(entry(2 + k, j), min_val=0, max_val=E - 1)
                    p = block_before(slot, used, 2)
                    if p is not None:
                        wait_apart(dve, h_filled[p[0]], p[1] + 1)
                    dve.tensor_copy(w1_e[:, slot % 2, :], w1_s[:, ds(e * F, F)]).then_inc(w1_ready[slot], 1)
                    dve.wait_ge(xt_in[slot], (used + 1) * 16)
                    if not (isinstance(used, int) and used == 0):
                        dve.wait_ge(ys_ready[slot], used)
                    dve.tensor_copy(meta[:, slot], xt[:, slot, :, P:ROW]).then_inc(meta_ready[slot], 1)
                    dve.wait_ge(xt_used[slot], used + 1)
                    dve.tensor_copy(xtT[:, slot % 2, :], bank[slot % 2][:, 0:BLK]).then_inc(xtT_ready[slot], 1)
                t = block_at(k, r, u, 2)
                if t is not None:
                    slot, used, _ = t
                    dve.wait_ge(yT_filled[slot], used + 1)
                    dve.tensor_copy(yT[:, slot % 2, :], PT[slot % 2][:, 0:BLK]).then_inc(yT_ready[slot], 1)
                t = block_at(k, r, u, 3)
                if t is not None:
                    slot, used, _ = t
                    if not (isinstance(used, int) and used == 0):
                        dve.wait_ge(y_sent[slot], used * B * 16)
                    dve.tensor_copy(yt[:, slot, :], meta[:, slot, :, 0].bitcast(I32))
                    dve.wait_ge(y_filled[slot], used + 1)
                    for a in range(B):
                        ins = dve.tensor_scalar(ys[:, slot, a, :], PT[slot % 2][:, BLK + a * P:BLK + (a + 1) * P],
                                                meta[:, slot, a, 1 + k:2 + k], None, ALU.mult)
                    ins.then_inc(ys_ready[slot], 1)
                t = group_at(k, r, u)
                if t is not None:
                    v, g = t
                    dve.wait_ge(y0_in[v], (r - (FIRST[1] - 2)) * 16)
                    dve.tensor_tensor(group(xs, g), group(xs, g), y0b[:, v], ALU.add).then_inc(y0_added[v], 1)

            dve.wait_ge(ffn_in, 32)
            dve.wait_ge(tables_ready, 1)
            ffn(dve, body, 3)

        def ffn_scalar(act):
            def body(k, r, u):
                t = block_at(k, r, u, 1)
                if t is not None:
                    slot, used, j = t
                    e = act.value_load(entry(2 + k, j), min_val=0, max_val=E - 1)
                    p = block_before(slot, used, 2)
                    if p is not None:
                        wait_apart(act, yT_filled[p[0]], p[1] + 1)
                    act.copy(w2_e[:, slot % 2, :], w2_s[:, ds(e * (FC * P), FC * P)]).then_inc(w2_ready[slot], 1)
                    act.wait_ge(h_filled[slot], used + 1)
                    q = 2 * (slot % 2)
                    act.activation(hT[:, slot % 2, :], S[:, q:q + 2, :].rearrange("p q c -> p (q c)"), ACT.Gelu)\
                       .then_inc(hT_ready[slot], 1)

            act.wait_ge(ffn_in, 32)
            act.wait_ge(tables_ready, 1)
            ffn(act, body, 1)

        def ffn_scatter(pool):
            def body(k, r, u):
                t = block_at(k, r, u, 3)
                if t is not None:
                    slot, used, _ = t
                    wait_apart(pool, ys_ready[slot], used + 1)
                    for a in range(B):
                        pool.indirect_dma_start(
                            out=y_rows[k], out_offset=bass.IndirectOffsetOnAxis(ap=yt[:, slot, a:a + 1], axis=0),
                            in_=ys[:, slot, a, :], in_offset=None,
                            bounds_check=NB * P - 1, oob_is_err=False).then_inc(y_sent[slot], 16)

            ffn(pool, body, 3)

        def make_tables(dve):
            done = [0]

            def step(ins):
                ins.then_inc(table_steps, 1)
                done[0] += 1
                dve.wait_ge(table_steps, done[0])

            dve.wait_ge(counted, NG * COUNT)
            step(dve.tensor_scalar(cnt[:], carry[:, 0, :], float(CAP), None, ALU.min))
            step(dve.tensor_tensor(tail_f[:], cnt[:], e_f[:, 0].rearrange("p k e -> p (k e)"), ALU.add))
            dve.tensor_scalar(tail_i[:], tail_f[:], 1.0, None, ALU.add).then_inc(tails_known, 1)
            step(dve.tensor_scalar(cnt_i[:], cnt[:], float(BLK - 1), None, ALU.add))
            step(dve.tensor_scalar(cnt_i[:], cnt_i[:], BLK.bit_length() - 1, None, ALU.arith_shift_right))
            step(dve.tensor_copy(nt[:], cnt_i[:]))
            for k in range(2):
                step(dve.tensor_tensor_scan(ends[:, k, :], ones[:, 0:E], nt[:, k * E:(k + 1) * E], 0.0,
                                            ALU.mult, ALU.add))
            step(dve.tensor_scalar(past[:, 0], ends[:], j_f[:], None, ALU.is_le))
            step(dve.tensor_tensor(past[:, 1], past[:, 0], nt[:].rearrange("p (k e) -> p k e", k=2), ALU.mult))
            step(dve.tensor_reduce(sums[:], past[:], AX.X, ALU.add))
            step(dve.tensor_scalar(rowf[:], sums[:, 1], j_f[:], -float(BLK), ALU.subtract, ALU.mult))
            step(dve.scalar_tensor_tensor(out=rowf[:], in0=sums[:, 0], scalar=float(REG), in1=rowf[:],
                                          op0=ALU.mult, op1=ALU.add))
            step(dve.tensor_scalar(rowf[:, 1:2], rowf[:, 1:2], float(E * REG), None, ALU.add))
            step(dve.tensor_scalar(none[:], sums[:, 0], float(E), float(EMPTY), ALU.is_ge, ALU.mult))
            step(dve.tensor_tensor(tab[:, 0:2], rowf[:], none[:], ALU.max))
            step(dve.tensor_scalar(tab[:, 0:2], tab[:, 0:2], float(EMPTY), None, ALU.min))
            step(dve.tensor_scalar(tab[:, 2:4], sums[:, 0], float(E - 1), None, ALU.min))
            dve.tensor_copy(tab[:, 4:8], tab[:, 0:4]).then_inc(tab_ready, 1)
            dve.wait_ge(tabT_filled, 1)
            dve.tensor_copy(tab_i[:], bank[0][0:4, 0:P]).then_inc(tables_ready, 1)

        def load_y(sp, k, g, into, done):
            src = (y_rows[k][g * T * P:(g + 1) * T * P] if isinstance(g, int)
                   else y_rows[k][ds(g * (T * P), T * P)])
            sp.dma_start(into, src.rearrange("(b s) h -> s b h", s=P)).then_inc(done, 16)

        def rounds(eng, body):
            for u in range(4):
                body(0, u)
            with eng.Fori(1, NG // 4) as r:
                for u in range(4):
                    body(r, u)

        def load_last(sp):
            for slot in range(4):
                sp.wait_ge(y_sent[slot], 2 * (NBLK // 4) * B * 16)

            def body(r, u):
                if not (isinstance(r, int) and r == 0):
                    sp.wait_ge(out_ready[u], r)
                load_y(sp, 1, r * 4 + u, yb[:, u], y_in[u])

            rounds(sp, body)

        def combine(dve):
            for v in range(2):
                dve.wait_ge(y0_added[v], NG // 2)

            def body(r, u):
                dve.wait_ge(y_in[u], (r + 1) * 16)
                if not (isinstance(r, int) and r == 0):
                    dve.wait_ge(out_stored[u], r * 16)
                dve.tensor_tensor(ob[:, u], yb[:, u], group(xs, r * 4 + u), ALU.add).then_inc(out_ready[u], 1)

            rounds(dve, body)

        def store_out(act):
            def body(r, u):
                g = r * 4 + u
                act.wait_ge(out_ready[u], r + 1)
                dst = out[g * T:(g + 1) * T] if isinstance(g, int) else out[ds(g * T, T)]
                act.dma_start(dst.rearrange("b s h -> s b h"), ob[:, u]).then_inc(out_stored[u], 16)

            rounds(act, body)
            for u in range(4):
                act.wait_ge(out_stored[u], NG // 4 * 16)

        @block.tensor
        def _(pe):
            pe.wait_ge(vectors_ready, 2)
            pe.matmul(PT[0][:, 0:P], bv2c[:], wA_s[:, W_O2], start=True, stop=True).then_inc(bo_filled, 1)
            pe.wait_ge(consts, 5)
            pe.wait_ge(bo_ready, 1)

            def begin(name, i):
                m, u = use_of(name, i)
                if not (isinstance(u, int) and u == 0):
                    pe.wait_ge(freed[m], u)
                return bank[m], filled[m]

            def scores(g, b, quadrants=range(HG)):
                n = g * T + b
                pe.wait_ge(kblk_ready, n + 1)
                for q in quadrants:
                    if not (isinstance(n, int) and n == 0):
                        pe.wait_ge(z_ready, n * 4 - 3 + q)
                    ins = pe.matmul(S[:, q, 0:HG * NK], q2[32 * q:32 * q + 32, b * P:(b + 1) * P],
                                    kblk[32 * q:32 * q + 32, b].rearrange("p h k -> p (h k)"),
                                    start=True, stop=True)
                    if q % 2:
                        ins.then_inc(scored, 1)

            def transposes(g, b, c):
                n = g * T + b
                if not (isinstance(n, int) and n == 0 and c < 2):
                    pe.wait_ge(pt_freed, n * 4 + c - 1)
                for h in range(HG):
                    at = (c * HG + h) * NK
                    ins = pe.transpose(PT[c % 2][0:NK, h * P:(h + 1) * P], z[:, b % 2, at:at + NK], ident[:])
                ins.then_inc(pt_filled, 1)

            def weights_T(g, b):
                pe.wait_ge(p_ready, g * T + b + 1)
                transposes(g, b, 0)
                transposes(g, b, 1)

            def by_values(g, b, i):
                n = g * T + b
                pv, done = begin(f"pv{b}", i)
                for q in range(HG):
                    pe.wait_ge(pt_freed, n * 4 + q + 1)
                    at = slice(64 * (q % 2), 64 * (q % 2) + 64)
                    for j in range(HG):
                        h = q * HG + j
                        ins = pe.matmul(pv[at, (q // 2) * P:(q // 2 + 1) * P], v2[:, b, h, :],
                                        pT[:, b % 2, h * P:(h + 1) * P], start=(j == 0), stop=(j == HG - 1))
                    if q < 2:
                        transposes(g, b, q + 2)
                ins.then_inc(done, 1)

            def output_T(g, b, i):
                m, u = use_of(f"pv{b}", i)
                pe.wait_ge(freed[m], u + 1)
                dst, done = begin(f"pvT{b}", i)
                for half in range(2):
                    ins = pe.transpose(dst[:, half * P:(half + 1) * P], pvs[:, b % 2, half * P:(half + 1) * P],
                                       ident[:])
                ins.then_inc(done, 1)

            def each_tile(name, i, lhsT, rhs, width=P, tiles=range(T)):
                dst, done = begin(name, i)
                for n, b in enumerate(tiles):
                    ins = pe.matmul(dst[:, n * width:(n + 1) * width], lhsT(b), rhs(b), start=True, stop=True)
                ins.then_inc(done, 1)

            def transpose_tiles(name, i, src):
                dst, done = begin(name, i)
                for b in range(T):
                    ins = pe.transpose(dst[:, b * P:(b + 1) * P], src(b), ident[:])
                ins.then_inc(done, 1)

            def part(ap):
                return lambda b: ap[:, b * P:(b + 1) * P]

            def body(i):
                L, M, X, R = (runs(stage, i) for stage in "LMXR")
                gm, gx, gr = (i - LAG[stage] for stage in "MXR")
                if X:
                    scores(gx, 0, range(2))
                if L:
                    pe.wait_ge(xn_ready, i * T + T)
                    transpose_tiles("xnT", i, lambda b: xn[:, b, :])
                if X:
                    if not (isinstance(gr, int) and gr < 1):
                        pe.wait_ge(ranks_read, gr)
                    scores(gx, 0, range(2, 4))
                if R:
                    transpose_tiles("aoT", i, lambda b: ao[:, b, :])
                if M:
                    pe.wait_ge(xn2_ready, gm * T + T)
                    transpose_tiles("xn2T", i, lambda b: xn2[:, b, :])
                if L:
                    m, u = use_of("xnT", i)
                    pe.wait_ge(freed[m], u + 1)
                    dst, done = begin("q", i)
                    pe.matmul(dst[:], wA_s[:, W_Q], xnT[:], start=True, stop=True).then_inc(done, 1)
                if R:
                    m, u = use_of("aoT", i)
                    pe.wait_ge(freed[m], u + 1)
                    each_tile("x2", i, part(aoT), lambda b: wA_s[:, W_O2])
                if L:
                    keys_and_values(i, 0)
                    keys_and_values(i, 1)
                if X:
                    weights_T(gx, 0)
                    scores(gx, 1)
                    by_values(gx, 0, i)
                if L:
                    m, u = use_of("kp1", i)
                    pe.wait_ge(freed[m], u + 1)
                    pe.wait_ge(kk_ready, i + 1)
                    for half in range(2):
                        each_tile(f"kv{half}", i, lambda b: kk[:, b, :], lambda b: kvb[:, b, P:2 * P + 1],
                                  width=P + 1, tiles=range(2 * half, 2 * half + 2))
                if X:
                    scores(gx, 2, range(2))
                    output_T(gx, 0, i)
                if L:
                    pe.wait_ge(qT_ready, i + 1)
                    numerators(i, 0)
                    numerators(i, 1)
                if X:
                    scores(gx, 2, range(2, 4))
                    weights_T(gx, 1)
                if L:
                    m, u = use_of("nd1", i)
                    pe.wait_ge(freed[m], u + 1)
                    transpose_tiles("cT", i, lambda b: cx[:, b, :])
                if X:
                    by_values(gx, 1, i)
                if L:
                    m, u = use_of("cT", i)
                    pe.wait_ge(freed[m], u + 1)
                    each_tile("hs", i, part(cT), lambda b: wA_s[:, W_D])
                if X:
                    output_T(gx, 1, i)
                    scores(gx, 3)
                    weights_T(gx, 2)
                if R:
                    pe.wait_ge(xn3_ready, gr * T + T)
                    transpose_tiles("xn3T", i, lambda b: xn3[:, b, :])
                if X:
                    by_values(gx, 2, i)
                if M:
                    pe.wait_ge(ctx_in, gm * 16 + 16)
                    dst, done = begin("k2T", i)
                    pe.matmul(dst[:, 0:T * NK], wC_s[:, 0], cg[:], start=True, stop=True).then_inc(done, 1)
                if X:
                    output_T(gx, 2, i)
                if R:
                    m, u = use_of("xn3T", i)
                    pe.wait_ge(freed[m], u + 1)
                    dst, done = begin("lgT", i)
                    pe.matmul(dst[0:E, :], wr_s[:], xn3T[:], start=True, stop=True).then_inc(done, 1)
                if X:
                    weights_T(gx, 3)
                if R:
                    m, u = use_of("lgT", i)
                    pe.wait_ge(z_ready, (gx * T + T) * 4 if X else NB * 4)
                    wait_apart(pe, freed[m], u + 1)
                    for b in range(T):
                        ins = pe.transpose(logits[:, b * E:(b + 1) * E], lgT[:, b * P:(b + 1) * P], ident[0:E, 0:E])
                    ins.then_inc(routed, 1)
                if M:
                    m, u = use_of("xn2T", i)
                    pe.wait_ge(freed[m], u + 1)
                    dst, done = begin("q2T", i)
                    pe.matmul(dst[:], wA_s[:, W_Q2], xn2T[:], start=True, stop=True).then_inc(done, 1)
                if X:
                    by_values(gx, 3, i)
                if M:
                    dst, done = begin("v2", i)
                    for b in range(T):
                        ins = pe.matmul(dst[0:NK, b * P:(b + 1) * P], cg[:, b * NK:(b + 1) * NK], wC_s[:, 1],
                                        start=True, stop=True)
                    ins.then_inc(done, 1)
                if R:
                    pe.wait_ge(chosen, (gr + 1) * CHOOSE)
                    if not (isinstance(gr, int) and gr == 0):
                        pe.wait_ge(ranks_read, gr)
                    flat = hot[:].rearrange("p b k e -> p (b k e)")
                    pe.matmul(ranks[:, 0:T * 2 * E], before[:], flat, start=True, stop=True)
                    pe.matmul(ranks[:, T * 2 * E:], ones[:], flat, start=True, stop=True).then_inc(ranked, 1)
                if X:
                    output_T(gx, 3, i)

            def keys_and_values(i, half):
                each_tile(f"kp{half}", i, part(xnT), lambda b: wA_s[:, W_K:W_V + 1].rearrange("p a h -> p (a h)"),
                          width=2 * P, tiles=range(2 * half, 2 * half + 2))

            def numerators(i, half):
                m, u = use_of(f"kv{half}", i)
                pe.wait_ge(freed[m], u + 1)
                each_tile(f"nd{half}", i, part(qT), lambda b: kvm[:, b, :], width=P + NH,
                          tiles=range(2 * half, 2 * half + 2))

            iterations(pe, body)
            pe.wait_ge(tab_ready, 1)
            pe.transpose(bank[0][0:4, 0:P], tab[:, 4:8], ident[:]).then_inc(tabT_filled, 1)
            ffn_tensor(pe)

        @block.sync
        def _(sp):
            sp.dma_start(vb[:], vrow.unsqueeze(0).broadcast_to([P, NV, P])).then_inc(weights_in, 16)
            sp.dma_start(vc[:], vcol).then_inc(weights_in, 16)
            sp.dma_start(wA_s[:], wA).then_inc(weights_in, 16)
            sp.dma_start(wC_s[:], wC).then_inc(weights_in, 16)
            sp.dma_start(wr_s[:], wr).then_inc(weights_in, 16)

            def load_x(g):
                if not (isinstance(g, int) and g == 0):
                    sp.wait_ge(x_in, g * 16)
                src = x[ds(g * T, T)] if not isinstance(g, int) else x[g * T:(g + 1) * T]
                sp.dma_start(group(xs, g), src.rearrange("b s h -> s b h")).then_inc(x_in, 16)

            def load_ctx(g):
                c = T * NK
                if not (isinstance(g, int) and g == 0):
                    b, n = use_of("v2", g - 1 + LAG["M"])
                    sp.wait_ge(filled[b], n + 1)
                src = ctxT[:, ds(g * c, c)] if not isinstance(g, int) else ctxT[:, g * c:(g + 1) * c]
                sp.dma_start(cg[:], src).then_inc(ctx_in, 16)

            load_x(0)
            load_ctx(0)
            load_x(1)
            sp.wait_ge(zeroed, 2)
            for rows in y_rows:
                flat = rows.rearrange("(a p r) h -> a p (r h)", p=P, r=8)
                for a in range(flat.shape[0]):
                    sp.dma_start(flat[a], zeros[:]).then_inc(cleared, 16)
            sp.dma_start(expert_rows[EMPTY:EMPTY + BLK, :].rearrange("(p a) r -> p a r", a=B), tail[:])\
              .then_inc(cleared, 16)
            sp.dma_start(w1_s[:], w1).then_inc(ffn_in, 16)
            sp.dma_start(w2_s[:], w2).then_inc(ffn_in, 16)
            load_x(2)
            load_ctx(1)
            load_x(3)
            load_ctx(2)
            with sp.Fori(3, NG - 1) as g:
                load_x(g + 1)
                load_ctx(g)
            load_ctx(NG - 1)
            write_tails(sp, range(E))
            ffn_load(sp)
            load_last(sp)

        @block.scalar
        def _(act):
            act.wait_ge(weights_in, 80)
            act.mul(bq2s[:], vc[:, V_BQ2:V_BQ2 + 1], SCALE).then_inc(vectors_ready, 1)
            act.wait_ge(consts, 1)
            act.activation(bv2c[:], ones[:], ACT.Copy, scale=vc[:, V_BV2:V_BV2 + 1]).then_inc(vectors_ready, 1)
            act.wait_ge(vectors_ready, 2)

            def empty(dst, name, i, cols=512, rows=P, **kw):
                b, n = use_of(name, i)
                act.wait_ge(filled[b], n + 1)
                if kw:
                    act.activation(dst, bank[b][0:rows, 0:cols], ACT.Identity, **kw).then_inc(freed[b], 1)
                else:
                    act.copy(dst, bank[b][0:rows, 0:cols]).then_inc(freed[b], 1)

            def normal(dst, src, rs, shift, rs_ready, ready, g):
                act.wait_ge(rs_ready, 2 * g + 2)
                for b in range(T):
                    act.activation(dst(b), src(b), ACT.Identity, bias=shift[:, b:b + 1], scale=rs[:, b:b + 1])\
                       .then_inc(ready, 1)

            def exponentials(g, b):
                n = g * T + b
                act.wait_ge(z_clipped, n + 1)
                act.activation(z[:, b % 2, :], z[:, b % 2, :], ACT.Exp).then_inc(p_ready, 1)

            def weights_T(g, b, quadrants):
                n = g * T + b
                for c in quadrants:
                    act.wait_ge(pt_filled, n * 4 + c + 1)
                    act.copy(pT[:, b % 2, c * 512:(c + 1) * 512], PT[c % 2][0:NK, :]).then_inc(pt_freed, 1)

            def products(b, i):
                empty(pvs[:, b % 2, :], f"pv{b}", i, cols=2 * P)

            def body(i):
                N, L, M, X, R, W = (runs(stage, i) for stage in "NLMXRW")
                gm, gx, gr, gw = (i - LAG[stage] for stage in "MXRW")
                if L:
                    empty(xnT[:], "xnT", i)
                if R:
                    empty(aoT[:], "aoT", i)
                if M:
                    empty(xn2T[:], "xn2T", i)
                if L:
                    b, n = use_of("q", i)
                    act.wait_ge(filled[b], n + 1)
                    act.activation(rq[:], bank[b][:], ACT.Identity, bias=vc[:, V_BQ:V_BQ + 1]).then_inc(freed[b], 1)
                    act.wait_ge(freed[b], n + 1)
                    act.activation(eq[:], rq[:], ACT.Exp).then_inc(eq_ready, 1)
                if X:
                    exponentials(gx, 0)
                if X:
                    weights_T(gx, 0, range(2))
                if L:
                    for half in range(2):
                        b, n = use_of(f"kp{half}", i)
                        act.wait_ge(freed[b], n + 1)
                    act.activation(ek[:], kvb[:, :, 0:P], ACT.Exp).then_inc(ek_ready, 1)
                    act.activation(rk[:], kvb[:, :, 0:P], ACT.Relu).then_inc(rk_ready, 1)
                if X:
                    weights_T(gx, 0, range(2, 4))
                    products(0, i)
                if W:
                    if not (isinstance(gw, int) and gw == 0):
                        act.wait_ge(sent, gw * (T * 2 * 16))
                    act.copy(row[:, :, 0:P], xn3[:]).then_inc(row_filled, 1)
                if X:
                    exponentials(gx, 1)
                    weights_T(gx, 1, range(2))
                if L:
                    empty(cT[:], "cT", i)
                if X:
                    weights_T(gx, 1, range(2, 4))
                    products(1, i)
                if R:
                    if W:
                        act.wait_ge(row_filled, gr)
                    normal(lambda b: xn3[:, b, :], tile_of(gr), rs3, shift3, rs3_ready, xn3_ready, gr)
                if X:
                    exponentials(gx, 2)
                    weights_T(gx, 2, range(2))
                if R:
                    empty(xn3T[:], "xn3T", i)
                if X:
                    weights_T(gx, 2, range(2, 4))
                    products(2, i)
                if M:
                    empty(k2[:], "k2T", i, cols=T * NK, bias=vc[:, V_BK2:V_BK2 + 1])
                if X:
                    exponentials(gx, 3)
                if R:
                    empty(lgT[:], "lgT", i, rows=E)
                if X:
                    weights_T(gx, 3, range(2))
                if M:
                    empty(q2[:], "q2T", i, bias=bq2s[:], scale=SCALE)
                if X:
                    weights_T(gx, 3, range(2, 4))
                if N:
                    normal(lambda b: xn[:, b, :], tile_of(i + 1), rs, shift, rs_ready, xn_ready, i + 1)
                if X:
                    products(3, i)
                if R:
                    act.wait_ge(chosen, (gr + 1) * CHOOSE)
                    act.activation(eg[:], gap[:], ACT.Exp).then_inc(eg_ready, 1)
                if M:
                    m, u = use_of("v2", i)
                    act.wait_ge(filled[m], u + 1)
                    heads = bank[m][0:NK, :].rearrange("k (g j d) -> k g j d", j=HG, d=HD)
                    into = v2[:].rearrange("k b (q j) c -> k (b q) j c", j=HG)
                    for j in range(HG):
                        ins = act.copy(into[:, :, j, j * HD:(j + 1) * HD], heads[:, :, j, :])
                    ins.then_inc(freed[m], 1)

            act.wait_ge(x_in, 16)
            normal(lambda b: xn[:, b, :], tile_of(0), rs, shift, rs_ready, xn_ready, 0)
            iterations(act, body)
            write_tails(act, range(E, NREG))
            ffn_scalar(act)
            store_out(act)

        @block.gpsimd
        def _(pool):
            pool.memset(ones[:], 1.0).then_inc(consts, 1)
            pool.memset(expo[:], -0.5)
            pool.memset(minus[:], -1.0)
            pool.memset(zeros[:], 0.0)
            pool.memset(tail[:], 0.0)
            pool.memset(carry[:], 0.0)
            pool.memset(ident[:], 0.0)
            pool.memset(before[:], 1.0)
            pool.memset(bmask[:], 1.0)
            pool.iota(tok_i[:], pattern=[[P, NB]], base=0, channel_multiplier=1)
            pool.iota(e_i[:, 0], pattern=[[E * REG, 2], [REG, E]], base=-1, channel_multiplier=0)
            pool.iota(e_i[:, 1], pattern=[[0, 2], [-1, E]], base=E, channel_multiplier=0)
            pool.iota(e_i[:, 2], pattern=[[0, 2], [1, E]], base=0, channel_multiplier=0)
            pool.iota(j_i[:], pattern=[[0, 1]], base=0, channel_multiplier=1)
            pool.memset(kvb[:], 1.0)
            pool.memset(v2[:], 0.0).then_inc(zeroed, 1)
            pool.wait_ge(zeroed, 1)
            for j in range(HG):
                pool.memset(v2[:].rearrange("k b (q j) c -> k (b q) j c", j=HG)[:, :, j, 32 + j:33 + j], 1.0)
            pool.iota(tail[:, :, P].bitcast(I32), pattern=[[0, B]], base=int(BIG), channel_multiplier=0)\
                .then_inc(zeroed, 1)
            pool.affine_select(out=ident[:], in_=ident[:], compare_op=ALU.not_equal, fill=1.0, base=0,
                               pattern=[[-1, P]], channel_multiplier=1)
            pool.affine_select(out=before[:], in_=before[:], compare_op=ALU.is_ge, fill=0.0, base=0,
                               pattern=[[1, P]], channel_multiplier=-1)
            heads = bmask[:].rearrange("p (h d) -> p h d", d=HD)
            pool.affine_select(out=heads, in_=heads, compare_op=ALU.is_ge, fill=0.0, base=0,
                               pattern=[[-HD, NH], [0, HD]], channel_multiplier=1).then_inc(consts, 1)
            pool.wait_ge(consts, 2)
            pool.affine_select(out=heads, in_=heads, compare_op=ALU.is_ge, fill=0.0, base=HD - 1,
                               pattern=[[HD, NH], [0, HD]], channel_multiplier=-1).then_inc(consts, 1)
            pool.tensor_copy(e_f[:], e_i[:]).then_inc(consts, 1)
            pool.tensor_copy(j_f[:], j_i[:]).then_inc(consts, 1)

            def inverse_root(dst, mv, eps, moments, part, ready, g, shift=None):
                wait_apart(pool, moments, g * T + T)
                if shift is not None:
                    pool.tensor_scalar(shift[:], mv[:, :, 0], -1.0, None, ALU.mult)
                pool.tensor_scalar(dst[:], mv[:, :, 1], eps, None, ALU.add).then_inc(part, 1)
                pool.wait_ge(part, g + 1)
                pool.tensor_tensor(dst[:], dst[:], expo[:], ALU.pow).then_inc(ready, 1)
                if shift is not None:
                    pool.wait_ge(ready, 2 * g + 1)
                    pool.tensor_tensor(shift[:], shift[:], dst[:], ALU.mult).then_inc(ready, 1)

            pool.wait_ge(weights_in, 80)
            pool.wait_ge(hmask_ready, 2)
            pool.wait_ge(bo_ready, 1)

            def body(i):
                N, L, M, R, W, V = (runs(stage, i) for stage in "NLMRWV")
                gm, gr, gw, gv = (i - LAG[stage] for stage in "MRWV")
                if V:
                    pool.wait_ge(gate_steps, gv * 3 + 3)
                    pool.wait_ge(row_filled, gv + 1)
                    wait_apart(pool, placed, (gv + 1) * PLACE)
                    for b in range(T):
                        for k in range(2):
                            pool.indirect_dma_start(
                                out=expert_rows, out_offset=bass.IndirectOffsetOnAxis(
                                    ap=slot[:, b * 2 + k:b * 2 + k + 1], axis=0),
                                in_=row[:, b, :], in_offset=None,
                                bounds_check=EMPTY - 1, oob_is_err=False).then_inc(sent, 16)
                if L:
                    pool.wait_ge(xn_ready, i * T + T)
                    pool.tensor_tensor(xb[:], xn[:], bc(vb[:, V_BD], 1, T), ALU.add).then_inc(xb_ready, 1)
                    pool.tensor_tensor(xbeta[:], group(xs, i), bc(vb[:, V_BETA], 1, T), ALU.add)\
                        .then_inc(xbeta_ready, 1)
                if W:
                    wait_apart(pool, eg_ready, gw + 1)
                    pool.tensor_scalar(eg1[:], eg[:], 1.0, None, ALU.add).then_inc(gate_steps, 1)
                    if V:
                        pool.wait_ge(sent, gw * (T * 2 * 16))
                    pool.wait_ge(gate_steps, gw * 3 + 1)
                    pool.tensor_tensor(row[:, :, P + 1], eg1[:], minus[:], ALU.pow).then_inc(gate_steps, 1)
                    pool.tensor_copy(row[:, :, P].bitcast(I32),
                                     tok_i[:, gw * T:(gw + 1) * T] if isinstance(gw, int) else tok_i[:, ds(gw * T, T)])
                    pool.wait_ge(gate_steps, gw * 3 + 2)
                    pool.tensor_tensor(row[:, :, P + 2], eg[:], row[:, :, P + 1], ALU.mult).then_inc(gate_steps, 1)
                if R:
                    inverse_root(rs3, mv3, EPS, moments3, rs3_part, rs3_ready, gr, shift3)
                if L:
                    inverse_root(hrs, hmv, EPS_ATTN_LN, hmoments, hrs_part, hrs_ready, i)
                    pool.wait_ge(hn_ready, i * T + T)
                    pool.tensor_tensor(hg[:], hn[:], bc(vb[:, V_GAMMA], 1, T), ALU.mult).then_inc(hg_ready, 1)
                    pool.wait_ge(hg_ready, i + 1)
                    pool.tensor_tensor(x1[:], hg[:], xbeta[:], ALU.add).then_inc(x1_ready, 1)
                if N:
                    inverse_root(rs, mv, EPS, moments, rs_part, rs_ready, i + 1, shift)
                if L:
                    inverse_root(rs2, mv2, EPS, moments2, rs2_part, rs2_ready, i)
                if M:
                    m, u = use_of("k2T", i)
                    pool.wait_ge(freed[m], u + 1)
                    for b in range(T):
                        pool.tensor_tensor(kblk[:, b], bc(k2[:, b * NK:(b + 1) * NK], 1, HG),
                                           bc(hmask[:], 2, NK), ALU.mult).then_inc(kblk_ready, 1)
                if L:
                    wait_apart(pool, x1_ready, i + 1)
                    pool.tensor_tensor(group(xs, i), x1[:], bc(bo_all[:], 1, T), ALU.add).then_inc(x1_kept, 1)

            inverse_root(rs, mv, EPS, moments, rs_part, rs_ready, 0, shift)
            iterations(pool, body)
            ffn_scatter(pool)

        @block.vector
        def _(dve):
            dve.wait_ge(consts, 5)
            dve.tensor_reduce(hmask[:], bmask[:].rearrange("p (q j d) -> p j q d", q=HG, d=HD)[:, :, :, 0],
                              AX.X, ALU.add).then_inc(hmask_ready, 1)
            dve.tensor_copy(hmask16[:], bmask[:].rearrange("p (h d) -> p h d", d=HD)[:, :, 0]).then_inc(hmask_ready, 1)
            dve.wait_ge(hmask_ready, 2)
            dve.wait_ge(bo_filled, 1)
            dve.tensor_tensor(bo_all[:], PT[0][:, 0:P], vb[:, V_BO2], ALU.add).then_inc(bo_ready, 1)

            def moments_of(src, st, mv, sem_stats, sem_moments, g):
                for b in range(T):
                    dve.bn_stats(st[:, b, :], src(b)).then_inc(sem_stats, 1)
                for b in range(T):
                    wait_apart(dve, sem_stats, g * T + b + 1)
                    dve.bn_aggr(mv[:, b, :], st[:, b, :]).then_inc(sem_moments, 1)

            def normal(dst, src, mv, rs, rs_ready, ready, g):
                dve.wait_ge(rs_ready, g + 1)
                for b in range(T):
                    dve.tensor_scalar(dst(b), src(b), mv[:, b, 0:1], rs[:, b:b + 1], ALU.subtract, ALU.mult)\
                       .then_inc(ready, 1)

            def softmax_shift(g, b):
                n = g * T + b
                for half in range(2):
                    qs = slice(2 * half, 2 * half + 2)
                    dve.wait_ge(scored, n * 2 + half + 1)
                    dve.tensor_reduce(mraw[:, half, :].rearrange("p (q h) -> p q h", q=2),
                                      S[:, qs, 0:HG * NK].rearrange("p q (h k) -> p q h k", k=NK),
                                      AX.X, ALU.max).then_inc(m_raw, 1)
                dve.wait_ge(m_raw, n * 2 + 2)
                dve.tensor_scalar(mclip[:], mraw[:], CLAMP, -CLAMP, ALU.min, ALU.max).then_inc(m_clipped, 1)
                dve.wait_ge(m_clipped, n + 1)
                if not (isinstance(n, int) and n < 2):
                    dve.wait_ge(pt_filled, n * 4 - 4)
                for q in range(HG):
                    c = q * HG * NK
                    dve.scalar_tensor_tensor(
                        out=z[:, b % 2, c:c + HG * NK].rearrange("p (h k) -> p h k", k=NK),
                        in0=S[:, q, 0:HG * NK].rearrange("p (h k) -> p h k", k=NK),
                        scalar=-CLAMP, in1=bc(mclip[:, q // 2, (q % 2) * HG:(q % 2 + 1) * HG], 2, NK),
                        op0=ALU.max, op1=ALU.subtract).then_inc(z_ready, 1)

                dve.wait_ge(z_ready, n * 4 + 4)
                dve.tensor_scalar(z[:, b % 2, :], z[:, b % 2, :], 0.0, None, ALU.min).then_inc(z_clipped, 1)

            def softmax_divide(g, b, i):
                n = g * T + b
                m, u = use_of(f"pvT{b}", i)
                pv = bank[m][:, 0:2 * P].rearrange("p (q c) -> p q c", c=64)
                dve.wait_ge(filled[m], u + 1)
                dve.reciprocal(rd[:], pv[:, :, 32:32 + HG]).then_inc(rd_ready, 1)
                dve.wait_ge(rd_ready, n + 1)
                dve.tensor_tensor(ao[:, b, :].rearrange("p (q j d) -> p q j d", j=HG, d=HD),
                                  pv[:, :, 0:32].rearrange("p q (j d) -> p q j d", d=HD),
                                  bc(rd[:], 3, HD), ALU.mult).then_inc(freed[m], 1)

            def choose(g, i):
                done = [0]

                def step(ins):
                    ins.then_inc(chosen, 1)
                    done[0] += 1

                def settle():
                    dve.wait_ge(chosen, g * CHOOSE + done[0])

                dve.wait_ge(routed, g + 1)
                step(dve.tensor_copy(lg[:], logits.rearrange("p (b e) -> p b e", e=E)))
                settle()
                src = lg
                for k in range(2):
                    step(dve.tensor_reduce(top[:, k, :], src[:], AX.X, ALU.max))
                    settle()
                    step(dve.tensor_tensor(tie[:], src[:], bc(top[:, k, :], 2, E), ALU.is_equal))
                    settle()
                    step(dve.tensor_tensor(tie[:], tie[:], bc(e_f[:, 1, 0, :], 1, T), ALU.mult))
                    settle()
                    step(dve.tensor_reduce(tiem[:], tie[:], AX.X, ALU.max))
                    settle()
                    step(dve.tensor_tensor(hot[:, :, k, :], bc(e_f[:, 1, 0, :], 1, T), bc(tiem[:], 2, E),
                                           ALU.is_equal))
                    if k == 0:
                        settle()
                        step(dve.scalar_tensor_tensor(out=low[:], in0=hot[:, :, 0, :], scalar=-3e38,
                                                      in1=lg[:], op0=ALU.mult, op1=ALU.add))
                        settle()
                        src = low
                step(dve.tensor_tensor(gap[:], top[:, 1, :], top[:, 0, :], ALU.subtract))
                assert done[0] == CHOOSE

            def count_up(g):
                done = [0]

                def step(ins):
                    ins.then_inc(counted, 1)
                    done[0] += 1

                def settle():
                    dve.wait_ge(counted, g * COUNT + done[0])

                wait_apart(dve, ranks_read, g + 1)
                for b in range(T):
                    if b:
                        settle()
                    step(dve.tensor_tensor(carry[:, b + 1, :], carry[:, b, :], rank[:, 1, b, :], ALU.add))
                settle()
                step(dve.tensor_tensor(pos[:], rank[:, 0], carry[:, 0:T, :], ALU.add))
                settle()
                step(dve.tensor_copy(carry[:, 0, :], carry[:, T, :]))
                assert done[0] == COUNT

            def place(g):
                done = [0]

                def step(ins):
                    ins.then_inc(placed, 1)
                    done[0] += 1

                def settle():
                    dve.wait_ge(placed, g * PLACE + done[0])

                hot8 = hot_kept[:].rearrange("p b k e -> p (b k) e")
                wait_apart(dve, kept, g + 1)
                wait_apart(dve, counted, (g + 1) * COUNT)
                step(dve.tensor_tensor(pick[:, 0], hot8, pos[:].rearrange("p b (k e) -> p (b k) e", k=2), ALU.mult))
                step(dve.tensor_tensor(pick[:, 1].rearrange("p (b k) e -> p b (k e)", k=2),
                                       hot_kept[:].rearrange("p b k e -> p b (k e)"),
                                       bc(e_f[:, 0].rearrange("p k e -> p (k e)"), 1, T), ALU.mult))
                settle()
                step(dve.tensor_reduce(sel[:], pick[:], AX.X, ALU.add))
                settle()
                step(dve.tensor_scalar(over[:], sel[:, 0], float(CAP), BIG, ALU.is_gt, ALU.mult))
                step(dve.tensor_tensor(slot_f[:], sel[:, 0], sel[:, 1], ALU.add))
                settle()
                if not (isinstance(g, int) and g == 0):
                    wait_apart(dve, sent, g * (T * 2 * 16))
                step(dve.tensor_tensor(slot[:], slot_f[:], over[:], ALU.add))
                assert done[0] == PLACE

            def body(i):
                N, L, X, R, W = (runs(stage, i) for stage in "NLXRW")
                gx, gr, gw = (i - LAG[stage] for stage in "XRW")
                if X:
                    softmax_shift(gx, 0)
                if R:
                    m, u = use_of("x2", i)
                    dve.wait_ge(filled[m], u + 1)
                    dve.wait_ge(x1_kept, gr + 1)
                    dve.tensor_tensor(group(xs, gr), bank[m][:].rearrange("p (b h) -> p b h", b=T),
                                      group(xs, gr), ALU.add).then_inc(freed[m], 1)
                if L:
                    for half in range(2):
                        m, u = use_of(f"kp{half}", i)
                        dve.wait_ge(filled[m], u + 1)
                        dve.tensor_tensor(kvb[:, 2 * half:2 * half + 2, 0:2 * P],
                                          bank[m][:].rearrange("p (b h) -> p b h", b=2),
                                          bc(vb[:, V_BK:V_BV + 1].rearrange("p a h -> p (a h)"), 1, 2),
                                          ALU.add).then_inc(freed[m], 1)
                    dve.wait_ge(eq_ready, i + 1)
                    m, u = use_of("q", i)
                    dve.wait_ge(freed[m], u + 1)
                    dve.tensor_scalar(eq[:], eq[:], 1.0, None, ALU.min).then_inc(eq_clipped, 1)
                    dve.wait_ge(eq_clipped, i + 1)
                    dve.scalar_tensor_tensor(out=qT[:], in0=rq[:], scalar=0.0, in1=eq[:], op0=ALU.max, op1=ALU.add)\
                       .then_inc(qT_ready, 1)
                    dve.wait_ge(ek_ready, i + 1)
                    dve.wait_ge(rk_ready, i + 1)
                    dve.scalar_tensor_tensor(out=kk[:], in0=ek[:], scalar=1.0, in1=rk[:], op0=ALU.min, op1=ALU.add)\
                       .then_inc(kk_ready, 1)
                if X:
                    softmax_shift(gx, 1)
                if L:
                    for half in range(2):
                        m, u = use_of(f"kv{half}", i)
                        pair = slice(2 * half, 2 * half + 2)
                        got = bank[m][:, 0:2 * (P + 1)].rearrange("p (b h) -> p b h", b=2)
                        dve.wait_ge(filled[m], u + 1)
                        dve.tensor_tensor(kvm[:, pair, 0:P], got[:, :, 0:P], bc(bmask[:], 1, 2), ALU.mult)\
                           .then_inc(kvm_ready, 1)
                        dve.scalar_tensor_tensor(out=kvm[:, pair, P:P + NH],
                                                 in0=got[:, :, P:P + 1].broadcast_to([P, 2, NH]), scalar=EPS_ATTN,
                                                 in1=bc(hmask16[:], 1, 2), op0=ALU.add, op1=ALU.mult)\
                           .then_inc(freed[m], 1)
                if X:
                    softmax_divide(gx, 0, i)
                if R:
                    m, u = use_of("x2", i)
                    wait_apart(dve, freed[m], u + 1)
                    moments_of(tile_of(gr), st3, mv3, stats3, moments3, gr)
                if L:
                    attention_divide(i, 0)
                    attention_divide(i, 1)
                if X:
                    softmax_shift(gx, 2)
                if L:
                    m, u = use_of("hs", i)
                    dve.wait_ge(filled[m], u + 1)
                    dve.wait_ge(xb_ready, i + 1)
                    dve.tensor_tensor(hs[:], bank[m][:].rearrange("p (b h) -> p b h", b=T), xb[:], ALU.add)\
                       .then_inc(freed[m], 1)
                    wait_apart(dve, freed[m], u + 1)
                    moments_of(lambda b: hs[:, b, :], hst, hmv, hstats, hmoments, i)
                if X:
                    softmax_divide(gx, 1, i)
                if X:
                    softmax_shift(gx, 3)
                if L:
                    normal(lambda b: hn[:, b, :], lambda b: hs[:, b, :], hmv, hrs, hrs_ready, hn_ready, i)
                if X:
                    softmax_divide(gx, 2, i)
                if N:
                    wait_apart(dve, x_in, (i + 1) * 16 + 16)
                    moments_of(tile_of(i + 1), st, mv, stats, moments, i + 1)
                if W:
                    count_up(gw)
                if L:
                    wait_apart(dve, x1_ready, i + 1)
                    moments_of(lambda b: x1[:, b, :], st2, mv2, stats2, moments2, i)
                if R:
                    choose(gr, i)
                if L:
                    normal(lambda b: xn2[:, b, :], lambda b: x1[:, b, :], mv2, rs2, rs2_ready, xn2_ready, i)
                if W:
                    place(gw)
                if R:
                    if W:
                        wait_apart(dve, placed, (gw + 1) * PLACE)
                    dve.wait_ge(chosen, (gr + 1) * CHOOSE)
                    dve.tensor_copy(hot_kept[:], hot[:]).then_inc(kept, 1)
                    dve.wait_ge(ranked, gr + 1)
                    dve.tensor_copy(rank[:].rearrange("p a b e -> p (a b e)"), ranks).then_inc(ranks_read, 1)
                if X:
                    softmax_divide(gx, 3, i)

            def attention_divide(i, half):
                m, u = use_of(f"nd{half}", i)
                pair = slice(2 * half, 2 * half + 2)
                got = bank[m][:, 0:2 * (P + NH)].rearrange("p (b h) -> p b h", b=2)
                dve.wait_ge(filled[m], u + 1)
                dve.reciprocal(rdn[:, pair, :], got[:, :, P:P + NH]).then_inc(rdn_ready, 1)
                dve.wait_ge(rdn_ready, i * 2 + half + 1)
                dve.tensor_tensor(cx[:, pair, :].rearrange("p b (h d) -> p b h d", d=HD),
                                  got[:, :, 0:P].rearrange("p b (h d) -> p b h d", d=HD),
                                  bc(rdn[:, pair, :], 3, HD), ALU.mult).then_inc(freed[m], 1)

            dve.wait_ge(x_in, 16)
            moments_of(tile_of(0), st, mv, stats, moments, 0)
            iterations(dve, body)
            make_tables(dve)
            ffn_vector(dve)
            combine(dve)


def kernel(**inputs):
    import numpy as np
    import concourse.bacc as bacc
    from concourse.bass_utils import run_bass_kernel_spmd

    a = {k: np.asarray(v) for k, v in inputs.items()}
    A, C, M = "L0_attn_", "L0_xattn_", "L0_ffn_"
    vectors = [a[A + n] for n in ("bq", "bk", "bv", "bd", "gamma", "beta")] + \
              [a[C + n] for n in ("bq", "bk", "bv", "bo")]
    arrays = {
        "x": a["x"],
        "ctxT": a["ctx_768"].reshape(NB * NK, CK).T,
        "wA": np.stack([a[A + "Wq"].T, a[A + "Wk"].T, a[A + "Wv"].T, a[A + "Wd"].T, a[C + "Wq"], a[C + "Wo"]], axis=1),
        "wC": np.stack([a[C + "Wk"], a[C + "Wv"]], axis=1),
        "wr": a[M + "router_w"].T,
        "w1": a[M + "w1"].transpose(1, 0, 2).reshape(P, E * F),
        "w2": a[M + "w2"].reshape(E, FC, P, P).transpose(2, 0, 1, 3).reshape(P, E * FC * P),
        "vrow": np.stack(vectors),
        "vcol": np.stack(vectors, axis=1),
    }
    arrays = {k: np.ascontiguousarray(v) for k, v in arrays.items()}
    nc = bacc.Bacc("TRN2", target_bir_lowering=False, num_devices=1)
    args = [nc.dram_tensor(k, v.shape, F32, kind="ExternalInput").ap() for k, v in arrays.items()]
    out = nc.dram_tensor("out", [NB, P, P], F32, kind="ExternalOutput").ap()
    expert_rows = nc.dram_tensor("expert_rows", [EMPTY + BLK, ROW], F32, kind="Internal").ap()
    y_rows = [nc.dram_tensor(f"y_rows{k}", [NB * P, P], F32, kind="Internal").ap() for k in range(2)]
    decoder_layer(nc, *args, out, expert_rows, y_rows)
    r = run_bass_kernel_spmd(nc, [arrays], core_ids=[0])
    return r.results[0]["out"]
```
